# Optimizing a Trainium2 kernel written in Bass

```python
import numpy as np
import jax
import jax.numpy as jnp

def _softmax(x, axis=-1):
    return jax.nn.softmax(x, axis=axis)

def _gelu(x):
    return jax.nn.gelu(x, approximate=True)

def _silu(x):
    return jax.nn.silu(x)

def _sigmoid(x):
    return jax.nn.sigmoid(x)

def _layernorm(x, axis=-1, eps=1e-05):
    m = jnp.mean(x, axis=axis, keepdims=True)
    v = jnp.var(x, axis=axis, keepdims=True)
    return (x - m) / jnp.sqrt(v + eps)

def _scatter_add(tgt, idx, src, axis=0):
    return tgt.at[idx].add(src)

def _segment_sum(src, seg, n):
    return jax.ops.segment_sum(src, seg, n)
kernel_name = 'mk_hybrid_d1_jaxref_r8_3f8856'

def setup_inputs(seed: int=0):
    np.random.seed(seed)
    _w = jnp.asarray

    def _L0_attn_a_setup():
        import jax, jax.numpy as jnp
        import numpy as np
        from jax import lax
        D_MODEL = 128
        D_STATE = 16
        D_CONV = 4
        EXPAND = 2
        D_INNER = EXPAND * D_MODEL
        DT_RANK = min(D_MODEL // 16, 64)
        EPS = 1e-05

        def _rmsnorm(x, w):
            var = jnp.mean(x * x, axis=-1, keepdims=True)
            return x * lax.rsqrt(var + EPS) * w

        def _selective_scan(u, delta, A, Bm, Cm, Dv):

            def step(h, inp):
                d_t, b_t, c_t, u_t = inp
                dA = jnp.exp(d_t[..., None] * A)
                dBu = d_t[..., None] * b_t[:, None, :] * u_t[..., None]
                h = dA * h + dBu
                y_t = jnp.einsum('bdn,bn->bd', h, c_t)
                return (h, y_t)
            xs = (jnp.swapaxes(delta, 0, 1), jnp.swapaxes(Bm, 0, 1), jnp.swapaxes(Cm, 0, 1), jnp.swapaxes(u, 0, 1))
            h0 = jnp.zeros((u.shape[0], D_INNER, D_STATE), u.dtype)
            _, ys = lax.scan(step, h0, xs)
            return jnp.swapaxes(ys, 0, 1) + u * Dv
        key = jax.random.key(seed)
        ks = jax.random.split(key, 8)

        def init(k, shape, s=0.02):
            return jax.random.normal(k, shape, jnp.float32) * s
        return {'x': jax.random.normal(ks[0], (8, 256, D_MODEL), jnp.float32), 'norm_w': jnp.ones((D_MODEL,), jnp.float32), 'in_proj_w': init(ks[1], (2 * D_INNER, D_MODEL)), 'conv_w': init(ks[2], (D_INNER, 1, D_CONV), 0.1), 'conv_b': jnp.zeros((D_INNER,), jnp.float32), 'x_proj_w': init(ks[3], (DT_RANK + 2 * D_STATE, D_INNER)), 'dt_proj_w': init(ks[4], (D_INNER, DT_RANK), 0.1), 'dt_proj_b': init(ks[5], (D_INNER,), 0.1), 'A_log': jnp.log(jnp.broadcast_to(jnp.arange(1, D_STATE + 1, dtype=jnp.float32), (D_INNER, D_STATE))), 'D': jnp.ones((D_INNER,), jnp.float32), 'out_proj_w': init(ks[6], (D_MODEL, D_INNER))}
    _L0_attn_a_in = _L0_attn_a_setup()

    def _L0_attn_b_setup():
        import jax, jax.numpy as jnp
        import numpy as np
        D_MODEL = 128
        D_STATE = 128
        D_CONV = 4
        EXPAND = 2
        HEADDIM = 64
        D_INNER = EXPAND * D_MODEL
        NHEADS = D_INNER // HEADDIM
        CONV_DIM = D_INNER + 2 * D_STATE
        D_IN_PROJ = 2 * D_INNER + 2 * D_STATE + NHEADS
        INTER = (int(D_MODEL * 8 / 3) + 63) // 64 * 64
        EPS = 1e-06
        BATCH, SEQLEN = (2, 128)

        def rmsnorm(x, w):
            return x * jax.lax.rsqrt(jnp.mean(x * x, axis=-1, keepdims=True) + EPS) * w

        def _mixer(u, in_proj_w, conv_w, conv_b, dt_bias, A_log, D, ssm_norm_w, out_proj_w):
            b, l, _ = u.shape
            zxbcdt = u @ in_proj_w.T
            z = zxbcdt[..., :D_INNER]
            xBC = zxbcdt[..., D_INNER:D_INNER + CONV_DIM]
            dt = zxbcdt[..., -NHEADS:]
            xp = jnp.pad(xBC, ((0, 0), (D_CONV - 1, 0), (0, 0)))
            xBC = sum((xp[:, k:k + l, :] * conv_w[:, k] for k in range(D_CONV))) + conv_b
            xBC = jax.nn.silu(xBC)
            xs = xBC[..., :D_INNER].reshape(b, l, NHEADS, HEADDIM)
            Bm = xBC[..., D_INNER:D_INNER + D_STATE]
            Cm = xBC[..., -D_STATE:]
            dt = jax.nn.softplus(dt + dt_bias)
            A = -jnp.exp(A_log)

            def step(h, inp):
                dt_t, x_t, B_t, C_t = inp
                dA = jnp.exp(dt_t * A)
                h = h * dA[..., None, None] + jnp.einsum('bh,bhp,bn->bhpn', dt_t, x_t, B_t)
                y_t = jnp.einsum('bhpn,bn->bhp', h, C_t)
                return (h, y_t)
            h0 = jnp.zeros((b, NHEADS, HEADDIM, D_STATE), u.dtype)
            xsT = (jnp.moveaxis(dt, 1, 0), jnp.moveaxis(xs, 1, 0), jnp.moveaxis(Bm, 1, 0), jnp.moveaxis(Cm, 1, 0))
            _, yT = jax.lax.scan(step, h0, xsT)
            y = jnp.moveaxis(yT, 0, 1) + D[None, None, :, None] * xs
            y = y.reshape(b, l, D_INNER)
            y = rmsnorm(y * jax.nn.silu(z), ssm_norm_w)
            return y @ out_proj_w.T
        key = jax.random.key(seed)
        ks = jax.random.split(key, 16)
        s = 0.02
        return {'hidden_states': jax.random.normal(ks[0], (BATCH, SEQLEN, D_MODEL), jnp.float32), 'norm_w': jnp.ones((D_MODEL,), jnp.float32), 'in_proj_w': jax.random.normal(ks[1], (D_IN_PROJ, D_MODEL), jnp.float32) * s, 'conv_w': jax.random.normal(ks[2], (CONV_DIM, D_CONV), jnp.float32) * 0.2, 'conv_b': jnp.zeros((CONV_DIM,), jnp.float32), 'dt_bias': jax.random.normal(ks[3], (NHEADS,), jnp.float32) * 0.5, 'A_log': jnp.log(jax.random.uniform(ks[4], (NHEADS,), jnp.float32, 1.0, 16.0)), 'D': jnp.ones((NHEADS,), jnp.float32) + jax.random.normal(ks[5], (NHEADS,), jnp.float32) * 0.05, 'ssm_norm_w': jnp.ones((D_INNER,), jnp.float32), 'out_proj_w': jax.random.normal(ks[6], (D_MODEL, D_INNER), jnp.float32) * s, 'post_norm_w': jnp.ones((D_MODEL,), jnp.float32), 'gate_w': jax.random.normal(ks[7], (INTER, D_MODEL), jnp.float32) * s, 'up_w': jax.random.normal(ks[8], (INTER, D_MODEL), jnp.float32) * s, 'down_w': jax.random.normal(ks[9], (D_MODEL, INTER), jnp.float32) * s}
    _L0_attn_b_in = _L0_attn_b_setup()

    def _L0_ffn_setup():
        import jax, jax.numpy as jnp
        import numpy as np
        B, S, D = (4, 256, 128)
        E = 8
        TOPK = 2
        I = 938

        def _swiglu(x, gate_up, down):
            h = jnp.einsum('bsd,fd->bsf', x, gate_up)
            g, u = jnp.split(h, 2, axis=-1)
            return jnp.einsum('bsi,di->bsd', jax.nn.silu(g) * u, down)
        key = jax.random.key(seed)
        ks = jax.random.split(key, 6)
        scale = 1.0 / np.sqrt(D)
        return {'hidden_states': jax.random.normal(ks[0], (B, S, D), dtype=jnp.float32), 'gate_weight': jax.random.normal(ks[1], (E, D), dtype=jnp.float32) * scale, 'shared_gate_up': jax.random.normal(ks[2], (2 * I, D), dtype=jnp.float32) * scale, 'shared_down': jax.random.normal(ks[3], (D, I), dtype=jnp.float32) * (1.0 / np.sqrt(I)), 'experts_gate_up': jax.random.normal(ks[4], (E, 2 * I, D), dtype=jnp.float32) * scale, 'experts_down': jax.random.normal(ks[5], (E, D, I), dtype=jnp.float32) * (1.0 / np.sqrt(I))}
    _L0_ffn_in = _L0_ffn_setup()
    _d = {'L0_attn_a_x': _L0_attn_a_in['x'], 'L0_attn_a_norm_w': _L0_attn_a_in['norm_w'], 'L0_attn_a_in_proj_w': _L0_attn_a_in['in_proj_w'], 'L0_attn_a_conv_w': _L0_attn_a_in['conv_w'], 'L0_attn_a_conv_b': _L0_attn_a_in['conv_b'], 'L0_attn_a_x_proj_w': _L0_attn_a_in['x_proj_w'], 'L0_attn_a_dt_proj_w': _L0_attn_a_in['dt_proj_w'], 'L0_attn_a_dt_proj_b': _L0_attn_a_in['dt_proj_b'], 'L0_attn_a_A_log': _L0_attn_a_in['A_log'], 'L0_attn_a_D': _L0_attn_a_in['D'], 'L0_attn_a_out_proj_w': _L0_attn_a_in['out_proj_w'], 'L0_attn_b_norm_w': _L0_attn_b_in['norm_w'], 'L0_attn_b_in_proj_w': _L0_attn_b_in['in_proj_w'], 'L0_attn_b_conv_w': _L0_attn_b_in['conv_w'], 'L0_attn_b_conv_b': _L0_attn_b_in['conv_b'], 'L0_attn_b_dt_bias': _L0_attn_b_in['dt_bias'], 'L0_attn_b_A_log': _L0_attn_b_in['A_log'], 'L0_attn_b_D': _L0_attn_b_in['D'], 'L0_attn_b_ssm_norm_w': _L0_attn_b_in['ssm_norm_w'], 'L0_attn_b_out_proj_w': _L0_attn_b_in['out_proj_w'], 'L0_attn_b_post_norm_w': _L0_attn_b_in['post_norm_w'], 'L0_attn_b_gate_w': _L0_attn_b_in['gate_w'], 'L0_attn_b_up_w': _L0_attn_b_in['up_w'], 'L0_attn_b_down_w': _L0_attn_b_in['down_w'], 'L0_ffn_gate_weight': _L0_ffn_in['gate_weight'], 'L0_ffn_shared_gate_up': _L0_ffn_in['shared_gate_up'], 'L0_ffn_shared_down': _L0_ffn_in['shared_down'], 'L0_ffn_experts_gate_up': _L0_ffn_in['experts_gate_up'], 'L0_ffn_experts_down': _L0_ffn_in['experts_down']}
    _x0 = _d['L0_attn_a_x']
    _d['L0_attn_a_x'] = jax.random.normal(jax.random.fold_in(jax.random.key(seed), 1), (2, 1024, 128), dtype=_x0.dtype)
    del _x0
    return _d

def reference(L0_attn_a_x, L0_attn_a_norm_w, L0_attn_a_in_proj_w, L0_attn_a_conv_w, L0_attn_a_conv_b, L0_attn_a_x_proj_w, L0_attn_a_dt_proj_w, L0_attn_a_dt_proj_b, L0_attn_a_A_log, L0_attn_a_D, L0_attn_a_out_proj_w, L0_attn_b_norm_w, L0_attn_b_in_proj_w, L0_attn_b_conv_w, L0_attn_b_conv_b, L0_attn_b_dt_bias, L0_attn_b_A_log, L0_attn_b_D, L0_attn_b_ssm_norm_w, L0_attn_b_out_proj_w, L0_attn_b_post_norm_w, L0_attn_b_gate_w, L0_attn_b_up_w, L0_attn_b_down_w, L0_ffn_gate_weight, L0_ffn_shared_gate_up, L0_ffn_shared_down, L0_ffn_experts_gate_up, L0_ffn_experts_down):

    def _L0_attn_a_ref(x, norm_w, in_proj_w, conv_w, conv_b, x_proj_w, dt_proj_w, dt_proj_b, A_log, D, out_proj_w):
        import jax, jax.numpy as jnp
        import numpy as np
        from jax import lax
        D_MODEL = 128
        D_STATE = 16
        D_CONV = 4
        EXPAND = 2
        D_INNER = EXPAND * D_MODEL
        DT_RANK = min(D_MODEL // 16, 64)
        EPS = 1e-05

        def _rmsnorm(x, w):
            var = jnp.mean(x * x, axis=-1, keepdims=True)
            return x * lax.rsqrt(var + EPS) * w

        def _selective_scan(u, delta, A, Bm, Cm, Dv):

            def step(h, inp):
                d_t, b_t, c_t, u_t = inp
                dA = jnp.exp(d_t[..., None] * A)
                dBu = d_t[..., None] * b_t[:, None, :] * u_t[..., None]
                h = dA * h + dBu
                y_t = jnp.einsum('bdn,bn->bd', h, c_t)
                return (h, y_t)
            xs = (jnp.swapaxes(delta, 0, 1), jnp.swapaxes(Bm, 0, 1), jnp.swapaxes(Cm, 0, 1), jnp.swapaxes(u, 0, 1))
            h0 = jnp.zeros((u.shape[0], D_INNER, D_STATE), u.dtype)
            _, ys = lax.scan(step, h0, xs)
            return jnp.swapaxes(ys, 0, 1) + u * Dv
        residual = x
        xn = _rmsnorm(x, norm_w)
        xz = xn @ in_proj_w.T
        x_part, z = jnp.split(xz, 2, axis=-1)
        xc = lax.conv_general_dilated(jnp.swapaxes(x_part, 1, 2), conv_w, window_strides=(1,), padding=((D_CONV - 1, 0),), feature_group_count=D_INNER, dimension_numbers=('NCH', 'OIH', 'NCH'))
        xc = jnp.swapaxes(xc + conv_b[None, :, None], 1, 2)
        u = jax.nn.silu(xc)
        x_dbl = u @ x_proj_w.T
        dt, Bm, Cm = jnp.split(x_dbl, [DT_RANK, DT_RANK + D_STATE], axis=-1)
        delta = jax.nn.softplus(dt @ dt_proj_w.T + dt_proj_b)
        A = -jnp.exp(A_log)
        y = _selective_scan(u, delta, A, Bm, Cm, D)
        y = y * jax.nn.silu(z)
        out = y @ out_proj_w.T
        return out + residual

    def _L0_attn_b_ref(hidden_states, norm_w, in_proj_w, conv_w, conv_b, dt_bias, A_log, D, ssm_norm_w, out_proj_w, post_norm_w, gate_w, up_w, down_w):
        import jax, jax.numpy as jnp
        import numpy as np
        D_MODEL = 128
        D_STATE = 128
        D_CONV = 4
        EXPAND = 2
        HEADDIM = 64
        D_INNER = EXPAND * D_MODEL
        NHEADS = D_INNER // HEADDIM
        CONV_DIM = D_INNER + 2 * D_STATE
        D_IN_PROJ = 2 * D_INNER + 2 * D_STATE + NHEADS
        INTER = (int(D_MODEL * 8 / 3) + 63) // 64 * 64
        EPS = 1e-06
        BATCH, SEQLEN = (2, 128)

        def rmsnorm(x, w):
            return x * jax.lax.rsqrt(jnp.mean(x * x, axis=-1, keepdims=True) + EPS) * w

        def _mixer(u, in_proj_w, conv_w, conv_b, dt_bias, A_log, D, ssm_norm_w, out_proj_w):
            b, l, _ = u.shape
            zxbcdt = u @ in_proj_w.T
            z = zxbcdt[..., :D_INNER]
            xBC = zxbcdt[..., D_INNER:D_INNER + CONV_DIM]
            dt = zxbcdt[..., -NHEADS:]
            xp = jnp.pad(xBC, ((0, 0), (D_CONV - 1, 0), (0, 0)))
            xBC = sum((xp[:, k:k + l, :] * conv_w[:, k] for k in range(D_CONV))) + conv_b
            xBC = jax.nn.silu(xBC)
            xs = xBC[..., :D_INNER].reshape(b, l, NHEADS, HEADDIM)
            Bm = xBC[..., D_INNER:D_INNER + D_STATE]
            Cm = xBC[..., -D_STATE:]
            dt = jax.nn.softplus(dt + dt_bias)
            A = -jnp.exp(A_log)

            def step(h, inp):
                dt_t, x_t, B_t, C_t = inp
                dA = jnp.exp(dt_t * A)
                h = h * dA[..., None, None] + jnp.einsum('bh,bhp,bn->bhpn', dt_t, x_t, B_t)
                y_t = jnp.einsum('bhpn,bn->bhp', h, C_t)
                return (h, y_t)
            h0 = jnp.zeros((b, NHEADS, HEADDIM, D_STATE), u.dtype)
            xsT = (jnp.moveaxis(dt, 1, 0), jnp.moveaxis(xs, 1, 0), jnp.moveaxis(Bm, 1, 0), jnp.moveaxis(Cm, 1, 0))
            _, yT = jax.lax.scan(step, h0, xsT)
            y = jnp.moveaxis(yT, 0, 1) + D[None, None, :, None] * xs
            y = y.reshape(b, l, D_INNER)
            y = rmsnorm(y * jax.nn.silu(z), ssm_norm_w)
            return y @ out_proj_w.T
        res = hidden_states
        h = rmsnorm(hidden_states, norm_w)
        h = _mixer(h, in_proj_w, conv_w, conv_b, dt_bias, A_log, D, ssm_norm_w, out_proj_w)
        x = res + h
        res = x
        h = rmsnorm(x, post_norm_w)
        h = jax.nn.silu(h @ gate_w.T) * (h @ up_w.T) @ down_w.T
        return res + h

    def _L0_ffn_ref(hidden_states, gate_weight, shared_gate_up, shared_down, experts_gate_up, experts_down):
        import jax, jax.numpy as jnp
        import numpy as np
        B, S, D = (4, 256, 128)
        E = 8
        TOPK = 2
        I = 938

        def _swiglu(x, gate_up, down):
            h = jnp.einsum('bsd,fd->bsf', x, gate_up)
            g, u = jnp.split(h, 2, axis=-1)
            return jnp.einsum('bsi,di->bsd', jax.nn.silu(g) * u, down)
        x = hidden_states
        out = _swiglu(x, shared_gate_up, shared_down)
        logits = jnp.einsum('bsd,ed->bse', x, gate_weight)
        probs = jax.nn.softmax(logits.astype(jnp.float32), axis=-1)
        top_p, sel = jax.lax.top_k(probs, TOPK)
        top_p = top_p / (jnp.sum(top_p, axis=-1, keepdims=True) + 1e-08)
        cw = jnp.sum(top_p[..., None] * jax.nn.one_hot(sel, E, dtype=top_p.dtype), axis=2)
        for e in range(E):
            y = _swiglu(x, experts_gate_up[e], experts_down[e])
            out = out + cw[..., e:e + 1] * y
        return out
    x = L0_attn_a_x
    x = x + _L0_attn_a_ref(_layernorm(x, axis=-1), L0_attn_a_norm_w, L0_attn_a_in_proj_w, L0_attn_a_conv_w, L0_attn_a_conv_b, L0_attn_a_x_proj_w, L0_attn_a_dt_proj_w, L0_attn_a_dt_proj_b, L0_attn_a_A_log, L0_attn_a_D, L0_attn_a_out_proj_w)
    x = x + _L0_ffn_ref(_layernorm(x, axis=-1), L0_ffn_gate_weight, L0_ffn_shared_gate_up, L0_ffn_shared_down, L0_ffn_experts_gate_up, L0_ffn_experts_down)
    x = x + _L0_attn_b_ref(_layernorm(x, axis=-1), L0_attn_b_norm_w, L0_attn_b_in_proj_w, L0_attn_b_conv_w, L0_attn_b_conv_b, L0_attn_b_dt_bias, L0_attn_b_A_log, L0_attn_b_D, L0_attn_b_ssm_norm_w, L0_attn_b_out_proj_w, L0_attn_b_post_norm_w, L0_attn_b_gate_w, L0_attn_b_up_w, L0_attn_b_down_w)
    x = x + _L0_ffn_ref(_layernorm(x, axis=-1), L0_ffn_gate_weight, L0_ffn_shared_gate_up, L0_ffn_shared_down, L0_ffn_experts_gate_up, L0_ffn_experts_down)
    return x

_drawn_inputs = setup_inputs


def setup_inputs(seed=0):
    import zlib

    import numpy as np

    out = dict(_drawn_inputs(seed))
    spreads = {'L0_attn_a_norm_w': (1.0, 0.2),
     'L0_attn_a_conv_b': (0.0, 0.1),
     'L0_attn_a_D': (1.0, 0.2),
     'L0_attn_b_norm_w': (1.0, 0.2),
     'L0_attn_b_conv_b': (0.0, 0.1),
     'L0_attn_b_ssm_norm_w': (1.0, 0.2),
     'L0_attn_b_post_norm_w': (1.0, 0.2)}
    factors = {}
    for name, (base, spread) in spreads.items():
        noise = np.random.default_rng([zlib.crc32(name.encode()), seed]).standard_normal(out[name].shape)
        drawn = base * np.exp(spread * noise) if base else spread * noise
        out[name] = jnp.asarray(drawn.astype(out[name].dtype))
    for name, factor in factors.items():
        out[name] = (out[name] * factor).astype(out[name].dtype)
    return out
```

```python
from contextlib import ExitStack

import numpy as np

import concourse.bass as bass
from concourse import mybir

F32 = mybir.dt.float32
F32R = mybir.dt.float32r
ALU = mybir.AluOpType
ACT = mybir.ActivationFunctionType
AX = mybir.AxisListType

P = 128
BATCH, SEQ = 2, 1024
T = BATCH * SEQ
CH = 512
NCH = T // CH
DI = 256
FT = DI // P
TAPS = 4
NST = 16
RANK = 8
PADC = 4
PADDED = SEQ + PADC
EXPERTS = 8
INTER = 938
NI = 7
TAIL = INTER - NI * P
UT = 64
GU = 2 * NI * P + UT + TAIL

VA_NORM, VA_CB, VA_DTB, VA_D, VA_ALOG = 0, 1, 3, 5, 7
VB_NORM, VB_POST, VB_SSM, VB_CB, VB_D = 39, 40, 41, 43, 47
NV = 49


class Core:

    def __init__(self, nc, ctx):
        self.nc, self.ctx = nc, ctx

    def sb(self, name, shape, dt=F32, ctx=None):
        return (ctx or self.ctx).enter_context(self.nc.sbuf_tensor(name, shape, dt))

    def sem(self, name, ctx=None):
        return (ctx or self.ctx).enter_context(self.nc.semaphore(name))


def cols(c):
    return slice(c * CH, (c + 1) * CH)


def load_stage(k, d):
    nc = k.nc
    k.x = k.sb("x", [P, T])
    k.big = k.sb("big", [P, 9, T])
    k.xn = k.big[:, 0, :]
    k.x_hi = k.sb("x_hi", [P, T], F32R)
    k.x_lo = k.sb("x_lo", [P, T], F32R)
    k.vec = k.sb("vec", [P, NV])
    k.ones = k.sb("ones", [P, P])
    k.eye = k.sb("eye", [P, P])
    k.eps5 = k.sb("eps5", [P, 1])
    k.eps6 = k.sb("eps6", [P, 1])
    k.sel = k.sb("sel", [64, 32, P], F32R)
    k.rows = k.sb("rows", [64, T], F32R)
    k.ps = k.ctx.enter_context(nc.psum_tensor("ps", [P, 8, CH], F32))
    k.x_loaded = k.sem("x_loaded")
    k.vec_loaded = k.sem("vec_loaded")
    k.eye_loaded = k.sem("eye_loaded")
    k.order = k.sb("order", [P, EXPERTS])
    consts_set = k.sem("consts_set")
    with nc.Block() as block:

        @block.sync
        def _(sp):
            for c in range(NCH):
                sp.dma_start(k.x[:, cols(c)], d["xT"][:, cols(c)]).then_inc(k.x_loaded, 16)
            sp.dma_start(k.vec[:, :], d["vec"]).then_inc(k.vec_loaded, 16)
            sp.dma_start(k.eye[:, :], d["eye"]).then_inc(k.eye_loaded, 16)
            sp.dma_start(k.order[:, :], d["order"].partition_broadcast(P)).then_inc(k.eye_loaded, 16)

        @block.vector
        def _(dve):
            nc.vector.memset(k.ones[:, :], 1.0 / P)
            nc.vector.memset(k.eps5[:, :], 1e-5)
            nc.vector.memset(k.eps6[:, :], 1e-6).then_inc(consts_set, 1)
            dve.wait_ge(k.eye_loaded, 32)
            for half in range(2):
                src = k.eye[32 * half:32 * half + 32, 32 * half:32 * half + 32]
                nc.vector.tensor_copy(k.sel[32 * half:32 * half + 32, :, :],
                                      src.unsqueeze(2).to_broadcast([32, 32, P])).then_inc(consts_set, 1)
            dve.wait_ge(consts_set, 3)


def norm_stage(k, tag, src, dst, center, eps, weight=None, rms_eps=None, out=None, split=False):
    nc = k.nc
    stage = ExitStack()
    sq = k.sb(tag + "_sq", [P, T], ctx=stage)
    rs = k.sb(tag + "_rs", [P, T], ctx=stage)
    mean_ready, centred, squared, var_ready, rstd_ready, normed, squared2, ms_ready, rms_ready, scaled, \
        high_ready, low_ready, log_done = [k.sem(f"{tag}_{n}", stage) for n in (
            "mean_ready centred squared var_ready rstd_ready normed squared2 ms_ready rms_ready scaled "
            "high_ready low_ready log_done").split()]
    final = out if out is not None else dst

    with stage, nc.Block() as block:

        @block.tensor
        def _(pe):
            if center:
                pe.wait_ge(k.x_loaded, 16 * NCH)
                for c in range(NCH):
                    nc.tensor.matmul(k.ps[:, c, :], k.ones[:, :], src[:, cols(c)], start=True, stop=True)\
                        .then_inc(mean_ready, 1)
                for c in range(NCH):
                    pe.wait_ge(squared, c + 1)
                    nc.tensor.matmul(k.ps[:, 4 + c, :], k.ones[:, :], sq[:, cols(c)], start=True, stop=True)\
                        .then_inc(var_ready, 1)
            if rms_eps is not None:
                for c in range(NCH):
                    pe.wait_ge(squared2, c + 1)
                    nc.tensor.matmul(k.ps[:, c, :], k.ones[:, :], sq[:, cols(c)], start=True, stop=True)\
                        .then_inc(ms_ready, 1)

        @block.scalar
        def _(act):
            logs = 0
            if center:
                for c in range(NCH):
                    act.wait_ge(centred, c + 1)
                    nc.scalar.activation(sq[:, cols(c)], dst[:, cols(c)], ACT.Square).then_inc(squared, 1)
                for c in range(NCH):
                    act.wait_ge(var_ready, c + 1)
                    nc.scalar.activation(rs[:, cols(c)], k.ps[:, 4 + c, :], ACT.Ln, bias=eps[:, 0:1])\
                        .then_inc(log_done, 1)
                    logs += 1
                    act.wait_ge(log_done, logs)
                    nc.scalar.activation(rs[:, cols(c)], rs[:, cols(c)], ACT.Exp, scale=-0.5)\
                        .then_inc(rstd_ready, 1)
            if rms_eps is not None:
                for c in range(NCH):
                    if center:
                        act.wait_ge(normed, c + 1)
                    nc.scalar.activation(sq[:, cols(c)], dst[:, cols(c)], ACT.Square).then_inc(squared2, 1)
                for c in range(NCH):
                    act.wait_ge(ms_ready, c + 1)
                    nc.scalar.activation(rs[:, cols(c)], k.ps[:, c, :], ACT.Ln, bias=rms_eps[:, 0:1])\
                        .then_inc(log_done, 1)
                    logs += 1
                    act.wait_ge(log_done, logs)
                    nc.scalar.activation(rs[:, cols(c)], rs[:, cols(c)], ACT.Exp, scale=-0.5)\
                        .then_inc(rms_ready, 1)
            if split:
                for c in range(NCH):
                    act.wait_ge(scaled if rms_eps is not None else normed, c + 1)
                    nc.scalar.activation(k.x_hi[:, cols(c)], final[:, cols(c)], ACT.Copy).then_inc(high_ready, 1)

        @block.vector
        def _(dve):
            if center:
                for c in range(NCH):
                    dve.wait_ge(mean_ready, c + 1)
                    nc.vector.tensor_tensor(dst[:, cols(c)], src[:, cols(c)], k.ps[:, c, :], ALU.subtract)\
                        .then_inc(centred, 1)
                for c in range(NCH):
                    dve.wait_ge(rstd_ready, c + 1)
                    nc.vector.tensor_tensor(dst[:, cols(c)], dst[:, cols(c)], rs[:, cols(c)], ALU.mult)\
                        .then_inc(normed, 1)
            if rms_eps is not None:
                for c in range(NCH):
                    dve.wait_ge(rms_ready, c + 1)
                    where = out[:, cols(c)] if len(out.shape) == 2 else out[:, c // 2, PADC + (c % 2) * CH:
                                                                           PADC + (c % 2 + 1) * CH]
                    nc.vector.scalar_tensor_tensor(out=where, in0=dst[:, cols(c)], scalar=weight,
                                                   in1=rs[:, cols(c)], op0=ALU.mult, op1=ALU.mult)\
                        .then_inc(scaled, 1)
            if split:
                for c in range(NCH):
                    dve.wait_ge(high_ready, c + 1)
                    nc.vector.tensor_tensor(k.x_lo[:, cols(c)], final[:, cols(c)],
                                            k.x_hi[:, cols(c)].bitcast(F32), ALU.subtract).then_inc(low_ready, 1)

    with nc.Block() as block:

        @block.sync
        def _(sp):
            for used in (mean_ready, centred, squared, var_ready, rstd_ready, normed, squared2, ms_ready, rms_ready,
                         scaled, high_ready, low_ready, log_done):
                sp.sem_clear(used)


def mixer_a_stage(k, d):
    nc = k.nc
    stage = ExitStack()
    sb = lambda name, shape, dt=F32: k.sb("a_" + name, shape, dt, ctx=stage)
    sem = lambda name: k.sem("a_" + name)
    w_in = sb("w_in", [P, 2 * DI])
    w_tap = sb("w_tap", [P, TAPS, DI])
    taps = sb("taps", [P, TAPS, DI])
    w_x = sb("w_x", [P, FT, 40])
    w_dt = sb("w_dt", [40, DI])
    w_out = sb("w_out", [P, FT, P])
    xp = sb("xp", [P, BATCH, PADDED])
    neg_a = sb("neg_a", [P, FT, NST])
    u = k.big[:, 1:3, :]
    sz = k.big[:, 3:5, :]
    delta = k.big[:, 5:7, :]
    du = k.big[:, 7:9, :]
    dt_row = sb("dt_row", [40, T])
    ps = k.ps

    w_loaded, taps_loaded, pad_zero, taps_ready, xz_ready, act_done, bc_ready, high_done, rows_done, dt_ready, \
        pre_ready, abs_done, exp_done, log_done, delta_ready, du_ready, a_ready = [sem(n) for n in (
            "w_loaded taps_loaded pad_zero taps_ready xz_ready act_done bc_ready high_done rows_done dt_ready "
            "pre_ready abs_done exp_done log_done delta_ready du_ready a_ready").split()]

    with nc.Block() as block:

        @block.sync
        def _(sp):
            sp.dma_start(taps[:, :, :].rearrange("p a b -> p (a b)"), d["tapsA"].partition_broadcast(P))\
                .then_inc(taps_loaded, 16)
            sp.dma_start(w_in[:, :], d["w_inA"]).then_inc(w_loaded, 16)
            sp.dma_start(w_x[:, :, :], d["w_xA"]).then_inc(w_loaded, 16)
            sp.dma_start(w_dt[32:40, :], d["w_dtA"]).then_inc(w_loaded, 16)
            sp.dma_start(w_out[:, :, :], d["w_outA"]).then_inc(w_loaded, 16)

        @block.gpsimd
        def _(pool):
            nc.gpsimd.memset(xp[:, :, 0:PADC], 0.0).then_inc(pad_zero, 1)

    norm_stage(k, "na", k.x, k.xn, True, k.eps5, weight=k.vec[:, VA_NORM:VA_NORM + 1], rms_eps=k.eps5, out=xp)

    with nc.Block() as block:

        @block.tensor
        def _(pe):
            pe.wait_ge(w_loaded, 16 * 4)
            pe.wait_ge(taps_ready, TAPS)
            pe.wait_ge(pad_zero, 1)

            def in_proj(c):
                b, t0 = divmod(c * CH, SEQ)
                for j in range(2 * FT):
                    n = c * 2 * FT + j
                    if n >= 4:
                        pe.wait_ge(act_done, n - 3)
                    if j < FT:
                        for tap in range(TAPS):
                            off = PADC + t0 - (TAPS - 1) + tap
                            last = nc.tensor.matmul(ps[:, n % 4, :], w_tap[:, tap, j * P:(j + 1) * P],
                                                    xp[:, b, off:off + CH], start=(tap == 0), stop=(tap == TAPS - 1))
                    else:
                        last = nc.tensor.matmul(ps[:, n % 4, :], w_in[:, j * P:(j + 1) * P],
                                                xp[:, b, PADC + t0:PADC + t0 + CH], start=True, stop=True)
                    last.then_inc(xz_ready, 1)

            def x_proj(c):
                pe.wait_ge(act_done, c * 2 * FT + FT)
                if c >= 1:
                    pe.wait_ge(rows_done, c)
                for f in range(FT):
                    last = nc.tensor.matmul(ps[0:40, 4, :], w_x[:, f, :], u[:, f, cols(c)],
                                            start=(f == 0), stop=(f == FT - 1))
                last.then_inc(bc_ready, 1)

            def dt_proj(c):
                pe.wait_ge(rows_done, c + 1)
                for f in range(FT):
                    n = c * FT + f
                    if n >= 2:
                        pe.wait_ge(pre_ready, n - 1)
                    nc.tensor.matmul(ps[:, 5 + n % 2, :], w_dt[32:40, f * P:(f + 1) * P],
                                     dt_row[32:40, cols(c)], start=True, stop=True).then_inc(dt_ready, 1)

            in_proj(0)
            for c in range(NCH):
                if c + 1 < NCH:
                    in_proj(c + 1)
                x_proj(c)
                dt_proj(c)

        @block.scalar
        def _(act):
            act.wait_ge(k.vec_loaded, 16)
            for c in range(NCH):
                for j in range(2 * FT):
                    n = c * 2 * FT + j
                    act.wait_ge(xz_ready, n + 1)
                    if j < FT:
                        nc.scalar.activation(u[:, j, cols(c)], ps[:, n % 4, :], ACT.Silu,
                                             bias=k.vec[:, VA_CB + j:VA_CB + j + 1]).then_inc(act_done, 1)
                    else:
                        nc.scalar.activation(sz[:, j - FT, cols(c)], ps[:, n % 4, :], ACT.Silu).then_inc(act_done, 1)
            nc.scalar.activation(neg_a[:, :, :], k.vec[:, VA_ALOG:VA_ALOG + FT * NST]
                                 .rearrange("p (f n) -> p f n", f=FT), ACT.Exp).then_inc(a_ready, 1)
            for b in range(BATCH):
                at = slice(b * SEQ, (b + 1) * SEQ)
                act.wait_ge(pre_ready, (b + 1) * 2 * FT)
                nc.scalar.activation(du[:, :, at], delta[:, :, at], ACT.Abs).then_inc(abs_done, 1)
                act.wait_ge(abs_done, b + 1)
                nc.scalar.activation(du[:, :, at], du[:, :, at], ACT.Exp, scale=-1.0).then_inc(exp_done, 1)
                act.wait_ge(exp_done, b + 1)
                nc.scalar.activation(du[:, :, at], du[:, :, at], ACT.Ln, bias=1.0).then_inc(log_done, 1)

        @block.vector
        def _(dve):
            dve.wait_ge(taps_loaded, 16)
            dve.wait_ge(w_loaded, 16 * 4)
            for tap in range(TAPS):
                nc.vector.tensor_tensor(w_tap[:, tap, :], w_in[:, 0:DI], taps[:, tap, :], ALU.mult)\
                    .then_inc(taps_ready, 1)
            dve.wait_ge(k.vec_loaded, 16)
            for c in range(NCH):
                dve.wait_ge(bc_ready, c + 1)
                nc.vector.tensor_copy(k.rows[0:32, cols(c)], ps[0:32, 4, :]).then_inc(high_done, 1)
                nc.vector.tensor_copy(dt_row[32:40, cols(c)], ps[32:40, 4, :])
                dve.wait_ge(high_done, c + 1)
                nc.vector.tensor_tensor(k.rows[32:64, cols(c)], ps[0:32, 4, :],
                                        k.rows[0:32, cols(c)].bitcast(F32), ALU.subtract).then_inc(rows_done, 1)
                for f in range(FT):
                    n = c * FT + f
                    dve.wait_ge(dt_ready, n + 1)
                    nc.vector.tensor_scalar(delta[:, f, cols(c)], ps[:, 5 + n % 2, :],
                                            k.vec[:, VA_DTB + f:VA_DTB + f + 1], None, ALU.add).then_inc(pre_ready, 1)
            dve.wait_ge(a_ready, 1)
            nc.vector.tensor_scalar(neg_a[:, :, :], neg_a[:, :, :], -1.0, None, ALU.mult).then_inc(a_ready, 1)
            for b in range(BATCH):
                at = slice(b * SEQ, (b + 1) * SEQ)
                dve.wait_ge(log_done, b + 1)
                nc.vector.scalar_tensor_tensor(out=delta[:, :, at], in0=delta[:, :, at], scalar=0.0,
                                               in1=du[:, :, at], op0=ALU.max, op1=ALU.add).then_inc(delta_ready, 1)
                dve.wait_ge(delta_ready, b + 1)
                nc.vector.tensor_tensor(du[:, :, at], delta[:, :, at], u[:, :, at], ALU.mult).then_inc(du_ready, 1)

    HALVES = SEQ // CH
    STEPS = NST * FT
    DEPTH = 4
    decayed_in = sb("b_u", [P, DEPTH, CH])
    h = sb("h", [P, DEPTH, CH])
    hc = sb("hc", [P, DEPTH, CH])
    c_sb = sb("c_sb", [P, 2, CH])
    state = sb("state", [P, STEPS])
    yz = sb("yz", [P, FT, CH])
    yd = sb("yd", [P, FT, CH])
    Y, B, C, A, O = 0, 2, 4, 5, 7
    b_ready, c_ready, c_copied, decay_ready, bu_ready, scanned, saved, hc_ready, y_added, y_ready, yd_ready, \
        yz_ready, out_ready, res_ready, x_added = [sem(n) for n in (
            "b_ready c_ready c_copied decay_ready bu_ready scanned saved hc_ready y_added y_ready yd_ready "
            "yz_ready out_ready res_ready x_added").split()]

    def at_half(b, half):
        return bass.ds(b * SEQ + half * CH, CH)

    with stage, nc.Block() as block:

        @block.tensor
        def _(pe):
            def half_sequence(b, half):
                first = half == 0 and b == 0
                g = b * HALVES + half
                def broadcast(n):
                    m = g * NST + n
                    if not (first and n < 2):
                        pe.wait_ge(bu_ready, (m - 1) * FT)
                    nc.tensor.matmul(ps[:, B + n % 2, :], k.sel[:, n, :], k.rows[:, at_half(b, half)],
                                     start=True, stop=True).then_inc(b_ready, 1)
                    if not (first and n < 1):
                        pe.wait_ge(c_copied, m)
                    nc.tensor.matmul(ps[:, C, :], k.sel[:, NST + n, :], k.rows[:, at_half(b, half)],
                                     start=True, stop=True).then_inc(c_ready, 1)

                def accumulate(n):
                    for f in range(FT):
                        s = n * FT + f
                        pe.wait_ge(hc_ready, g * STEPS + s + 1)
                        if n == 0 and not first:
                            pe.wait_ge(yd_ready, (g - 1) * FT + f + 1)
                        nc.tensor.matmul(ps[:, Y + f, :], k.eye[:, :], hc[:, s % DEPTH, :],
                                         start=(n == 0), stop=(n == NST - 1)).then_inc(y_added, 1)

                broadcast(0)
                broadcast(1)
                for n in range(2, NST):
                    broadcast(n)
                    accumulate(n - 2)
                accumulate(NST - 2)
                accumulate(NST - 1)
                if not first:
                    pe.wait_ge(res_ready, g)
                for f in range(FT):
                    pe.wait_ge(yz_ready, g * FT + f + 1)
                    last = nc.tensor.matmul(ps[:, O, :], w_out[:, f, :], yz[:, f, :], start=(f == 0), stop=(f == FT - 1))
                last.then_inc(out_ready, 1)

            SEQUENCES(pe, half_sequence, HALVES)

        @block.scalar
        def _(act):
            def half_sequence(b, half):
                first = half == 0 and b == 0
                g = b * HALVES + half
                for n in range(NST):
                    for f in range(FT):
                        s = n * FT + f
                        if not (first and s < 2):
                            act.wait_ge(scanned, g * STEPS + s - 1)
                        nc.scalar.activation(ps[:, A + s % 2, :], delta[:, f, at_half(b, half)], ACT.Exp,
                                             scale=neg_a[:, f, n:n + 1]).then_inc(decay_ready, 1)
                        if f == 0:
                            act.wait_ge(c_ready, g * NST + n + 1)
                            if not (first and n < 2):
                                act.wait_ge(hc_ready, g * STEPS + s - 2)
                            nc.scalar.activation(c_sb[:, n % 2, :], ps[:, C, :], ACT.Copy).then_inc(c_copied, 1)
                        if half + 1 < HALVES and s >= 1:
                            act.wait_ge(scanned, g * STEPS + s)
                            nc.scalar.activation(state[:, s - 1:s], h[:, (s - 1) % DEPTH, CH - 1:CH], ACT.Copy)\
                                .then_inc(saved, 1)
                if half + 1 < HALVES:
                    act.wait_ge(scanned, (g + 1) * STEPS)
                    nc.scalar.activation(state[:, STEPS - 1:STEPS], h[:, (STEPS - 1) % DEPTH, CH - 1:CH], ACT.Copy)\
                        .then_inc(saved, 1)

            SEQUENCES(act, half_sequence, HALVES)

        @block.vector
        def _(dve):
            def half_sequence(b, half):
                first = half == 0 and b == 0
                g = b * HALVES + half
                def times_b(s):
                    n, f = divmod(s, FT)
                    if f == 0:
                        dve.wait_ge(b_ready, g * NST + n + 1)
                    if not (first and s < DEPTH):
                        dve.wait_ge(scanned, g * STEPS + s - DEPTH + 1)
                    nc.vector.tensor_tensor(decayed_in[:, s % DEPTH, :], du[:, f, at_half(b, half)], ps[:, B + n % 2, :],
                                            ALU.mult).then_inc(bu_ready, 1)

                times_b(0)
                for s in range(STEPS):
                    if s + 1 < STEPS:
                        times_b(s + 1)
                    dve.wait_ge(decay_ready, g * STEPS + s + 1)
                    dve.wait_ge(bu_ready, g * STEPS + s + 1)
                    if not (first and s < DEPTH):
                        dve.wait_ge(hc_ready, g * STEPS + s - DEPTH + 1)
                    if half == 0 and s >= DEPTH:
                        dve.wait_ge(saved, b * STEPS + s - DEPTH + 1)
                    if half == 1:
                        dve.wait_ge(saved, b * STEPS + (STEPS if s < DEPTH else s + 1))
                    initial = state[:, s:s + 1] if half else 0.0
                    nc.vector.tensor_tensor_scan(h[:, s % DEPTH, :], ps[:, A + s % 2, :], decayed_in[:, s % DEPTH, :],
                                                 initial, ALU.mult, ALU.add).then_inc(scanned, 1)
                for f in range(FT):
                    dve.wait_ge(y_added, (g + 1) * STEPS)
                    nc.vector.scalar_tensor_tensor(out=yd[:, f, :], in0=u[:, f, at_half(b, half)],
                                                   scalar=k.vec[:, VA_D + f:VA_D + f + 1], in1=ps[:, Y + f, :],
                                                   op0=ALU.mult, op1=ALU.add).then_inc(yd_ready, 1)
                for f in range(FT):
                    dve.wait_ge(yd_ready, g * FT + f + 1)
                    nc.vector.tensor_tensor(yz[:, f, :], yd[:, f, :], sz[:, f, at_half(b, half)], ALU.mult)\
                        .then_inc(yz_ready, 1)
                dve.wait_ge(out_ready, g + 1)
                nc.vector.tensor_tensor(yd[:, 0, :], ps[:, O, :], k.xn[:, at_half(b, half)], ALU.add)\
                    .then_inc(res_ready, 1)
                dve.wait_ge(res_ready, g + 1)
                nc.vector.tensor_tensor(k.x[:, at_half(b, half)], k.x[:, at_half(b, half)], yd[:, 0, :], ALU.add)\
                    .then_inc(x_added, 1)

            SEQUENCES(dve, half_sequence, HALVES)

        @block.gpsimd
        def _(pool):
            def half_sequence(b, half):
                first = half == 0 and b == 0
                g = b * HALVES + half
                for s in range(STEPS):
                    n, f = divmod(s, FT)
                    pool.wait_ge(scanned, g * STEPS + s + 1)
                    if f == 0:
                        pool.wait_ge(c_copied, g * NST + n + 1)
                    if not (first and s < DEPTH):
                        pool.wait_ge(y_added, g * STEPS + s - DEPTH + 1)
                    nc.gpsimd.tensor_tensor(hc[:, s % DEPTH, :], h[:, s % DEPTH, :], c_sb[:, n % 2, :], ALU.mult)\
                        .then_inc(hc_ready, 1)

            SEQUENCES(pool, half_sequence, HALVES)


def SEQUENCES(eng, half_sequence, halves):
    for b in range(BATCH):
        for half in range(halves):
            half_sequence(b, half) if b == 0 else half_sequence(b, half)


def ffn_stage(k, d, tag):
    nc, ps = k.nc, k.ps
    norm_stage(k, tag + "n", k.x, k.xn, True, k.eps5, split=True)
    stage = ExitStack()
    sb = lambda name, shape, dt=F32, ctx=None: k.sb(f"{tag}_{name}", shape, dt, ctx=ctx or stage)
    sem = lambda name: k.sem(f"{tag}_{name}")
    TT = T // P
    ORDERS = EXPERTS + 1
    TILES = NI + 1
    PER = NCH * TILES

    router = ExitStack()
    w_gate = sb("w_gate", [P, EXPERTS], ctx=router)
    names = "logit prob taken rank hit spare"
    logit, prob, taken, rank, hit, spare = [sb(n, [P, TT, EXPERTS], ctx=router) for n in names.split()]
    top, best, den, first_max = [sb(n, [P, TT], ctx=router) for n in "top best den first_max".split()]
    gate_loaded, logits_ready, step, exp_ready, weights_ready, transposed, rows_high, rows_done = [sem(n) for n in (
        "gate_loaded logits_ready router_step exp_ready weights_ready transposed rows_high rows_done").split()]

    def wide(v):
        return v[:, :].unsqueeze(2).to_broadcast([P, TT, EXPERTS])

    with router, nc.Block() as block:

        @block.sync
        def _(sp):
            sp.dma_start(w_gate[:, :], d["w_gateF"]).then_inc(gate_loaded, 16)

        @block.tensor
        def _(pe):
            pe.wait_ge(gate_loaded, 16)
            for t in range(TT):
                last = nc.tensor.matmul(ps[:, 0, t * EXPERTS:(t + 1) * EXPERTS], k.xn[:, t * P:(t + 1) * P],
                                        w_gate[:, :], start=True, stop=True)
            last.then_inc(logits_ready, 1)
            pe.wait_ge(weights_ready, 1)
            for t in range(TT):
                last = nc.tensor.transpose(ps[0:EXPERTS, 1 + t // 4, (t % 4) * P:(t % 4 + 1) * P], taken[:, t, :],
                                           k.eye[:, :])
                if t % 4 == 3:
                    last.then_inc(transposed, 1)

        @block.scalar
        def _(act):
            act.wait_ge(step, 2)
            nc.scalar.activation(prob[:, :, :], logit[:, :, :], ACT.Exp).then_inc(exp_ready, 1)

        @block.vector
        def _(dve):
            done = [0]

            def then(ins):
                done[0] += 1
                ins.then_inc(step, 1)
                dve.wait_ge(step, done[0])

            dve.wait_ge(logits_ready, 1)
            logits = ps[:, 0, 0:TT * EXPERTS].rearrange("p (t e) -> p t e", e=EXPERTS)
            then(nc.vector.tensor_reduce(top[:, :], logits, AX.X, ALU.max))
            then(nc.vector.tensor_tensor(logit[:, :, :], logits, wide(top), ALU.subtract))
            dve.wait_ge(exp_ready, 1)
            then(nc.vector.tensor_reduce(den[:, :], prob[:, :, :], AX.X, ALU.add))
            then(nc.vector.reciprocal(den[:, :], den[:, :]))
            then(nc.vector.tensor_tensor(prob[:, :, :], prob[:, :, :], wide(den), ALU.mult))
            then(nc.vector.tensor_copy(spare[:, :, :], prob[:, :, :]))
            for pick in range(2):
                then(nc.vector.tensor_reduce(best[:, :], spare[:, :, :], AX.X, ALU.max))
                then(nc.vector.tensor_tensor(rank[:, :, :], spare[:, :, :], wide(best), ALU.is_ge))
                then(nc.vector.tensor_tensor(rank[:, :, :], rank[:, :, :],
                                             k.order[:, :].unsqueeze(1).to_broadcast([P, TT, EXPERTS]), ALU.mult))
                then(nc.vector.tensor_reduce(first_max[:, :], rank[:, :, :], AX.X, ALU.max))
                then(nc.vector.tensor_tensor(hit[:, :, :], rank[:, :, :], wide(first_max), ALU.is_equal))
                if pick == 0:
                    then(nc.vector.tensor_copy(den[:, :], best[:, :]))
                    then(nc.vector.tensor_copy(taken[:, :, :], hit[:, :, :]))
                    then(nc.vector.scalar_tensor_tensor(out=spare[:, :, :], in0=hit[:, :, :], scalar=-4.0,
                                                        in1=prob[:, :, :], op0=ALU.mult, op1=ALU.add))
                else:
                    then(nc.vector.scalar_tensor_tensor(out=den[:, :], in0=den[:, :], scalar=1e-8,
                                                        in1=best[:, :], op0=ALU.add, op1=ALU.add))
                    then(nc.vector.tensor_tensor(taken[:, :, :], taken[:, :, :], hit[:, :, :], ALU.add))
            then(nc.vector.reciprocal(den[:, :], den[:, :]))
            then(nc.vector.tensor_tensor(taken[:, :, :], taken[:, :, :], prob[:, :, :], ALU.mult))
            nc.vector.tensor_tensor(taken[:, :, :], taken[:, :, :], wide(den), ALU.mult).then_inc(weights_ready, 1)
            for c in range(NCH):
                dve.wait_ge(transposed, c + 1)
                nc.vector.tensor_copy(k.rows[0:EXPERTS, cols(c)], ps[0:EXPERTS, 1 + c, :]).then_inc(rows_high, 1)
                dve.wait_ge(rows_high, c + 1)
                nc.vector.tensor_tensor(k.rows[32:32 + EXPERTS, cols(c)], ps[0:EXPERTS, 1 + c, :],
                                        k.rows[0:EXPERTS, cols(c)].bitcast(F32), ALU.subtract).then_inc(rows_done, 1)

    raw_gu = sb("raw_gu", [P, GU])
    raw_dn = sb("raw_dn", [P, TILES, P])
    gu_hi, gu_lo = [sb(n, [P, 2, GU], F32R) for n in ("gu_hi", "gu_lo")]
    dn_hi, dn_lo = [sb(n, [P, 2, TILES * P], F32R) for n in ("dn_hi", "dn_lo")]
    cw = k.big
    gate = sb("gate", [P, 2, CH])
    prod = sb("prod", [P, 2, CH])
    p_hi, p_lo = [sb(n, [P, 4, CH], F32R) for n in ("p_hi", "p_lo")]
    ysc = sb("ysc", [P, 2, CH])
    zero = sb("zero", [P, 1])
    G, U, Y, W = 0, 2, 4, 6
    raw_loaded, gap_zero, split_step, w_ready, g_ready, gu_ready, silu_done, prod_done, high_ready, \
        low_ready, tile_summed, ones_set, scaled, cw_ready, cw_copied, x_added = [sem(n) for n in (
            "raw_loaded gap_zero split_step w_ready g_ready gu_ready silu_done prod_done high_ready "
            "low_ready tile_summed ones_set scaled cw_ready cw_copied x_added").split()]
    PIECES = [(raw_gu, gu_hi, gu_lo, a, min(a + CH, GU)) for a in range(0, GU, CH)]
    NPIECE = len(PIECES) + 2

    def all_orders(eng, emit):
        emit(0, 0)
        with eng.Fori(0, EXPERTS // 2) as turn:
            for par in range(2):
                emit(turn * 2 + (1 + par), (1 + par) % 2)

    def k_of(i):
        return P if i < NI else TAIL

    with stage, nc.Block() as block:

        @block.sync
        def _(sp):
            def load(n):
                sp.dma_start(raw_gu[:, 0:2 * NI * P + TAIL], d["gu"][n, :, 0:2 * NI * P + TAIL])\
                    .then_inc(raw_loaded, 16)
                sp.dma_start(raw_gu[:, GU - TAIL:GU], d["gu"][n, :, 2 * NI * P + TAIL:2 * NI * P + 2 * TAIL])\
                    .then_inc(raw_loaded, 16)
                sp.dma_start(raw_dn[:, 0:NI, :], d["dn"][n, 0:NI * P, :].rearrange("(i p) m -> p i m", p=P))\
                    .then_inc(raw_loaded, 16)
                sp.dma_start(raw_dn[0:TAIL, NI, :], d["dn"][n, NI * P:INTER, :]).then_inc(raw_loaded, 16)

            sp.wait_ge(gap_zero, 2)
            load(0)
            with sp.Fori(1, ORDERS) as n:
                sp.wait_ge(w_ready, n * NPIECE)
                load(n)

        @block.gpsimd
        def _(pool):
            def split(n, buf):
                pool.wait_ge(raw_loaded, n * 64 + 64)
                if not isinstance(n, int) or n >= 2:
                    pool.wait_ge(tile_summed, n * PER - PER)
                parts = [(raw_gu[:, a:b], gu_hi[:, buf, a:b], gu_lo[:, buf, a:b]) for _, _, _, a, b in PIECES]
                dn = raw_dn[:, :, :].rearrange("p i m -> p (i m)")
                parts += [(dn[:, a:a + CH], dn_hi[:, buf, a:a + CH], dn_lo[:, buf, a:a + CH]) for a in (0, CH)]
                for j, (src, hi, lo) in enumerate(parts):
                    nc.gpsimd.tensor_tensor(hi, src, zero[:, :].to_broadcast([P, src.shape[1]]), ALU.add).then_inc(split_step, 1)
                    if j:
                        s, h, l = parts[j - 1]
                        pool.wait_ge(split_step, n * NPIECE + j)
                        nc.gpsimd.tensor_tensor(l, s, h.bitcast(F32), ALU.subtract).then_inc(w_ready, 1)
                pool.wait_ge(split_step, n * NPIECE + NPIECE)
                s, h, l = parts[-1]
                nc.gpsimd.tensor_tensor(l, s, h.bitcast(F32), ALU.subtract).then_inc(w_ready, 1)

            def add(n, last=False):
                for c in range(NCH):
                    g = n * NCH + c
                    pool.wait_ge(scaled, g + 1)
                    if not (isinstance(n, int) and n == 0):
                        pool.wait_ge(x_added, g - NCH + 1)
                    nc.gpsimd.tensor_tensor(k.x[:, cols(c)], k.x[:, cols(c)], ysc[:, c % 2, :], ALU.add)\
                        .then_inc(x_added, 1)

            nc.gpsimd.memset(raw_gu[:, GU - TAIL - (UT - TAIL):GU - TAIL], 0.0).then_inc(gap_zero, 1)
            nc.gpsimd.memset(raw_dn[:, NI, :], 0.0).then_inc(gap_zero, 1)
            nc.gpsimd.memset(zero[:, :], 0.0).then_inc(gap_zero, 1)
            pool.wait_ge(gap_zero, 3)
            nc.gpsimd.memset(cw[:, 0, :], 1.0).then_inc(ones_set, 1)
            split(0, 0)
            split(1, 1)
            add(0)
            split(2, 0)
            with pool.Fori(0, (ORDERS - 3) // 2) as turn:
                for par in range(2):
                    n = turn * 2 + (1 + par)
                    add(n)
                    split(n + 2, (1 + par) % 2)
            add(ORDERS - 2)
            add(ORDERS - 1)

        @block.tensor
        def _(pe):
            def product(out, w_hi, w_lo, v_hi, v_lo, start, stop):
                nc.tensor.matmul(out, w_hi, v_hi, start=start, stop=False)
                nc.tensor.matmul(out, w_hi, v_lo, start=False, stop=False)
                return nc.tensor.matmul(out, w_lo, v_hi, start=False, stop=stop)

            def gate_up(n, buf, c, i):
                q = n * PER + (c * TILES + i)
                xs = (k.x_hi[:, cols(c)], k.x_lo[:, cols(c)])
                if not isinstance(n, int) or c * TILES + i >= 2:
                    pe.wait_ge(prod_done, q - 1)
                if i < NI:
                    a = i * P
                    product(ps[:, G + i % 2, :], gu_hi[:, buf, a:a + P], gu_lo[:, buf, a:a + P], *xs, True, True)\
                        .then_inc(g_ready, 1)
                    a += NI * P
                    product(ps[:, U + i % 2, :], gu_hi[:, buf, a:a + P], gu_lo[:, buf, a:a + P], *xs, True, True)\
                        .then_inc(gu_ready, 1)
                else:
                    a, m = 2 * NI * P, UT + TAIL
                    product(ps[0:m, G + i % 2, :], gu_hi[:, buf, a:a + m], gu_lo[:, buf, a:a + m], *xs, True, True)\
                        .then_inc(g_ready, 1)

            def down(n, buf, c, i):
                q = n * PER + (c * TILES + i)
                j = (c * TILES + i) % 2
                if i == 0 and not (isinstance(n, int) and n == 0 and c < 2):
                    pe.wait_ge(scaled, n * NCH + c - 1)
                pe.wait_ge(low_ready, q + 1)
                m, a, b3 = k_of(i), i * P, (c * TILES + i) % 4
                last = product(ps[:, Y + c % 2, :], dn_hi[0:m, buf, a:a + P], dn_lo[0:m, buf, a:a + P],
                               p_hi[0:m, b3, :], p_lo[0:m, b3, :], i == 0, i == TILES - 1)
                last.then_inc(tile_summed, 1)

            def expert(n, buf):
                pe.wait_ge(w_ready, n * NPIECE + NPIECE)
                for c in range(NCH):
                    for i in range(TILES):
                        gate_up(n, buf, c, i)
                        at = c * TILES + i
                        if isinstance(n, int):
                            if at:
                                pe.wait_ge(cw_copied, at)
                            nc.tensor.matmul(ps[:, W, :], k.sel[:, i, :], k.rows[:, cols(c)], start=True, stop=True)\
                                .then_inc(cw_ready, 1)
                        if at >= 2:
                            down(n, buf, (at - 2) // TILES, (at - 2) % TILES)
                        elif not isinstance(n, int):
                            down(n - 1, 1 - buf, NCH - 1, TILES - 2 + at)

            all_orders(pe, expert)
            for i in (TILES - 2, TILES - 1):
                down(ORDERS - 1, (ORDERS - 1) % 2, NCH - 1, i)

        @block.scalar
        def _(act):
            def high(n, at):
                q, m = n * PER + at, k_of(at % TILES)
                act.wait_ge(prod_done, q + 1)
                if not isinstance(n, int) or at >= 4:
                    act.wait_ge(tile_summed, q - 3)
                nc.scalar.activation(p_hi[0:m, at % 4, :], prod[0:m, at % 2, :], ACT.Copy).then_inc(high_ready, 1)

            def expert(n, buf):
                for at in range(PER):
                    q, i, m = n * PER + at, at % TILES, k_of(at % TILES)
                    act.wait_ge(g_ready, q + 1)
                    nc.scalar.activation(gate[0:m, at % 2, :], ps[0:m, G + i % 2, :], ACT.Silu).then_inc(silu_done, 1)
                    if at:
                        high(n, at - 1)
                    elif not isinstance(n, int):
                        high(n - 1, PER - 1)
                    if isinstance(n, int):
                        act.wait_ge(cw_ready, at + 1)
                        nc.scalar.activation(cw[:, 1 + i, cols(at // TILES)], ps[:, W, :], ACT.Copy).then_inc(cw_copied, 1)

            all_orders(act, expert)
            high(ORDERS - 1, PER - 1)

        @block.vector
        def _(dve):
            def low(n, at):
                q, m = n * PER + at, k_of(at % TILES)
                dve.wait_ge(high_ready, q + 1)
                nc.vector.tensor_tensor(p_lo[0:m, at % 4, :], prod[0:m, at % 2, :],
                                        p_hi[0:m, at % 4, :].bitcast(F32), ALU.subtract).then_inc(low_ready, 1)

            def scale(n, c):
                g = n * NCH + c
                dve.wait_ge(tile_summed, n * PER + (c + 1) * TILES)
                if not (isinstance(n, int) and n == 0 and c < 2):
                    dve.wait_ge(x_added, g - 1)
                nc.vector.tensor_tensor(ysc[:, c % 2, :], ps[:, Y + c % 2, :], cw[:, n, cols(c)], ALU.mult)\
                    .then_inc(scaled, 1)

            def expert(n, buf):
                for at in range(PER):
                    q, i, m = n * PER + at, at % TILES, k_of(at % TILES)
                    c = at // TILES
                    dve.wait_ge(silu_done, q + 1)
                    if i < NI:
                        dve.wait_ge(gu_ready, n * (NCH * NI) + (c * NI + i + 1))
                        up = ps[:, U + i % 2, :]
                    else:
                        up = ps[UT:UT + TAIL, G + i % 2, :]
                    if not isinstance(n, int) or at >= 2:
                        dve.wait_ge(low_ready, q - 1)
                    nc.vector.tensor_tensor(prod[0:m, at % 2, :], gate[0:m, at % 2, :], up, ALU.mult)\
                        .then_inc(prod_done, 1)
                    if at:
                        low(n, at - 1)
                    elif not isinstance(n, int):
                        low(n - 1, PER - 1)
                    if i == 3 and c:
                        scale(n, c - 1)
                    elif i == 3 and not isinstance(n, int):
                        scale(n - 1, NCH - 1)

            dve.wait_ge(ones_set, 1)
            all_orders(dve, expert)
            low(ORDERS - 1, PER - 1)
            scale(ORDERS - 1, NCH - 1)


def mixer_b_stage(k, d):
    nc, ps, big = k.nc, k.ps, k.big
    stage = ExitStack()
    sb = lambda name, shape, dt=F32, ctx=None: k.sb("b_" + name, shape, dt, ctx=ctx or stage)
    sem = lambda name: k.sem("b_" + name)
    HEADS, HD = 4, 64
    TT = T // P
    CONV = 4
    MT = 3
    xs, bT, cT, sz, y = big[:, 1:3, :], big[:, 3, :], big[:, 4, :], big[:, 5:7, :], big[:, 7:9, :]
    head_rows = sb("head_rows", [P, 2, HEADS])
    dt = sb("dt", [P, TT, HEADS])
    dt_log = sb("dt_log", [P, TT, HEADS])
    dta = sb("dta", [P, TT, HEADS])
    neg_a = sb("neg_a", [P, HEADS])
    w_out = sb("w_out", [P, FT, P])
    pre = ExitStack()
    xp = sb("xp", [P, BATCH, PADDED], ctx=pre)
    w_in = sb("w_in", [P, 2 * DI + 2 * P + HEADS], ctx=pre)
    w_tap = sb("w_tap", [P, TAPS, CONV * P], ctx=pre)
    taps = sb("taps", [P, TAPS, CONV * P], ctx=pre)
    loaded, pad_zero, taps_ready, xz_ready, silu_done, dt_ready, dt_step, a_ready, dta_ready = [sem(n) for n in (
        "loaded pad_zero taps_ready xz_ready silu_done dt_ready dt_step a_ready dta_ready").split()]

    with nc.Block() as block:

        @block.sync
        def _(sp):
            sp.dma_start(taps[:, :, :].rearrange("p a b -> p (a b)"), d["tapsB"].partition_broadcast(P))\
                .then_inc(loaded, 16)
            sp.dma_start(w_in[:, :], d["w_inB"]).then_inc(loaded, 16)
            sp.dma_start(w_out[:, :, :], d["w_outB"]).then_inc(loaded, 16)
            sp.dma_start(head_rows[:, :, :].rearrange("p a b -> p (a b)"), d["headsB"].partition_broadcast(P))\
                .then_inc(loaded, 16)

        @block.gpsimd
        def _(pool):
            nc.gpsimd.memset(xp[:, :, 0:PADC], 0.0).then_inc(pad_zero, 1)

    norm_stage(k, "nb", k.x, k.xn, True, k.eps5, weight=k.vec[:, VB_NORM:VB_NORM + 1], rms_eps=k.eps6, out=xp)

    JT = CONV + FT
    with pre, nc.Block() as block:

        @block.tensor
        def _(pe):
            pe.wait_ge(loaded, 16 * 4)
            pe.wait_ge(pad_zero, 1)
            for t in range(TT):
                b, t0 = divmod(t * P, SEQ)
                last = nc.tensor.matmul(ps[:, 4, t * HEADS:(t + 1) * HEADS], xp[:, b, PADC + t0:PADC + t0 + P],
                                        w_in[:, 2 * DI + 2 * P:], start=True, stop=True)
            last.then_inc(dt_ready, 1)
            pe.wait_ge(taps_ready, TAPS)
            for c in range(NCH):
                b, t0 = divmod(c * CH, SEQ)
                for j in range(JT):
                    n = c * JT + j
                    if n >= 4:
                        pe.wait_ge(silu_done, n - 3)
                    if j < CONV:
                        for tap in range(TAPS):
                            off = PADC + t0 - (TAPS - 1) + tap
                            last = nc.tensor.matmul(ps[:, n % 4, :], w_tap[:, tap, j * P:(j + 1) * P],
                                                    xp[:, b, off:off + CH], start=(tap == 0), stop=(tap == TAPS - 1))
                    else:
                        last = nc.tensor.matmul(ps[:, n % 4, :], w_in[:, (j - CONV) * P:(j - CONV + 1) * P],
                                                xp[:, b, PADC + t0:PADC + t0 + CH], start=True, stop=True)
                    last.then_inc(xz_ready, 1)

        @block.scalar
        def _(act):
            act.wait_ge(dt_step, 1)
            nc.scalar.activation(dt_log[:, :, :], dt[:, :, :], ACT.Abs).then_inc(dt_step, 1)
            act.wait_ge(dt_step, 2)
            nc.scalar.activation(dt_log[:, :, :], dt_log[:, :, :], ACT.Exp, scale=-1.0).then_inc(dt_step, 1)
            nc.scalar.activation(neg_a[:, :], head_rows[:, 1, :], ACT.Exp).then_inc(a_ready, 1)
            act.wait_ge(dt_step, 3)
            nc.scalar.activation(dt_log[:, :, :], dt_log[:, :, :], ACT.Ln, bias=1.0).then_inc(dt_step, 1)
            for c in range(NCH):
                for j in range(JT):
                    n = c * JT + j
                    act.wait_ge(xz_ready, n + 1)
                    if j < CONV:
                        nc.scalar.activation(big[:, 1 + j, cols(c)], ps[:, n % 4, :], ACT.Silu,
                                             bias=k.vec[:, VB_CB + j:VB_CB + j + 1]).then_inc(silu_done, 1)
                    else:
                        nc.scalar.activation(sz[:, j - CONV, cols(c)], ps[:, n % 4, :], ACT.Silu).then_inc(silu_done, 1)

        @block.vector
        def _(dve):
            dve.wait_ge(loaded, 16 * 4)
            for tap in range(TAPS):
                nc.vector.tensor_tensor(w_tap[:, tap, :], w_in[:, DI:DI + CONV * P], taps[:, tap, :], ALU.mult)\
                    .then_inc(taps_ready, 1)
            dve.wait_ge(dt_ready, 1)
            nc.vector.tensor_tensor(dt[:, :, :], ps[:, 4, 0:TT * HEADS].rearrange("p (t h) -> p t h", h=HEADS),
                                    head_rows[:, 0, :].unsqueeze(1).to_broadcast([P, TT, HEADS]), ALU.add)\
                .then_inc(dt_step, 1)
            dve.wait_ge(dt_step, 4)
            nc.vector.scalar_tensor_tensor(out=dt[:, :, :], in0=dt[:, :, :], scalar=0.0, in1=dt_log[:, :, :],
                                           op0=ALU.max, op1=ALU.add).then_inc(dt_step, 1)
            dve.wait_ge(a_ready, 1)
            nc.vector.tensor_scalar(neg_a[:, :], neg_a[:, :], -1.0, None, ALU.mult).then_inc(a_ready, 1)
            dve.wait_ge(dt_step, 5)
            dve.wait_ge(a_ready, 2)
            nc.vector.tensor_tensor(dta[:, :, :], dt[:, :, :],
                                    neg_a[:, :].unsqueeze(1).to_broadcast([P, TT, HEADS]), ALU.mult)\
                .then_inc(dta_ready, 1)

    ssd = ExitStack()
    one = sb("one", [P, P], ctx=ssd)
    masks = sb("masks", [P, 2, P], ctx=ssd)
    steps = sb("steps", [P, 2, HEADS, P], ctx=ssd)
    decay = sb("decay", [P, 2, HEADS, P], ctx=ssd)
    into = sb("into", [P, 2, HEADS, P], ctx=ssd)
    toks = sb("toks", [P, 2, 3 * P], ctx=ssd)
    gram = sb("gram", [P, 2, P], ctx=ssd)
    mix = sb("mix", [P, 2, HEADS, P], ctx=ssd)
    c_in = sb("c_in", [P, 2, HEADS, P], ctx=ssd)
    x_dt = sb("x_dt", [P, 2, HEADS, HD], ctx=ssd)
    x_end = sb("x_end", [P, 2, HEADS, HD], ctx=ssd)
    state = sb("state", [P, 2, HEADS, HD], ctx=ssd)
    kept = sb("kept", [P, HEADS, HD], ctx=ssd)
    D, E, F, TR, Y, S = 0, 1, 2, 3, 4, 6
    PER_SEQ = SEQ // P
    masks_loaded, one_set, steps_ready, d_ready, e_ready, f_ready, tr_ready, decay_ready, into_ready, toks_ready, \
        gram_ready, mix_ready, c_in_ready, x_dt_ready, x_end_ready, y_summed, ds_ready, kept_ready, state_ready, \
        yd_ready, yz_ready = [sem(n) for n in (
            "masks_loaded one_set steps_ready d_ready e_ready f_ready tr_ready decay_ready into_ready toks_ready "
            "gram_ready mix_ready c_in_ready x_dt_ready x_end_ready y_summed ds_ready kept_ready state_ready "
            "yd_ready yz_ready").split()]

    with ssd, nc.Block() as block:

        @block.sync
        def _(sp):
            sp.dma_start(masks[:, :, :], d["masks"]).then_inc(masks_loaded, 16)

        @block.tensor
        def _(pe):
            def chunk_inputs(c):
                ts = slice(c * P, (c + 1) * P)
                pe.wait_ge(steps_ready, c + 1)
                if c >= 1:
                    pe.wait_ge(decay_ready, c)
                    pe.wait_ge(into_ready, c)
                    pe.wait_ge(gram_ready, c)
                    pe.wait_ge(toks_ready, c)
                nc.tensor.matmul(ps[:, F, 0:P], bT[:, ts], cT[:, ts], start=True, stop=True).then_inc(f_ready, 1)
                nc.tensor.matmul(ps[:, D, :], masks[:, 1, :], steps[:, c % 2, :, :].rearrange("p h i -> p (h i)"),
                                 start=True, stop=True).then_inc(d_ready, 1)
                nc.tensor.transpose(ps[:, TR, 0:P], xs[:, 0, ts], k.eye[:, :])
                nc.tensor.transpose(ps[:, TR, P:2 * P], xs[:, 1, ts], k.eye[:, :])
                nc.tensor.transpose(ps[:, TR, 2 * P:3 * P], bT[:, ts], k.eye[:, :]).then_inc(tr_ready, 1)
                nc.tensor.matmul(ps[:, E, :], one[:, :], steps[:, c % 2, :, :].rearrange("p h i -> p (h i)"),
                                 start=True, stop=True).then_inc(e_ready, 1)

            def chunk_outputs(c):
                if c % 4 == 0 and c:
                    pe.wait_ge(yd_ready, c // 4 * FT)
                pe.wait_ge(x_dt_ready, c + 1)
                pe.wait_ge(mix_ready, c + 1)
                pe.wait_ge(c_in_ready, c + 1)
                pe.wait_ge(state_ready, c + 1)
                for h in range(HEADS):
                    out = ps[HD * (h % 2):HD * (h % 2) + HD, Y + h // 2, (c % 4) * P:(c % 4 + 1) * P]
                    nc.tensor.matmul(out, x_dt[:, c % 2, h, :], mix[:, c % 2, h, :], start=True, stop=False)
                    last = nc.tensor.matmul(out, state[:, c % 2, h, :], c_in[:, c % 2, h, :], start=False, stop=True)
                last.then_inc(y_summed, 1)
                pe.wait_ge(x_end_ready, c + 1)
                nc.tensor.matmul(ps[:, S, 0:HEADS * HD], toks[:, c % 2, 2 * P:3 * P],
                                 x_end[:, c % 2, :, :].rearrange("p h q -> p (h q)"), start=True, stop=True)\
                    .then_inc(ds_ready, 1)

            pe.wait_ge(one_set, 1)
            pe.wait_ge(masks_loaded, 16)
            chunk_inputs(0)
            for c in range(TT):
                if c + 1 < TT:
                    chunk_inputs(c + 1)
                chunk_outputs(c)

        @block.scalar
        def _(act):
            for c in range(TT):
                if c >= 2:
                    act.wait_ge(ds_ready, c - 1)
                    act.wait_ge(kept_ready, c - 1)
                act.wait_ge(d_ready, c + 1)
                nc.scalar.activation(decay[:, c % 2, :, :].rearrange("p h i -> p (h i)"), ps[:, D, :], ACT.Exp)\
                    .then_inc(decay_ready, 1)
                act.wait_ge(tr_ready, c + 1)
                nc.scalar.activation(toks[:, c % 2, :], ps[:, TR, 0:3 * P], ACT.Copy).then_inc(toks_ready, 1)
                act.wait_ge(e_ready, c + 1)
                nc.scalar.activation(into[:, c % 2, :, :].rearrange("p h i -> p (h i)"), ps[:, E, :], ACT.Exp)\
                    .then_inc(into_ready, 1)

        @block.gpsimd
        def _(pool):
            def make_steps(c):
                if c >= 2:
                    pool.wait_ge(e_ready, c - 1)
                nc.gpsimd.tensor_tensor(steps[:, c % 2, :, :], masks[:, 0, :].unsqueeze(1).to_broadcast([P, HEADS, P]),
                                        dta[:, c, :].unsqueeze(2).to_broadcast([P, HEADS, P]), ALU.mult)\
                    .then_inc(steps_ready, 1)

            nc.gpsimd.memset(one[:, :], 1.0).then_inc(one_set, 1)
            pool.wait_ge(masks_loaded, 16)
            make_steps(0)
            for c in range(TT):
                if c + 1 < TT:
                    make_steps(c + 1)
                if c >= 2:
                    pool.wait_ge(ds_ready, c - 1)
                pool.wait_ge(toks_ready, c + 1)
                nc.gpsimd.tensor_tensor(x_dt[:, c % 2, :, :],
                                        toks[:, c % 2, 0:2 * P].rearrange("p (h q) -> p h q", h=HEADS),
                                        dt[:, c, :].unsqueeze(2).to_broadcast([P, HEADS, HD]), ALU.mult)\
                    .then_inc(x_dt_ready, 1)
                pool.wait_ge(x_dt_ready, c + 1)
                pool.wait_ge(decay_ready, c + 1)
                nc.gpsimd.tensor_tensor(x_end[:, c % 2, :, :], x_dt[:, c % 2, :, :],
                                        decay[:, c % 2, :, P - 1:P].to_broadcast([P, HEADS, HD]), ALU.mult)\
                    .then_inc(x_end_ready, 1)

        @block.vector
        def _(dve):
            nc.vector.memset(state[:, 0, :, :], 0.0).then_inc(state_ready, 1)
            dve.wait_ge(masks_loaded, 16)
            for c in range(TT):
                ts = slice(c * P, (c + 1) * P)
                dve.wait_ge(f_ready, c + 1)
                if c >= 2:
                    dve.wait_ge(y_summed, c - 1)
                    dve.wait_ge(mix_ready, c - 1)
                nc.vector.tensor_tensor(gram[:, c % 2, :], ps[:, F, 0:P], masks[:, 0, :], ALU.mult)\
                    .then_inc(gram_ready, 1)
                dve.wait_ge(decay_ready, c + 1)
                dve.wait_ge(gram_ready, c + 1)
                nc.vector.tensor_tensor(mix[:, c % 2, :, :], decay[:, c % 2, :, :],
                                        gram[:, c % 2, :].unsqueeze(1).to_broadcast([P, HEADS, P]), ALU.mult)\
                    .then_inc(mix_ready, 1)
                dve.wait_ge(into_ready, c + 1)
                nc.vector.tensor_tensor(c_in[:, c % 2, :, :], into[:, c % 2, :, :],
                                        cT[:, ts].unsqueeze(1).to_broadcast([P, HEADS, P]), ALU.mult)\
                    .then_inc(c_in_ready, 1)
                if c + 1 < TT:
                    if c >= 1:
                        dve.wait_ge(y_summed, c)
                    if (c + 1) % PER_SEQ == 0:
                        nc.vector.memset(kept[:, :, :], 0.0).then_inc(kept_ready, 1)
                        dve.wait_ge(kept_ready, c + 1)
                        nc.vector.memset(state[:, (c + 1) % 2, :, :], 0.0).then_inc(state_ready, 1)
                    else:
                        dve.wait_ge(state_ready, c + 1)
                        nc.vector.tensor_tensor(kept[:, :, :], state[:, c % 2, :, :],
                                                into[:, c % 2, :, P - 1:P].to_broadcast([P, HEADS, HD]), ALU.mult)\
                            .then_inc(kept_ready, 1)
                        dve.wait_ge(kept_ready, c + 1)
                        dve.wait_ge(ds_ready, c + 1)
                        nc.vector.tensor_tensor(state[:, (c + 1) % 2, :, :], kept[:, :, :],
                                                ps[:, S, 0:HEADS * HD].rearrange("p (h q) -> p h q", h=HEADS), ALU.add)\
                            .then_inc(state_ready, 1)
                if c % 4 == 3:
                    g = c // 4
                    dve.wait_ge(y_summed, c + 1)
                    for f in range(FT):
                        nc.vector.scalar_tensor_tensor(out=y[:, f, cols(g)], in0=xs[:, f, cols(g)],
                                                       scalar=k.vec[:, VB_D + f:VB_D + f + 1], in1=ps[:, Y + f, :],
                                                       op0=ALU.mult, op1=ALU.add).then_inc(yd_ready, 1)
                    for f in range(FT):
                        dve.wait_ge(yd_ready, g * FT + f + 1)
                        nc.vector.tensor_tensor(y[:, f, cols(g)], y[:, f, cols(g)], sz[:, f, cols(g)], ALU.mult)\
                            .then_inc(yz_ready, 1)

    post = ExitStack()
    sq = sb("sq", [P, FT, T], ctx=post)
    rs = sb("rs", [P, T], ctx=post)
    squared, ms_ready, log_done, rms_ready, scaled, out_ready, res_done = [sem(n) for n in (
        "squared ms_ready log_done rms_ready scaled out_ready res_done").split()]

    with post, nc.Block() as block:

        @block.tensor
        def _(pe):
            for c in range(NCH):
                for f in range(FT):
                    pe.wait_ge(squared, c * FT + f + 1)
                    last = nc.tensor.matmul(ps[:, c, :], k.ones[:, :], sq[:, f, cols(c)],
                                            start=(f == 0), stop=(f == FT - 1))
                last.then_inc(ms_ready, 1)
            for c in range(NCH):
                for f in range(FT):
                    pe.wait_ge(scaled, c * FT + f + 1)
                    last = nc.tensor.matmul(ps[:, 4 + c, :], w_out[:, f, :], y[:, f, cols(c)],
                                            start=(f == 0), stop=(f == FT - 1))
                last.then_inc(out_ready, 1)

        @block.scalar
        def _(act):
            for c in range(NCH):
                for f in range(FT):
                    nc.scalar.activation(sq[:, f, cols(c)], y[:, f, cols(c)], ACT.Square).then_inc(squared, 1)
            for c in range(NCH):
                act.wait_ge(ms_ready, c + 1)
                nc.scalar.activation(rs[:, cols(c)], ps[:, c, :], ACT.Ln, bias=k.eps6[:, 0:1], scale=P / DI)\
                    .then_inc(log_done, 1)
                act.wait_ge(log_done, c + 1)
                nc.scalar.activation(rs[:, cols(c)], rs[:, cols(c)], ACT.Exp, scale=-0.5).then_inc(rms_ready, 1)

        @block.vector
        def _(dve):
            for c in range(NCH):
                dve.wait_ge(rms_ready, c + 1)
                for f in range(FT):
                    nc.vector.scalar_tensor_tensor(out=y[:, f, cols(c)], in0=y[:, f, cols(c)],
                                                   scalar=k.vec[:, VB_SSM + f:VB_SSM + f + 1], in1=rs[:, cols(c)],
                                                   op0=ALU.mult, op1=ALU.mult).then_inc(scaled, 1)
            for c in range(NCH):
                dve.wait_ge(out_ready, c + 1)
                nc.vector.tensor_tensor(k.xn[:, cols(c)], k.xn[:, cols(c)], ps[:, 4 + c, :], ALU.add)\
                    .then_inc(res_done, 1)

    mlp_in = big[:, 1, :]
    norm_stage(k, "nm", None, k.xn, False, None, weight=k.vec[:, VB_POST:VB_POST + 1], rms_eps=k.eps6,
               out=mlp_in, split=True)
    mlp = ExitStack()
    WC = 3 * MT * P
    raw = sb("raw", [P, WC], ctx=mlp)
    w_hi, w_lo = sb("w_hi", [P, WC], F32R, ctx=mlp), sb("w_lo", [P, WC], F32R, ctx=mlp)
    gate, prod = sb("gate", [P, 2, CH], ctx=mlp), sb("prod", [P, 2, CH], ctx=mlp)
    p_hi, p_lo = sb("p_hi", [P, 4, CH], F32R, ctx=mlp), sb("p_lo", [P, 4, CH], F32R, ctx=mlp)
    total = sb("total", [P, 2, CH], ctx=mlp)
    G, U, O = 0, 2, 4
    raw_loaded, w_high, w_ready, g_ready, u_ready, gate_done, prod_done, high_ready, low_ready, tile_summed, \
        total_ready, x_added = [sem("mlp_" + n) for n in (
            "raw_loaded w_high w_ready g_ready u_ready gate_done prod_done high_ready low_ready tile_summed "
            "total_ready x_added").split()]

    with stage, mlp, nc.Block() as block:

        @block.sync
        def _(sp):
            sp.dma_start(raw[:, 0:2 * MT * P], d["w_guB"]).then_inc(raw_loaded, 16)
            sp.dma_start(raw[:, 2 * MT * P:], d["w_dnB"]).then_inc(raw_loaded, 16)

        @block.gpsimd
        def _(pool):
            pool.wait_ge(raw_loaded, 32)
            nc.gpsimd.tensor_copy(w_hi[:, :], raw[:, :]).then_inc(w_high, 1)
            pool.wait_ge(w_high, 1)
            nc.gpsimd.tensor_tensor(w_lo[:, :], raw[:, :], w_hi[:, :].bitcast(F32), ALU.subtract).then_inc(w_ready, 1)

        @block.tensor
        def _(pe):
            def product(out, a, v_hi, v_lo, start, stop):
                nc.tensor.matmul(out, w_hi[:, a:a + P], v_hi, start=start, stop=False)
                nc.tensor.matmul(out, w_hi[:, a:a + P], v_lo, start=False, stop=False)
                return nc.tensor.matmul(out, w_lo[:, a:a + P], v_hi, start=False, stop=stop)

            def down(q):
                c, i = divmod(q, MT)
                if i == 0 and c >= 2:
                    pe.wait_ge(total_ready, c - 1)
                pe.wait_ge(low_ready, q + 1)
                product(ps[:, O + c % 2, :], (2 * MT + i) * P, p_hi[:, q % 4, :], p_lo[:, q % 4, :],
                        i == 0, i == MT - 1).then_inc(tile_summed, 1)

            pe.wait_ge(w_ready, 1)
            for q in range(NCH * MT):
                c, i = divmod(q, MT)
                if q >= 2:
                    pe.wait_ge(prod_done, q - 1)
                xh, xl = k.x_hi[:, cols(c)], k.x_lo[:, cols(c)]
                product(ps[:, G + q % 2, :], i * P, xh, xl, True, True).then_inc(g_ready, 1)
                product(ps[:, U + q % 2, :], (MT + i) * P, xh, xl, True, True).then_inc(u_ready, 1)
                if q >= 2:
                    down(q - 2)
            down(NCH * MT - 2)
            down(NCH * MT - 1)

        @block.scalar
        def _(act):
            def high(q):
                act.wait_ge(prod_done, q + 1)
                if q >= 4:
                    act.wait_ge(tile_summed, q - 3)
                nc.scalar.activation(p_hi[:, q % 4, :], prod[:, q % 2, :], ACT.Copy).then_inc(high_ready, 1)

            for q in range(NCH * MT):
                act.wait_ge(g_ready, q + 1)
                nc.scalar.activation(gate[:, q % 2, :], ps[:, G + q % 2, :], ACT.Silu).then_inc(gate_done, 1)
                if q:
                    high(q - 1)
            high(NCH * MT - 1)

        @block.vector
        def _(dve):
            def low(q):
                dve.wait_ge(high_ready, q + 1)
                nc.vector.tensor_tensor(p_lo[:, q % 4, :], prod[:, q % 2, :], p_hi[:, q % 4, :].bitcast(F32),
                                        ALU.subtract).then_inc(low_ready, 1)

            def finish(c):
                dve.wait_ge(tile_summed, (c + 1) * MT)
                if c >= 2:
                    dve.wait_ge(x_added, c - 1)
                nc.vector.tensor_tensor(total[:, c % 2, :], ps[:, O + c % 2, :], k.xn[:, cols(c)], ALU.add)\
                    .then_inc(total_ready, 1)
                dve.wait_ge(total_ready, c + 1)
                nc.vector.tensor_tensor(k.x[:, cols(c)], k.x[:, cols(c)], total[:, c % 2, :], ALU.add)\
                    .then_inc(x_added, 1)

            for q in range(NCH * MT):
                dve.wait_ge(gate_done, q + 1)
                dve.wait_ge(u_ready, q + 1)
                if q >= 2:
                    dve.wait_ge(low_ready, q - 1)
                nc.vector.tensor_tensor(prod[:, q % 2, :], gate[:, q % 2, :], ps[:, U + q % 2, :], ALU.mult)\
                    .then_inc(prod_done, 1)
                if q:
                    low(q - 1)
                if q % MT == 2 and q > MT:
                    finish(q // MT - 1)
            low(NCH * MT - 1)
            finish(NCH - 1)


def store_stage(k, out):
    nc = k.nc
    stored = k.sem("stored")
    with nc.Block() as block:

        @block.sync
        def _(sp):
            sp.dma_start(out, k.x[:, :]).then_inc(stored, 16)
            sp.wait_ge(stored, 16)


def build(nc, d, out, stages=4):
    ctx = ExitStack()
    with ctx:
        k = Core(nc, ctx)
        load_stage(k, d)
        mixer_a_stage(k, d)
        if stages > 1:
            ffn_stage(k, d, "f")
        if stages > 2:
            mixer_b_stage(k, d)
        if stages > 3:
            ffn_stage(k, d, "g")
        store_stage(k, out)


def layout(i):
    a = lambda n: np.asarray(i[n])
    col = lambda v: a(v).reshape(-1, P).T
    vec = [col("L0_attn_a_norm_w"), col("L0_attn_a_conv_b"), col("L0_attn_a_dt_proj_b"), col("L0_attn_a_D"),
           a("L0_attn_a_A_log").reshape(FT, P, NST).transpose(1, 0, 2).reshape(P, FT * NST),
           col("L0_attn_b_norm_w"), col("L0_attn_b_post_norm_w"), col("L0_attn_b_ssm_norm_w"),
           col("L0_attn_b_conv_b"), np.repeat(a("L0_attn_b_D"), 64).reshape(FT, P).T]
    xw = a("L0_attn_a_x_proj_w")
    order = np.concatenate([xw[RANK:], xw[:RANK]])
    m = {
        "xT": a("L0_attn_a_x").reshape(T, P).T,
        "vec": np.concatenate(vec, axis=1),
        "eye": np.eye(P, dtype=np.float32),
        "tapsA": a("L0_attn_a_conv_w")[:, 0, :].T.reshape(TAPS * DI),
        "w_inA": a("L0_attn_a_in_proj_w").T,
        "w_xA": order.T.reshape(FT, P, 40).transpose(1, 0, 2),
        "w_dtA": a("L0_attn_a_dt_proj_w").T,
        "w_outA": a("L0_attn_a_out_proj_w").T.reshape(FT, P, P).transpose(1, 0, 2),
    }
    w = a("L0_attn_b_in_proj_w")
    m["w_inB"] = w.T
    m["tapsB"] = a("L0_attn_b_conv_w").T.reshape(TAPS * 4 * P)
    m["headsB"] = np.concatenate([a("L0_attn_b_dt_bias"), a("L0_attn_b_A_log")])
    m["w_outB"] = a("L0_attn_b_out_proj_w").T.reshape(FT, P, P).transpose(1, 0, 2)
    m["masks"] = np.stack([np.triu(np.ones((P, P), np.float32)), np.tril(np.ones((P, P), np.float32), -1)], axis=1)
    m["w_guB"] = np.concatenate([a("L0_attn_b_gate_w"), a("L0_attn_b_up_w")]).T
    m["w_dnB"] = a("L0_attn_b_down_w").T.reshape(3, P, P).transpose(1, 0, 2).reshape(P, 3 * P)
    gu = np.concatenate([a("L0_ffn_shared_gate_up")[None], a("L0_ffn_experts_gate_up")])
    full = NI * P
    gu = np.concatenate([gu[:, :full], gu[:, INTER:INTER + full], gu[:, full:INTER], gu[:, INTER + full:]], axis=1)
    m["gu"] = gu.transpose(0, 2, 1)
    m["dn"] = np.concatenate([a("L0_ffn_shared_down")[None], a("L0_ffn_experts_down")]).transpose(0, 2, 1)
    m["w_gateF"] = a("L0_ffn_gate_weight").T
    m["order"] = np.arange(EXPERTS, 0, -1, dtype=np.float32)
    return {n: np.ascontiguousarray(v) for n, v in m.items()}


def kernel(**inputs):
    import concourse.bacc as bacc
    from concourse.bass_utils import run_bass_kernel_spmd

    nc = bacc.Bacc("TRN2", target_bir_lowering=False, num_devices=1)
    arrays = layout(inputs)
    d = {n: nc.dram_tensor("in_" + n, v.shape, mybir.dt.from_np(v.dtype), kind="ExternalInput").ap()
         for n, v in arrays.items()}
    out = nc.dram_tensor("out", (P, T), F32, kind="ExternalOutput").ap()
    build(nc, d, out)
    r = run_bass_kernel_spmd(nc, [{"in_" + n: v for n, v in arrays.items()}], core_ids=[0])
    return r.results[0]["out"].T.reshape(BATCH, SEQ, P)
```

```python
from contextlib import ExitStack

import numpy as np

import concourse.bass as bass
from concourse import mybir

F32 = mybir.dt.float32
F32R = mybir.dt.float32r
I32 = mybir.dt.int32
ALU = mybir.AluOpType
ACT = mybir.ActivationFunctionType
AX = mybir.AxisListType

P = 128
BATCH, SEQ = 2, 1024
T = BATCH * SEQ
CH = 512
NCH = T // CH
DI = 256
FT = DI // P
TAPS = 4
NST = 16
RANK = 8
PADC = 4
PADDED = SEQ + PADC
EXPERTS = 8
INTER = 938
NI = 7
TAIL = INTER - NI * P
UT = 64
GU = 2 * NI * P + UT + TAIL
TOP = 2
TT = T // P
TILES = NI + 1
RING = 4
SLOT_TILES = (TOP * T + EXPERTS * (P - 1)) // P
ROW = P + 2
HALVES = (INTER // 2 + 1, INTER // 2 - 1)
NFC = EXPERTS + TT + SLOT_TILES + EXPERTS - 1

VA_NORM, VA_CB, VA_DTB, VA_D, VA_ALOG = 0, 1, 3, 5, 7
VB_NORM, VB_POST, VB_SSM, VB_CB, VB_D = 39, 40, 41, 43, 47
VA_TAPS, VB_TAPS = 49, 57
NV = 73


class Core:

    def __init__(self, nc, ctx):
        self.nc, self.ctx = nc, ctx

    def sb(self, name, shape, dt=F32, ctx=None):
        return (ctx or self.ctx).enter_context(self.nc.sbuf_tensor(name, shape, dt))

    def sem(self, name, ctx=None):
        return (ctx or self.ctx).enter_context(self.nc.semaphore(name))


def cols(c):
    return slice(c * CH, (c + 1) * CH)


def load_stage(k, d):
    nc = k.nc
    k.x = k.sb("x", [P, T])
    k.xn = k.sb("xn", [P, T])
    k.vec = k.sb("vec", [P, NV])
    k.ones = k.sb("ones", [P, P])
    k.eye = k.sb("eye", [P, P])
    k.eps5 = k.sb("eps5", [P, 1])
    k.eps6 = k.sb("eps6", [P, 1])
    k.ps = k.ctx.enter_context(nc.psum_tensor("ps", [P, 8, CH], F32))
    k.x_loaded = k.sem("x_loaded")
    k.vec_loaded = k.sem("vec_loaded")
    k.eye_loaded = k.sem("eye_loaded")
    k.fc = k.sb("fc", [P, NFC])
    k.places = k.sb("places", [P, TOP * TT], I32)
    k.slot_rows = [nc.dram_tensor(f"slot_rows{i}", (SLOT_TILES * P, ROW), F32, kind="Internal").ap() for i in range(2)]
    k.token_rows = nc.dram_tensor("token_rows", ((TOP * T + SLOT_TILES * P), P), F32, kind="Internal").ap()
    k.slots_filled = k.sem("slots_filled")
    k.rows_sent, k.outputs_sent = k.sem("rows_sent"), k.sem("outputs_sent")
    k.late_loaded = [k.sem("late_loaded0"), k.sem("late_loaded1")]
    consts_set = k.sem("consts_set")
    with nc.Block() as block:

        @block.sync
        def _(sp):
            for c in range(NCH):
                sp.dma_start(k.x[:, cols(c)], d["xT"][:, cols(c)]).then_inc(k.x_loaded, 16)
            sp.dma_start(k.vec[:, :], d["vec"]).then_inc(k.vec_loaded, 16)
            sp.dma_start(k.eye[:, :], d["eye"]).then_inc(k.eye_loaded, 16)
            sp.dma_start(k.fc[:, :], d["fc"].partition_broadcast(P)).then_inc(k.eye_loaded, 16)
            sp.dma_start(k.places[:, :], d["places"]).then_inc(k.eye_loaded, 16)

        @block.vector
        def _(dve):
            nc.vector.memset(k.ones[:, :], 1.0 / P)
            nc.vector.memset(k.eps5[:, :], 1e-5)
            nc.vector.memset(k.eps6[:, :], 1e-6).then_inc(consts_set, 1)


def norm_stage(k, tag, src, dst, center, eps, weight=None, rms_eps=None, out=None, split=None,
               sync_part=None, pool_part=None):
    nc = k.nc
    stage = ExitStack()
    sq = k.sb(tag + "_sq", [P, T], ctx=stage)
    rs = k.sb(tag + "_rs", [P, T], ctx=stage)
    mean_ready, centred, squared, var_ready, rstd_ready, normed, squared2, ms_ready, rms_ready, scaled, \
        high_ready, low_ready, log_done = [k.sem(f"{tag}_{n}", stage) for n in (
            "mean_ready centred squared var_ready rstd_ready normed squared2 ms_ready rms_ready scaled "
            "high_ready low_ready log_done").split()]
    final = out if out is not None else dst

    with stage, nc.Block() as block:
        if sync_part is not None:
            @block.sync
            def _(sp):
                sync_part(sp)

            @block.gpsimd
            def _(pool):
                pool_part(pool)

        @block.tensor
        def _(pe):
            if center:
                pe.wait_ge(k.x_loaded, 16 * NCH)
                for c in range(NCH):
                    nc.tensor.matmul(k.ps[:, c, :], k.ones[:, :], src[:, cols(c)], start=True, stop=True)\
                        .then_inc(mean_ready, 1)
                for c in range(NCH):
                    pe.wait_ge(squared, c + 1)
                    nc.tensor.matmul(k.ps[:, 4 + c, :], k.ones[:, :], sq[:, cols(c)], start=True, stop=True)\
                        .then_inc(var_ready, 1)
            if rms_eps is not None:
                for c in range(NCH):
                    pe.wait_ge(squared2, c + 1)
                    nc.tensor.matmul(k.ps[:, c, :], k.ones[:, :], sq[:, cols(c)], start=True, stop=True)\
                        .then_inc(ms_ready, 1)

        @block.scalar
        def _(act):
            if center:
                for c in range(NCH):
                    act.wait_ge(centred, c + 1)
                    nc.scalar.activation(sq[:, cols(c)], dst[:, cols(c)], ACT.Square).then_inc(squared, 1)
                for c in range(NCH):
                    act.wait_ge(var_ready, c + 1)
                    nc.scalar.activation(rs[:, cols(c)], k.ps[:, 4 + c, :], ACT.Ln, bias=eps[:, 0:1])\
                        .then_inc(log_done, 1)
                for c in range(NCH):
                    act.wait_ge(log_done, NCH)
                    nc.scalar.activation(rs[:, cols(c)], rs[:, cols(c)], ACT.Exp, scale=-0.5)\
                        .then_inc(rstd_ready, 1)
            if rms_eps is not None:
                for c in range(NCH):
                    if center:
                        act.wait_ge(normed, c + 1)
                    nc.scalar.activation(sq[:, cols(c)], dst[:, cols(c)], ACT.Square).then_inc(squared2, 1)
                for c in range(NCH):
                    act.wait_ge(ms_ready, c + 1)
                    nc.scalar.activation(rs[:, cols(c)], k.ps[:, c, :], ACT.Ln, bias=rms_eps[:, 0:1])\
                        .then_inc(log_done, 1)
                for c in range(NCH):
                    act.wait_ge(log_done, NCH * (2 if center else 1))
                    nc.scalar.activation(rs[:, cols(c)], rs[:, cols(c)], ACT.Exp, scale=-0.5)\
                        .then_inc(rms_ready, 1)
            if split:
                for c in range(NCH):
                    act.wait_ge(scaled if rms_eps is not None else normed, c + 1)
                    nc.scalar.activation(split[0][:, cols(c)], final[:, cols(c)], ACT.Copy).then_inc(high_ready, 1)

        @block.vector
        def _(dve):
            if center:
                for c in range(NCH):
                    dve.wait_ge(mean_ready, c + 1)
                    nc.vector.tensor_tensor(dst[:, cols(c)], src[:, cols(c)], k.ps[:, c, :], ALU.subtract)\
                        .then_inc(centred, 1)
                for c in range(NCH):
                    dve.wait_ge(rstd_ready, c + 1)
                    nc.vector.tensor_tensor(dst[:, cols(c)], dst[:, cols(c)], rs[:, cols(c)], ALU.mult)\
                        .then_inc(normed, 1)
            if rms_eps is not None:
                for c in range(NCH):
                    dve.wait_ge(rms_ready, c + 1)
                    where = out[:, cols(c)] if len(out.shape) == 2 else out[:, c // 2, PADC + (c % 2) * CH:
                                                                           PADC + (c % 2 + 1) * CH]
                    nc.vector.scalar_tensor_tensor(out=where, in0=dst[:, cols(c)], scalar=weight,
                                                   in1=rs[:, cols(c)], op0=ALU.mult, op1=ALU.mult)\
                        .then_inc(scaled, 1)
            if split:
                for c in range(NCH):
                    dve.wait_ge(high_ready, c + 1)
                    nc.vector.tensor_tensor(split[1][:, cols(c)], final[:, cols(c)],
                                            split[0][:, cols(c)].bitcast(F32), ALU.subtract).then_inc(low_ready, 1)

    with nc.Block() as block:

        @block.sync
        def _(sp):
            for used in (mean_ready, centred, squared, var_ready, rstd_ready, normed, squared2, ms_ready, rms_ready,
                         scaled, high_ready, low_ready, log_done):
                sp.sem_clear(used)


def mixer_a_stage(k, d):
    nc = k.nc
    stage = ExitStack()
    sb = lambda name, shape, dt=F32: k.sb("a_" + name, shape, dt, ctx=stage)
    sem = lambda name: k.sem("a_" + name)
    w_in = sb("w_in", [P, 2 * DI])
    w_tap = sb("w_tap", [P, TAPS, P])
    taps = sb("taps", [P, TAPS, P])
    raw = sb("raw", [P, BATCH, PADDED])
    w_x = sb("w_x", [P, FT, 40])
    w_dt = sb("w_dt", [40, DI])
    w_out = sb("w_out", [P, FT, P])
    xp = sb("xp", [P, BATCH, PADDED])
    neg_a = sb("neg_a", [P, FT, NST])
    u, sz, delta, du = [sb(n, [P, FT, T]) for n in ("u", "sz", "delta", "du")]
    sel = sb("sel", [64, 32, P], F32R)
    rows = sb("rows", [64, T], F32R)
    sel_set = sem("sel_set")
    dt_row = sb("dt_row", [40, T])
    ps = k.ps

    w_loaded, taps_loaded, pad_zero, taps_ready, xz_ready, bank_read, conv_step, u_ready, bc_ready, high_done, rows_done, dt_ready, \
        pre_ready, abs_done, exp_done, log_done, delta_ready, du_ready, a_ready = [sem(n) for n in (
            "w_loaded taps_loaded pad_zero taps_ready xz_ready bank_read conv_step u_ready bc_ready high_done rows_done dt_ready "
            "pre_ready abs_done exp_done log_done delta_ready du_ready a_ready").split()]

    with nc.Block() as block:

        @block.sync
        def _(sp):
            sp.dma_start(taps[:, :, :].rearrange("p a b -> p (a b)"), d["tapsA"].partition_broadcast(P))\
                .then_inc(taps_loaded, 16)
            sp.dma_start(w_in[:, :], d["w_inA"]).then_inc(w_loaded, 16)
            sp.dma_start(w_x[:, :, :], d["w_xA"]).then_inc(w_loaded, 16)
            sp.dma_start(w_dt[32:40, :], d["w_dtA"]).then_inc(w_loaded, 16)
            sp.dma_start(w_out[:, :, :], d["w_outA"]).then_inc(w_loaded, 16)
            for scratch in k.slot_rows:
                sp.dma_start(scratch, d["slots"]).then_inc(k.slots_filled, 16)

        @block.gpsimd
        def _(pool):
            nc.gpsimd.memset(xp[:, :, 0:PADC], 0.0).then_inc(pad_zero, 1)
            nc.gpsimd.memset(raw[:, :, 0:PADC], 0.0).then_inc(pad_zero, 1)

        @block.vector
        def _(dve):
            dve.wait_ge(k.eye_loaded, 48)
            for half in range(2):
                src = k.eye[32 * half:32 * half + 32, 32 * half:32 * half + 32]
                nc.vector.tensor_copy(sel[32 * half:32 * half + 32, :, :],
                                      src.unsqueeze(2).to_broadcast([32, 32, P])).then_inc(sel_set, 1)

    norm_stage(k, "na", k.x, k.xn, True, k.eps5, weight=k.vec[:, VA_NORM:VA_NORM + 1], rms_eps=k.eps5, out=xp)

    with nc.Block() as block:

        @block.tensor
        def _(pe):
            pe.wait_ge(w_loaded, 16 * 4)
            pe.wait_ge(taps_ready, TAPS)
            pe.wait_ge(pad_zero, 2)

            def in_proj(c):
                b, t0 = divmod(c * CH, SEQ)
                for j in range(2 * FT):
                    n = c * 2 * FT + j
                    if n >= 4:
                        pe.wait_ge(bank_read, n - 3)
                    if j == 1:
                        for tap in range(TAPS):
                            off = PADC + t0 - (TAPS - 1) + tap
                            last = nc.tensor.matmul(ps[:, n % 4, :], w_tap[:, tap, :],
                                                    xp[:, b, off:off + CH], start=(tap == 0), stop=(tap == TAPS - 1))
                    else:
                        last = nc.tensor.matmul(ps[:, n % 4, :], w_in[:, j * P:(j + 1) * P],
                                                xp[:, b, PADC + t0:PADC + t0 + CH], start=True, stop=True)
                    last.then_inc(xz_ready, 1)

            def x_proj(c):
                pe.wait_ge(bank_read, c * 2 * FT + 2)
                pe.wait_ge(u_ready, c + 1)
                if c >= 1:
                    pe.wait_ge(rows_done, c)
                for f in range(FT):
                    last = nc.tensor.matmul(ps[0:40, 4, :], w_x[:, f, :], u[:, f, cols(c)],
                                            start=(f == 0), stop=(f == FT - 1))
                last.then_inc(bc_ready, 1)

            def dt_proj(c):
                pe.wait_ge(rows_done, c + 1)
                for f in range(FT):
                    n = c * FT + f
                    if n >= 2:
                        pe.wait_ge(pre_ready, n - 1)
                    nc.tensor.matmul(ps[:, 5 + n % 2, :], w_dt[32:40, f * P:(f + 1) * P],
                                     dt_row[32:40, cols(c)], start=True, stop=True).then_inc(dt_ready, 1)

            in_proj(0)
            for c in range(NCH):
                if c + 1 < NCH:
                    in_proj(c + 1)
                x_proj(c)
                dt_proj(c)

        @block.scalar
        def _(act):
            act.wait_ge(k.vec_loaded, 16)
            act.wait_ge(pad_zero, 2)
            for c in range(NCH):
                b, t0 = divmod(c * CH, SEQ)
                for j in range(2 * FT):
                    n = c * 2 * FT + j
                    act.wait_ge(xz_ready, n + 1)
                    if j == 0:
                        nc.scalar.activation(raw[:, b, PADC + t0:PADC + t0 + CH], ps[:, n % 4, :], ACT.Copy)\
                            .then_inc(bank_read, 1)
                    elif j < FT:
                        nc.scalar.activation(u[:, j, cols(c)], ps[:, n % 4, :], ACT.Silu,
                                             bias=k.vec[:, VA_CB + j:VA_CB + j + 1]).then_inc(bank_read, 1)
                    else:
                        nc.scalar.activation(sz[:, j - FT, cols(c)], ps[:, n % 4, :], ACT.Silu).then_inc(bank_read, 1)
                act.wait_ge(conv_step, (c + 1) * TAPS)
                nc.scalar.activation(u[:, 0, cols(c)], u[:, 0, cols(c)], ACT.Silu, bias=k.vec[:, VA_CB:VA_CB + 1])\
                    .then_inc(u_ready, 1)
            nc.scalar.activation(neg_a[:, :, :], k.vec[:, VA_ALOG:VA_ALOG + FT * NST]
                                 .rearrange("p (f n) -> p f n", f=FT), ACT.Exp).then_inc(a_ready, 1)
            for b in range(BATCH):
                at = slice(b * SEQ, (b + 1) * SEQ)
                act.wait_ge(pre_ready, (b + 1) * 2 * FT)
                nc.scalar.activation(du[:, :, at], delta[:, :, at], ACT.Abs).then_inc(abs_done, 1)
                act.wait_ge(abs_done, b + 1)
                nc.scalar.activation(du[:, :, at], du[:, :, at], ACT.Exp, scale=-1.0).then_inc(exp_done, 1)
                act.wait_ge(exp_done, b + 1)
                nc.scalar.activation(du[:, :, at], du[:, :, at], ACT.Ln, bias=1.0).then_inc(log_done, 1)

        @block.vector
        def _(dve):
            dve.wait_ge(taps_loaded, 16)
            dve.wait_ge(w_loaded, 16 * 4)
            for tap in range(TAPS):
                nc.vector.tensor_tensor(w_tap[:, tap, :], w_in[:, P:DI], taps[:, tap, :], ALU.mult)\
                    .then_inc(taps_ready, 1)
            dve.wait_ge(k.vec_loaded, 16)
            dve.wait_ge(pad_zero, 2)

            def convolve(c):
                b, t0 = divmod(c * CH, SEQ)
                for tap in range(TAPS):
                    off = PADC + t0 - (TAPS - 1) + tap
                    src, to, w = raw[:, b, off:off + CH], u[:, 0, cols(c)], k.vec[:, VA_TAPS + tap:VA_TAPS + tap + 1]
                    if tap == 0:
                        dve.wait_ge(bank_read, c * 2 * FT + 1)
                        nc.vector.tensor_scalar(to, src, w, None, ALU.mult).then_inc(conv_step, 1)
                    else:
                        dve.wait_ge(conv_step, c * TAPS + tap)
                        nc.vector.scalar_tensor_tensor(out=to, in0=src, scalar=w, in1=to, op0=ALU.mult,
                                                       op1=ALU.add).then_inc(conv_step, 1)

            convolve(0)
            for c in range(NCH):
                if c + 1 < NCH:
                    convolve(c + 1)
                dve.wait_ge(bc_ready, c + 1)
                nc.vector.tensor_copy(rows[0:32, cols(c)], ps[0:32, 4, :]).then_inc(high_done, 1)
                nc.vector.tensor_copy(dt_row[32:40, cols(c)], ps[32:40, 4, :])
                dve.wait_ge(high_done, c + 1)
                nc.vector.tensor_tensor(rows[32:64, cols(c)], ps[0:32, 4, :],
                                        rows[0:32, cols(c)].bitcast(F32), ALU.subtract).then_inc(rows_done, 1)
                for f in range(FT):
                    n = c * FT + f
                    dve.wait_ge(dt_ready, n + 1)
                    nc.vector.tensor_scalar(delta[:, f, cols(c)], ps[:, 5 + n % 2, :],
                                            k.vec[:, VA_DTB + f:VA_DTB + f + 1], None, ALU.add).then_inc(pre_ready, 1)
            dve.wait_ge(a_ready, 1)
            nc.vector.tensor_scalar(neg_a[:, :, :], neg_a[:, :, :], -1.0, None, ALU.mult).then_inc(a_ready, 1)
            for b in range(BATCH):
                at = slice(b * SEQ, (b + 1) * SEQ)
                dve.wait_ge(log_done, b + 1)
                nc.vector.scalar_tensor_tensor(out=delta[:, :, at], in0=delta[:, :, at], scalar=0.0,
                                               in1=du[:, :, at], op0=ALU.max, op1=ALU.add).then_inc(delta_ready, 1)
                dve.wait_ge(delta_ready, b + 1)
                nc.vector.tensor_tensor(du[:, :, at], delta[:, :, at], u[:, :, at], ALU.mult).then_inc(du_ready, 1)

    HALVES = SEQ // CH
    STEPS = NST * FT
    DEPTH = 4
    decayed_in = sb("b_u", [P, DEPTH, CH])
    h = sb("h", [P, DEPTH, CH])
    hc = sb("hc", [P, DEPTH, CH])
    c_sb = sb("c_sb", [P, 2, CH])
    state = sb("state", [P, STEPS])
    yz = sb("yz", [P, FT, CH])
    yd = sb("yd", [P, FT, CH])
    Y, B, C, A, O = 0, 2, 4, 5, 7
    b_ready, c_ready, c_copied, decay_ready, bu_ready, scanned, saved, hc_ready, y_added, y_ready, yd_ready, \
        yz_ready, out_ready, res_ready, x_added = [sem(n) for n in (
            "b_ready c_ready c_copied decay_ready bu_ready scanned saved hc_ready y_added y_ready yd_ready "
            "yz_ready out_ready res_ready x_added").split()]

    def at_half(b, half):
        return bass.ds(b * SEQ + half * CH, CH)

    with stage, nc.Block() as block:

        @block.tensor
        def _(pe):
            def half_sequence(b, half):
                first = half == 0 and b == 0
                g = b * HALVES + half
                def broadcast(n):
                    m = g * NST + n
                    if not (first and n < 2):
                        pe.wait_ge(bu_ready, (m - 1) * FT)
                    nc.tensor.matmul(ps[:, B + n % 2, :], sel[:, n, :], rows[:, at_half(b, half)],
                                     start=True, stop=True).then_inc(b_ready, 1)
                    if not (first and n < 1):
                        pe.wait_ge(c_copied, m)
                    nc.tensor.matmul(ps[:, C, :], sel[:, NST + n, :], rows[:, at_half(b, half)],
                                     start=True, stop=True).then_inc(c_ready, 1)

                def accumulate(n):
                    for f in range(FT):
                        s = n * FT + f
                        pe.wait_ge(hc_ready, g * STEPS + s + 1)
                        if n == 0 and not first:
                            pe.wait_ge(yd_ready, (g - 1) * FT + f + 1)
                        nc.tensor.matmul(ps[:, Y + f, :], k.eye[:, :], hc[:, s % DEPTH, :],
                                         start=(n == 0), stop=(n == NST - 1)).then_inc(y_added, 1)

                broadcast(0)
                broadcast(1)
                for n in range(2, NST):
                    broadcast(n)
                    accumulate(n - 2)
                accumulate(NST - 2)
                accumulate(NST - 1)
                if not first:
                    pe.wait_ge(res_ready, g)
                for f in range(FT):
                    pe.wait_ge(yz_ready, g * FT + f + 1)
                    last = nc.tensor.matmul(ps[:, O, :], w_out[:, f, :], yz[:, f, :], start=(f == 0), stop=(f == FT - 1))
                last.then_inc(out_ready, 1)

            SEQUENCES(pe, half_sequence, HALVES)

        @block.scalar
        def _(act):
            def half_sequence(b, half):
                first = half == 0 and b == 0
                g = b * HALVES + half
                for n in range(NST):
                    for f in range(FT):
                        s = n * FT + f
                        if not (first and s < 2):
                            act.wait_ge(scanned, g * STEPS + s - 1)
                        nc.scalar.activation(ps[:, A + s % 2, :], delta[:, f, at_half(b, half)], ACT.Exp,
                                             scale=neg_a[:, f, n:n + 1]).then_inc(decay_ready, 1)
                        if f == 0:
                            act.wait_ge(c_ready, g * NST + n + 1)
                            if not (first and n < 2):
                                act.wait_ge(hc_ready, g * STEPS + s - 2)
                            nc.scalar.activation(c_sb[:, n % 2, :], ps[:, C, :], ACT.Copy).then_inc(c_copied, 1)
                        if half + 1 < HALVES and s >= 1:
                            act.wait_ge(scanned, g * STEPS + s)
                            nc.scalar.activation(state[:, s - 1:s], h[:, (s - 1) % DEPTH, CH - 1:CH], ACT.Copy)\
                                .then_inc(saved, 1)
                if half + 1 < HALVES:
                    act.wait_ge(scanned, (g + 1) * STEPS)
                    nc.scalar.activation(state[:, STEPS - 1:STEPS], h[:, (STEPS - 1) % DEPTH, CH - 1:CH], ACT.Copy)\
                        .then_inc(saved, 1)

            SEQUENCES(act, half_sequence, HALVES)

        @block.vector
        def _(dve):
            def half_sequence(b, half):
                first = half == 0 and b == 0
                g = b * HALVES + half
                def times_b(s):
                    n, f = divmod(s, FT)
                    if f == 0:
                        dve.wait_ge(b_ready, g * NST + n + 1)
                    if not (first and s < DEPTH):
                        dve.wait_ge(scanned, g * STEPS + s - DEPTH + 1)
                    nc.vector.tensor_tensor(decayed_in[:, s % DEPTH, :], du[:, f, at_half(b, half)], ps[:, B + n % 2, :],
                                            ALU.mult).then_inc(bu_ready, 1)

                times_b(0)
                for s in range(STEPS):
                    if s + 1 < STEPS:
                        times_b(s + 1)
                    dve.wait_ge(decay_ready, g * STEPS + s + 1)
                    dve.wait_ge(bu_ready, g * STEPS + s + 1)
                    if not (first and s < DEPTH):
                        dve.wait_ge(hc_ready, g * STEPS + s - DEPTH + 1)
                    if half == 0 and s >= DEPTH:
                        dve.wait_ge(saved, b * STEPS + s - DEPTH + 1)
                    if half == 1:
                        dve.wait_ge(saved, b * STEPS + (STEPS if s < DEPTH else s + 1))
                    initial = state[:, s:s + 1] if half else 0.0
                    nc.vector.tensor_tensor_scan(h[:, s % DEPTH, :], ps[:, A + s % 2, :], decayed_in[:, s % DEPTH, :],
                                                 initial, ALU.mult, ALU.add).then_inc(scanned, 1)
                for f in range(FT):
                    dve.wait_ge(y_added, (g + 1) * STEPS)
                    nc.vector.scalar_tensor_tensor(out=yd[:, f, :], in0=u[:, f, at_half(b, half)],
                                                   scalar=k.vec[:, VA_D + f:VA_D + f + 1], in1=ps[:, Y + f, :],
                                                   op0=ALU.mult, op1=ALU.add).then_inc(yd_ready, 1)
                for f in range(FT):
                    dve.wait_ge(yd_ready, g * FT + f + 1)
                    nc.vector.tensor_tensor(yz[:, f, :], yd[:, f, :], sz[:, f, at_half(b, half)], ALU.mult)\
                        .then_inc(yz_ready, 1)
                dve.wait_ge(out_ready, g + 1)
                nc.vector.tensor_tensor(yd[:, 0, :], ps[:, O, :], k.xn[:, at_half(b, half)], ALU.add)\
                    .then_inc(res_ready, 1)
                dve.wait_ge(res_ready, g + 1)
                nc.vector.tensor_tensor(k.x[:, at_half(b, half)], k.x[:, at_half(b, half)], yd[:, 0, :], ALU.add)\
                    .then_inc(x_added, 1)

            SEQUENCES(dve, half_sequence, HALVES)

        @block.gpsimd
        def _(pool):
            def half_sequence(b, half):
                first = half == 0 and b == 0
                g = b * HALVES + half
                for s in range(STEPS):
                    n, f = divmod(s, FT)
                    pool.wait_ge(scanned, g * STEPS + s + 1)
                    if f == 0:
                        pool.wait_ge(c_copied, g * NST + n + 1)
                    if not (first and s < DEPTH):
                        pool.wait_ge(y_added, g * STEPS + s - DEPTH + 1)
                    nc.gpsimd.tensor_tensor(hc[:, s % DEPTH, :], h[:, s % DEPTH, :], c_sb[:, n % 2, :], ALU.mult)\
                        .then_inc(hc_ready, 1)

            SEQUENCES(pool, half_sequence, HALVES)


def SEQUENCES(eng, half_sequence, halves):
    for b in range(BATCH):
        for half in range(halves):
            half_sequence(b, half) if b == 0 else half_sequence(b, half)


def ffn_stage(k, d, which, tag):
    nc, ps, slot_rows = k.nc, k.ps, k.slot_rows[which]
    stage, counters = ExitStack(), ExitStack()
    sb = lambda name, shape, dt=F32, ctx=None: k.sb(f"{tag}_{name}", shape, dt, ctx=ctx or stage)
    used = []

    def sems(names):
        out = [k.sem(f"{tag}_{n}", counters) for n in names.split()]
        used.extend(out)
        return out

    gu_hi, gu_lo = [sb(n, [P, RING, GU], F32R) for n in ("gu_hi", "gu_lo")]
    dn_w = sb("dn_w", [P, RING, 2, TILES * P], F32R)
    raw_gu = sb("raw_gu", [P, 2, GU])
    raw_dn = sb("raw_dn", [P, 2, TILES, P])
    zero = sb("zero", [P, 1])
    B3 = 3
    xg = sb("xg", [P, B3, ROW])
    x_loaded = sems(" ".join(f"x_loaded{b}" for b in range(B3)))
    slot = sb("slot", [P, TOP, TT], I32)
    table = sb("table", [1, 2 * SLOT_TILES + EXPERTS], I32)
    gap_zero, split_step, w_ready, summed = sems("gap_zero split_step w_ready summed")
    raw_loaded = sems("raw_loaded0 raw_loaded1")
    rows_sent, late_loaded, sent = k.rows_sent, k.late_loaded, k.outputs_sent
    EARLY = 3
    LATE = (EXPERTS + 1 - EARLY) // 2
    PIECES = [(a, min(a + CH, GU)) for a in range(0, GU, CH)]
    NPIECE = len(PIECES) + TILES * P // CH

    def load_weights(eng, n):
        done = raw_loaded[n % 2] if n < EARLY else late_loaded[n % 2]
        gu, dn = raw_gu[:, n % 2, :], raw_dn[:, n % 2, :, :]
        if n == 0:
            eng.dma_start(gu[:, 0:2 * NI * P + TAIL], d["gu_shared"][:, 0:2 * NI * P + TAIL]).then_inc(done, 16)
            eng.dma_start(gu[:, GU - TAIL:GU], d["gu_shared"][:, 2 * NI * P + TAIL:2 * NI * P + 2 * TAIL])\
                .then_inc(done, 16)
        else:
            eng.dma_start(gu[:, 0:INTER], d["gu"][n - 1, :, 0:INTER]).then_inc(done, 16)
            eng.dma_start(gu[:, INTER:2 * INTER], d["gu"][n - 1, :, INTER:2 * INTER]).then_inc(done, 16)
        eng.dma_start(dn[:, 0:NI, :], d["dn"][n, 0:NI * P, :].rearrange("(i p) m -> p i m", p=P)).then_inc(done, 16)
        eng.dma_start(dn[0:TAIL, NI, :], d["dn"][n, NI * P:INTER, :]).then_inc(done, 16)

    def split_weights(pool, n):
        if n < EARLY:
            pool.wait_ge(raw_loaded[n % 2], 64 * (n // 2 + 1))
        else:
            pool.wait_ge(late_loaded[n % 2], 64 * ((n - EARLY) // 2 + 1 + LATE * which))
        place = n % RING
        gu, dn = raw_gu[:, n % 2, :], raw_dn[:, n % 2, :, :].rearrange("p i m -> p (i m)")
        parts = [(gu[:, a:b], gu_hi[:, place, a:b], gu_lo[:, place, a:b]) for a, b in PIECES]
        parts += [(dn[:, a:a + CH], dn_w[:, place, 0, a:a + CH], dn_w[:, place, 1, a:a + CH])
                  for a in range(0, TILES * P, CH)]

        def low(j):
            src, hi, lo = parts[j]
            pool.wait_ge(split_step, n * NPIECE + j + 1)
            nc.gpsimd.tensor_tensor(lo, src, hi.bitcast(F32), ALU.subtract).then_inc(w_ready, 1)

        for j, (src, hi, lo) in enumerate(parts):
            nc.gpsimd.tensor_tensor(hi, src, zero[:, :].to_broadcast([P, src.shape[1]]), ALU.add)\
                .then_inc(split_step, 1)
            if j:
                low(j - 1)
        low(NPIECE - 1)

    shared = ExitStack()
    x_hi, x_lo = [sb(n, [P, T], F32R, ctx=shared) for n in ("x_hi", "x_lo")]
    w_gate = sb("w_gate", [P, EXPERTS], ctx=shared)
    masks = sb("masks", [P, 2, P], ctx=shared)
    one = sb("one", [P, P], ctx=shared)
    names = "logit prob chosen rank hit1 hit2 spare place"
    logit, prob, chosen, rank, hit1, hit2, spare, place = [sb(n, [P, TT, EXPERTS], ctx=shared) for n in names.split()]
    top, best1, best2, den, first_max, slot_f = [sb(n, [P, TT], ctx=shared) for n in
                                                 "top best1 best2 den first_max slot_f".split()]
    total, upto, keep, more = [sb(n, [P, EXPERTS, TT], ctx=shared) for n in "total upto keep more".split()]
    tiles, tiles_upto = [sb(n, [P, EXPERTS], ctx=shared) for n in ("tiles", "tiles_upto")]
    past = sb("past", [1, SLOT_TILES, EXPERTS - 1], ctx=shared)
    found = sb("found", [1, SLOT_TILES], ctx=shared)
    gate_loaded, one_set, logits_ready, step, exp_ready, chosen_ready, counts_ready, turned, slots_ready, rows_copied, rows_ready, \
        table_ready = sems("gate_loaded one_set logits_ready router_step exp_ready chosen_ready counts_ready turned "
                           "slots_ready rows_copied rows_ready table_ready")
    L = EXPERTS
    thresholds = k.fc[:, L:L + TT]
    numbers = k.fc[0:1, L + TT:L + TT + SLOT_TILES]
    ring_steps = k.fc[0:1, L + TT + SLOT_TILES:]

    def first_load(sp):
        sp.dma_start(w_gate[:, :], d["w_gateF"]).then_inc(gate_loaded, 16)
        sp.dma_start(masks[:, :, :], d["masks"]).then_inc(gate_loaded, 16)
        sp.wait_ge(gap_zero, 4)
        load_weights(sp, 0)
        load_weights(sp, 1)

    def first_split(pool):
        nc.gpsimd.memset(raw_gu[:, 0, GU - UT:GU - TAIL], 0.0).then_inc(gap_zero, 1)
        nc.gpsimd.memset(raw_gu[:, 1, 2 * INTER:GU], 0.0).then_inc(gap_zero, 1)
        nc.gpsimd.memset(raw_dn[:, :, NI, :], 0.0).then_inc(gap_zero, 1)
        nc.gpsimd.memset(zero[:, :], 0.0).then_inc(gap_zero, 1)
        nc.gpsimd.memset(one[:, :], 1.0).then_inc(one_set, 1)
        pool.wait_ge(gap_zero, 4)
        split_weights(pool, 0)

    norm_stage(k, tag + "n", k.x, k.xn, True, k.eps5, split=(x_hi, x_lo), sync_part=first_load, pool_part=first_split)
    rows = sb("rows", [P, TOP, TT, ROW], ctx=shared)

    def wide(v):
        return v[:, :].unsqueeze(2).to_broadcast([P, TT, EXPERTS])

    gate = sb("gate", [P, 2, CH], ctx=shared)
    prod = sb("prod", [P, 2, CH], ctx=shared)
    p_hi, p_lo = [sb(n, [P, 4, CH], F32R, ctx=shared) for n in ("p_hi", "p_lo")]
    G, U, Y, R, TR1 = 0, 2, 4, 6, 7
    N = TT * EXPERTS
    PER = NCH * TILES
    g_ready, gu_ready, silu_done, prod_done, high_ready, low_ready, x_added = sems(
        "g_ready gu_ready silu_done prod_done high_ready low_ready x_added")

    def k_of(i):
        return P if i < NI else TAIL

    with shared, nc.Block() as block:

        @block.sync
        def _(sp):
            load_weights(sp, 2)
            sp.wait_ge(rows_sent, 16 * TOP * TT * (which + 1))
            for j in range(B3):
                sp.dma_start(xg[:, j, :], slot_rows[j * P:(j + 1) * P, :]).then_inc(x_loaded[j], 16)

        @block.gpsimd
        def _(pool):
            split_weights(pool, 1)
            pool.wait_ge(k.slots_filled, 32)
            pool.wait_ge(rows_copied, TOP * TT // 4)
            pool.wait_ge(rows_ready, 1 + TOP)
            pool.wait_ge(slots_ready, TOP)
            for t in range(TT):
                for c in range(TOP):
                    nc.gpsimd.indirect_dma_start(slot_rows, bass.IndirectOffsetOnAxis(ap=slot[:, c, t:t + 1], axis=0),
                                                 rows[:, c, t, :], None).then_inc(rows_sent, 16)
            pool.wait_ge(rows_sent, 16 * TOP * TT * (which + 1))

        @block.tensor
        def _(pe):
            def product(out, w_hi, w_lo, v_hi, v_lo, start, stop):
                nc.tensor.matmul(out, w_hi, v_hi, start=start, stop=False)
                nc.tensor.matmul(out, w_hi, v_lo, start=False, stop=False)
                return nc.tensor.matmul(out, w_lo, v_hi, start=False, stop=stop)

            def gate_up(q):
                c, i = divmod(q, TILES)
                xs = (x_hi[:, cols(c)], x_lo[:, cols(c)])
                if q >= 2:
                    pe.wait_ge(prod_done, q - 1)
                if i < NI:
                    a = i * P
                    product(ps[:, G + i % 2, :], gu_hi[:, 0, a:a + P], gu_lo[:, 0, a:a + P], *xs, True, True)\
                        .then_inc(g_ready, 1)
                    a += NI * P
                    product(ps[:, U + i % 2, :], gu_hi[:, 0, a:a + P], gu_lo[:, 0, a:a + P], *xs, True, True)\
                        .then_inc(gu_ready, 1)
                else:
                    a, m = 2 * NI * P, UT + TAIL
                    product(ps[0:m, G + i % 2, :], gu_hi[:, 0, a:a + m], gu_lo[:, 0, a:a + m], *xs, True, True)\
                        .then_inc(g_ready, 1)

            def down(q):
                c, i = divmod(q, TILES)
                if i == 0 and c >= 2:
                    pe.wait_ge(x_added, c - 1)
                pe.wait_ge(low_ready, q + 1)
                m, a = k_of(i), i * P
                product(ps[:, Y + c % 2, :], dn_w[0:m, 0, 0, a:a + P], dn_w[0:m, 0, 1, a:a + P],
                        p_hi[0:m, q % 4, :], p_lo[0:m, q % 4, :], i == 0, i == TILES - 1).then_inc(summed, 1)

            pe.wait_ge(gate_loaded, 32)
            for t in range(TT):
                last = nc.tensor.matmul(ps[:, R, t * EXPERTS:(t + 1) * EXPERTS], k.xn[:, t * P:(t + 1) * P],
                                        w_gate[:, :], start=True, stop=True)
            last.then_inc(logits_ready, 1)
            for q in range(PER):
                gate_up(q)
                if q >= 2:
                    down(q - 2)
                if 2 <= q < 2 + TT // 4:
                    g = q - 2
                    if g:
                        pe.wait_ge(rows_copied, TOP * g)
                    for t in range(4):
                        last = nc.tensor.transpose(ps[:, TR1, t * P:(t + 1) * P],
                                                   k.xn[:, (4 * g + t) * P:(4 * g + t + 1) * P], k.eye[:, :])
                    last.then_inc(turned, 1)
                if q == 7:
                    pe.wait_ge(one_set, 1)
                    pe.wait_ge(chosen_ready, 1)
                    flat = chosen[:, :, :].rearrange("p t e -> p (t e)")
                    nc.tensor.matmul(ps[:, R, N:2 * N], masks[:, 0, :], flat, start=True, stop=True)
                    nc.tensor.matmul(ps[:, R, 2 * N:3 * N], one[:, :], flat, start=True, stop=True)\
                        .then_inc(counts_ready, 1)
            down(PER - 2)
            down(PER - 1)

        @block.scalar
        def _(act):
            def high(q):
                m = k_of(q % TILES)
                act.wait_ge(prod_done, q + 1)
                if q >= 4:
                    act.wait_ge(summed, q - 3)
                nc.scalar.activation(p_hi[0:m, q % 4, :], prod[0:m, q % 2, :], ACT.Copy).then_inc(high_ready, 1)

            act.wait_ge(step, 2)
            nc.scalar.activation(prob[:, :, :], logit[:, :, :], ACT.Exp).then_inc(exp_ready, 1)
            for q in range(PER):
                i, m = q % TILES, k_of(q % TILES)
                if 3 <= q < 3 + TT // 4:
                    g = q - 3
                    act.wait_ge(turned, g + 1)
                    for c in range(TOP):
                        nc.scalar.activation(rows[:, c, 4 * g:4 * g + 4, 0:P],
                                             ps[:, TR1, :].rearrange("p (t d) -> p t d", d=P), ACT.Copy)\
                            .then_inc(rows_copied, 1)
                act.wait_ge(g_ready, q + 1)
                nc.scalar.activation(gate[0:m, q % 2, :], ps[0:m, G + i % 2, :], ACT.Silu).then_inc(silu_done, 1)
                if q:
                    high(q - 1)
            high(PER - 1)

        @block.vector
        def _(dve):
            done = [0]

            def then(ins):
                done[0] += 1
                ins.then_inc(step, 1)
                dve.wait_ge(step, done[0])

            def softmax():
                dve.wait_ge(logits_ready, 1)
                logits = ps[:, R, 0:N].rearrange("p (t e) -> p t e", e=EXPERTS)
                then(nc.vector.tensor_reduce(top[:, :], logits, AX.X, ALU.max))
                then(nc.vector.tensor_tensor(logit[:, :, :], logits, wide(top), ALU.subtract))
                nc.vector.tensor_copy(rows[:, :, :, P:P + 1].rearrange("p a t o -> p (a t) o").bitcast(I32),
                                      k.places[:, 0:TOP * TT].unsqueeze(2)).then_inc(rows_ready, 1)
                nc.vector.memset(keep[:, :, :], 1.0).then_inc(step, 1)
                dve.wait_ge(step, 3)
                nc.vector.memset(keep[:, :, 0:1], 0.0).then_inc(step, 1)
                done[0] += 2
                dve.wait_ge(exp_ready, 1)
                then(nc.vector.tensor_reduce(den[:, :], prob[:, :, :], AX.X, ALU.add))
                then(nc.vector.reciprocal(den[:, :], den[:, :]))
                then(nc.vector.tensor_tensor(prob[:, :, :], prob[:, :, :], wide(den), ALU.mult))

            def choose(left, best, hit):
                then(nc.vector.tensor_reduce(best[:, :], left[:, :, :], AX.X, ALU.max))
                then(nc.vector.tensor_tensor(rank[:, :, :], left[:, :, :], wide(best), ALU.is_ge))
                then(nc.vector.tensor_tensor(rank[:, :, :], rank[:, :, :],
                                             k.fc[:, 0:L].unsqueeze(1).to_broadcast([P, TT, EXPERTS]), ALU.mult))
                then(nc.vector.tensor_reduce(first_max[:, :], rank[:, :, :], AX.X, ALU.max))
                then(nc.vector.tensor_tensor(hit[:, :, :], rank[:, :, :], wide(first_max), ALU.is_equal))
                if hit is hit1:
                    then(nc.vector.scalar_tensor_tensor(out=spare[:, :, :], in0=hit1[:, :, :], scalar=-4.0,
                                                        in1=prob[:, :, :], op0=ALU.mult, op1=ALU.add))

            def weigh():
                then(nc.vector.tensor_tensor(chosen[:, :, :], hit1[:, :, :], hit2[:, :, :], ALU.add))
                nc.vector.scalar_tensor_tensor(out=den[:, :], in0=best1[:, :], scalar=1e-8, in1=best2[:, :],
                                               op0=ALU.add, op1=ALU.add).then_inc(chosen_ready, 1)
                dve.wait_ge(chosen_ready, 1)
                then(nc.vector.reciprocal(den[:, :], den[:, :]))
                for c, best in enumerate((best1, best2)):
                    nc.vector.tensor_tensor(rows[:, c, :, P + 1], best[:, :], den[:, :], ALU.mult).then_inc(rows_ready, 1)

            def count_tiles():
                dve.wait_ge(counts_ready, 1)
                then(nc.vector.tensor_copy(total[:, :, :], ps[:, R, 2 * N:3 * N].rearrange("p (t e) -> p e t", e=EXPERTS)))
                then(nc.vector.tensor_tensor_scan(upto[:, :, :].rearrange("p e t -> p (e t)"),
                                                  keep[:, :, :].rearrange("p e t -> p (e t)"),
                                                  total[:, :, :].rearrange("p e t -> p (e t)"), 0.0, ALU.mult, ALU.add))
                then(nc.vector.tensor_tensor(more[:, :, :], upto[:, :, TT - 1:TT].to_broadcast([P, EXPERTS, TT]),
                                             thresholds.unsqueeze(1).to_broadcast([P, EXPERTS, TT]), ALU.is_gt))
                then(nc.vector.tensor_reduce(tiles[:, :], more[:, :, :], AX.X, ALU.add))
                then(nc.vector.tensor_tensor_scan(tiles_upto[:, :], one[:, 0:EXPERTS], tiles[:, :], 0.0,
                                                  ALU.mult, ALU.add))
                then(nc.vector.tensor_tensor(tiles[:, :], tiles_upto[:, :], tiles[:, :], ALU.subtract))
                then(nc.vector.tensor_tensor(upto[:, :, :], upto[:, :, :], total[:, :, :], ALU.subtract))
                then(nc.vector.scalar_tensor_tensor(out=upto[:, :, :],
                                                    in0=tiles[:, :].unsqueeze(2).to_broadcast([P, EXPERTS, TT]),
                                                    scalar=float(P), in1=upto[:, :, :], op0=ALU.mult, op1=ALU.add))

            def find_slots():
                then(nc.vector.tensor_tensor(place[:, :, :], ps[:, R, N:2 * N].rearrange("p (t e) -> p t e", e=EXPERTS),
                                             chosen[:, :, :], ALU.subtract))
                then(nc.vector.tensor_tensor(place[:, :, :], place[:, :, :],
                                             upto[:, :, :].rearrange("p e t -> p t e"), ALU.add))
                for c, hit in enumerate((hit1, hit2)):
                    then(nc.vector.tensor_tensor(rank[:, :, :], hit[:, :, :], place[:, :, :], ALU.mult))
                    then(nc.vector.tensor_reduce(slot_f[:, :], rank[:, :, :], AX.X, ALU.add))
                    nc.vector.tensor_copy(slot[:, c, :], slot_f[:, :]).then_inc(slots_ready, 1)
                    dve.wait_ge(slots_ready, c + 1)

            def fill_table():
                then(nc.vector.tensor_tensor(past[:, :, :], numbers.unsqueeze(2).to_broadcast([1, SLOT_TILES, EXPERTS - 1]),
                                             tiles[0:1, 1:EXPERTS].unsqueeze(1).to_broadcast([1, SLOT_TILES, EXPERTS - 1]),
                                             ALU.is_ge))
                then(nc.vector.tensor_reduce(found[:, :], past[:, :, :], AX.X, ALU.add))
                then(nc.vector.tensor_copy(table[:, 0:SLOT_TILES], found[:, :]))
                then(nc.vector.tensor_tensor(past[:, :, :], past[:, :, :],
                                             ring_steps.unsqueeze(1).to_broadcast([1, SLOT_TILES, EXPERTS - 1]), ALU.mult))
                then(nc.vector.tensor_reduce(found[:, :], past[:, :, :], AX.X, ALU.add))
                then(nc.vector.tensor_scalar(found[:, :], found[:, :], 1.0, None, ALU.add))
                then(nc.vector.tensor_copy(table[:, SLOT_TILES:2 * SLOT_TILES], found[:, :]))
                nc.vector.tensor_copy(table[:, 2 * SLOT_TILES:], tiles[0:1, :]).then_inc(table_ready, 1)

            def low(q):
                m = k_of(q % TILES)
                dve.wait_ge(high_ready, q + 1)
                nc.vector.tensor_tensor(p_lo[0:m, q % 4, :], prod[0:m, q % 2, :],
                                        p_hi[0:m, q % 4, :].bitcast(F32), ALU.subtract).then_inc(low_ready, 1)

            def add(c):
                dve.wait_ge(summed, (c + 1) * TILES)
                nc.vector.tensor_tensor(k.x[:, cols(c)], k.x[:, cols(c)], ps[:, Y + c % 2, :], ALU.add)\
                    .then_inc(x_added, 1)

            softmax()
            for q in range(PER):
                c, i = divmod(q, TILES)
                m = k_of(i)
                dve.wait_ge(silu_done, q + 1)
                if i < NI:
                    dve.wait_ge(gu_ready, c * NI + i + 1)
                    up = ps[:, U + i % 2, :]
                else:
                    up = ps[UT:UT + TAIL, G + i % 2, :]
                if q >= 2:
                    dve.wait_ge(low_ready, q - 1)
                nc.vector.tensor_tensor(prod[0:m, q % 2, :], gate[0:m, q % 2, :], up, ALU.mult).then_inc(prod_done, 1)
                if q:
                    low(q - 1)
                if i == 3 and c:
                    add(c - 1)
                if q == 1:
                    choose(prob, best1, hit1)
                if q == 3:
                    choose(spare, best2, hit2)
                if q == 5:
                    weigh()
                if q == 8:
                    count_tiles()
                if q == 9:
                    find_slots()
                if q == 12:
                    fill_table()
            low(PER - 1)
            add(NCH - 1)

    routed = ExitStack()
    HF = HALVES
    xt_hi, xt_lo = [sb(n, [P, B3, P], F32R, ctx=routed) for n in ("xt_hi", "xt_lo")]
    gate2 = sb("gate2", [P, 2, HF[0]], ctx=routed)
    prod2 = sb("prod2", [P, B3, TILES * P], ctx=routed)
    q_hi, q_lo = [sb(n, [P, B3, TILES * P], F32R, ctx=routed) for n in ("q_hi", "q_lo")]
    cross = sb("cross", [P, B3, P], ctx=routed)
    ys = sb("ys", [P, SLOT_TILES, P], ctx=routed)
    back = sb("back", [P, SLOT_TILES], I32, ctx=routed)
    share = sb("share", [P, B3], ctx=routed)
    XB, TR, YB = 4, 5, 7
    pp_zero, back_ready, share_ready, x_turned, xh_ready, xl_ready, gg_ready, uu_ready, ss_ready, pp_ready, \
        pt_ready, qh_ready, ql_ready, cross_ready, ys_ready = sems(
            "pp_zero back_ready share_ready x_turned xh_ready xl_ready gg_ready uu_ready ss_ready pp_ready "
            "pt_ready qh_ready ql_ready cross_ready ys_ready")

    def all_tiles(eng, tile):
        for b in range(B3):
            tile(b, b, 0)
        with eng.Fori(1, SLOT_TILES // B3) as turn:
            for b in range(B3):
                tile(turn * B3 + b, b, turn)

    def from_tile(eng, j, first, sem, value):
        if not (isinstance(j, int) and j < first):
            eng.wait_ge(sem, value)

    with routed, nc.Block() as block:

        @block.sync
        def _(sp):
            with sp.Fori(1, SLOT_TILES // B3) as turn:
                for b in range(B3):
                    j = turn * B3 + b
                    sp.wait_ge(x_turned, j - B3 + 1)
                    sp.wait_ge(back_ready, j - B3 + 1)
                    sp.wait_ge(share_ready, j - B3 + 1)
                    sp.dma_start(xg[:, b, :], slot_rows[bass.ds(j * P, P), :]).then_inc(x_loaded[b], 16)

        @block.gpsimd
        def _(pool):
            load_weights(pool, EARLY)
            for n in range(2, EXPERTS + 1):
                if EARLY < n + 1 <= EXPERTS:
                    pool.wait_ge(w_ready, n * NPIECE)
                    load_weights(pool, n + 1)
                if n == RING:
                    pool.wait_ge(summed, PER)
                if n > RING:
                    first = pool.value_load(table[0:1, 2 * SLOT_TILES + n - RING:2 * SLOT_TILES + n - RING + 1],
                                            min_val=1, max_val=SLOT_TILES)
                    pool.wait_ge(summed, first + PER)
                split_weights(pool, n)
            for j in range(SLOT_TILES):
                pool.wait_ge(back_ready, j + 1)
                pool.wait_ge(ys_ready, j + 1)
                nc.gpsimd.indirect_dma_start(k.token_rows, bass.IndirectOffsetOnAxis(ap=back[:, j:j + 1], axis=0),
                                             ys[:, j, :], None).then_inc(sent, 16)
            pool.wait_ge(sent, 16 * SLOT_TILES * (which + 1))

        @block.tensor
        def _(pe):
            def turn_products(j, b):
                pe.wait_ge(pp_ready, 2 * j + 2)
                from_tile(pe, j, 1, ql_ready, 2 * j)
                for i in range(TILES):
                    last = nc.tensor.transpose(ps[:, TR + i // 4, (i % 4) * P:(i % 4 + 1) * P],
                                               prod2[:, b, i * P:(i + 1) * P], k.eye[:, :])
                    if i % 4 == 3:
                        last.then_inc(pt_ready, 1)

            def down(j, b, ring):
                pe.wait_ge(ql_ready, 2 * j + 2)
                from_tile(pe, j, 1, ys_ready, j)
                for i in range(TILES):
                    a = slice(i * P, (i + 1) * P)
                    nc.tensor.matmul(ps[:, YB, 0:2 * P], q_hi[:, b, a], dn_at(ring, i), start=(i == 0),
                                     stop=False, skip_group_check=True)
                    last = nc.tensor.matmul(ps[:, YB, 0:P], q_lo[:, b, a], dn_high_at(ring, i), start=False,
                                            stop=(i == TILES - 1), skip_group_check=True)
                last.then_inc(summed, 1)
                return last

            def dn_at(ring, i):
                return dn_w[:, bass.ds(ring, 1), :, i * P:(i + 1) * P].rearrange("p r h m -> p (r h) m")

            def dn_high_at(ring, i):
                return dn_w[:, bass.ds(ring, 1), 0, i * P:(i + 1) * P].rearrange("p r m -> p (r m)")

            def tile(j, b, turn):
                expert = pe.value_load(table[0:1, bass.ds(j, 1)], min_val=0, max_val=EXPERTS - 1)
                ring = pe.value_load(table[0:1, bass.ds(SLOT_TILES + j, 1)], min_val=0, max_val=RING - 1)
                pe.wait_ge(x_loaded[b], turn * 16 + 16)
                from_tile(pe, j, 1, xl_ready, j)
                nc.tensor.transpose(ps[:, XB, 0:P], xg[:, b, 0:P], k.eye[:, :]).then_inc(x_turned, 1)
                if not (isinstance(j, int) and j < 2):
                    before = pe.value_load(table[0:1, bass.ds(SLOT_TILES + j - 2, 1)], min_val=0, max_val=RING - 1)
                    down(j - 2, (b - 2) % B3, before)
                if not (isinstance(j, int) and j < 1):
                    turn_products(j - 1, (b - 1) % B3)
                pe.wait_ge(w_ready, expert * NPIECE + 2 * NPIECE)
                pe.wait_ge(xl_ready, j + 1)
                for half in range(2):
                    for up in range(2):
                        a, m = (half * 2 * HF[0]) + up * HF[half], HF[half]
                        out = ps[:, 2 * half + up, 0:m]
                        w_hi = gu_hi[:, bass.ds(ring, 1), a:a + m].rearrange("p r m -> p (r m)")
                        w_lo = gu_lo[:, bass.ds(ring, 1), a:a + m].rearrange("p r m -> p (r m)")
                        nc.tensor.matmul(out, xt_hi[:, b, :], w_hi, start=True, stop=False)
                        nc.tensor.matmul(out, xt_hi[:, b, :], w_lo, start=False, stop=False)
                        nc.tensor.matmul(out, xt_lo[:, b, :], w_hi, start=False, stop=True)\
                            .then_inc(uu_ready if up else gg_ready, 1)

            pe.wait_ge(pp_zero, 1)
            all_tiles(pe, tile)
            J = SLOT_TILES
            before = pe.value_load(table[0:1, 2 * J - 2:2 * J - 1], min_val=0, max_val=RING - 1)
            down(J - 2, (J - 2) % B3, before)
            turn_products(J - 1, (J - 1) % B3)
            before = pe.value_load(table[0:1, 2 * J - 1:2 * J], min_val=0, max_val=RING - 1)
            down(J - 1, (J - 1) % B3, before)

        @block.scalar
        def _(act):
            def evac(j, b):
                for half in range(2):
                    act.wait_ge(pt_ready, 2 * j + half + 1)
                    from_tile(act, j, B3, summed, PER + j - B3 + 1)
                    nc.scalar.activation(q_hi[:, b, half * CH:(half + 1) * CH], ps[:, TR + half, :], ACT.Copy)\
                        .then_inc(qh_ready, 1)

            def crossed(j, b):
                act.wait_ge(summed, PER + j + 1)
                act.wait_ge(share_ready, j + 1)
                nc.scalar.activation(cross[:, b, :], ps[:, YB, P:2 * P], ACT.Copy, scale=share[:, b:b + 1]).then_inc(cross_ready, 1)

            def tile(j, b, turn):
                act.wait_ge(x_turned, j + 1)
                nc.scalar.activation(xt_hi[:, b, :], ps[:, XB, 0:P], ACT.Copy).then_inc(xh_ready, 1)
                if not (isinstance(j, int) and j < 2):
                    crossed(j - 2, (b - 2) % B3)
                if not (isinstance(j, int) and j < 1):
                    evac(j - 1, (b - 1) % B3)
                for half in range(2):
                    act.wait_ge(gg_ready, 2 * j + half + 1)
                    if not (isinstance(j, int) and j < 1):
                        act.wait_ge(pp_ready, 2 * j + half - 1)
                    nc.scalar.activation(gate2[:, half, 0:HF[half]], ps[:, 2 * half, 0:HF[half]], ACT.Silu)\
                        .then_inc(ss_ready, 1)

            all_tiles(act, tile)
            J = SLOT_TILES
            crossed(J - 2, (J - 2) % B3)
            evac(J - 1, (J - 1) % B3)
            crossed(J - 1, (J - 1) % B3)

        @block.vector
        def _(dve):
            def evac(j, b):
                for half in range(2):
                    dve.wait_ge(qh_ready, 2 * j + half + 1)
                    at = slice(half * CH, (half + 1) * CH)
                    nc.vector.tensor_tensor(q_lo[:, b, at], ps[:, TR + half, :], q_hi[:, b, at].bitcast(F32),
                                            ALU.subtract).then_inc(ql_ready, 1)

            def finish(j, b):
                dve.wait_ge(cross_ready, j + 1)
                nc.vector.scalar_tensor_tensor(out=ys[:, bass.ds(j, 1), :].rearrange("p a m -> p (a m)"),
                                               in0=ps[:, YB, 0:P], scalar=share[:, b:b + 1], in1=cross[:, b, :],
                                               op0=ALU.mult, op1=ALU.add).then_inc(ys_ready, 1)

            def tile(j, b, turn):
                dve.wait_ge(xh_ready, j + 1)
                nc.vector.tensor_copy(back[:, bass.ds(j, 1)], xg[:, b, P:P + 1].bitcast(I32)).then_inc(back_ready, 1)
                from_tile(dve, j, B3, cross_ready, j - B3 + 1)
                from_tile(dve, j, B3, ys_ready, j - B3 + 1)
                nc.vector.tensor_copy(share[:, b:b + 1], xg[:, b, P + 1:ROW]).then_inc(share_ready, 1)
                nc.vector.tensor_tensor(xt_lo[:, b, :], ps[:, XB, 0:P], xt_hi[:, b, :].bitcast(F32),
                                        ALU.subtract).then_inc(xl_ready, 1)
                if not (isinstance(j, int) and j < 2):
                    finish(j - 2, (b - 2) % B3)
                if not (isinstance(j, int) and j < 1):
                    evac(j - 1, (b - 1) % B3)
                for half in range(2):
                    dve.wait_ge(ss_ready, 2 * j + half + 1)
                    dve.wait_ge(uu_ready, 2 * j + half + 1)
                    nc.vector.tensor_tensor(prod2[:, b, half * HF[0]:half * HF[0] + HF[half]],
                                            gate2[:, half, 0:HF[half]], ps[:, 2 * half + 1, 0:HF[half]], ALU.mult)\
                        .then_inc(pp_ready, 1)

            nc.vector.memset(prod2[:, :, INTER:], 0.0).then_inc(pp_zero, 1)
            all_tiles(dve, tile)
            J = SLOT_TILES
            finish(J - 2, (J - 2) % B3)
            evac(J - 1, (J - 1) % B3)
            finish(J - 1, (J - 1) % B3)

    combine = ExitStack()
    chosen_out = sb("chosen_out", [P, TOP, TT, P], ctx=combine)
    out_loaded = sems(" ".join(f"out_loaded{g}" for g in range(NCH)))
    both_ready, tokens_ready, out_added = sems("both_ready tokens_ready out_added")
    PT = TT // NCH
    with combine, nc.Block() as block:

        @block.sync
        def _(sp):
            for g in range(NCH):
                for c in range(TOP):
                    sp.dma_start(chosen_out[:, c, g * PT:(g + 1) * PT, :],
                                 k.token_rows[c * T + g * CH:c * T + (g + 1) * CH, :]
                                 .rearrange("(t p) m -> p t m", p=P)).then_inc(out_loaded[g], 16)

        @block.tensor
        def _(pe):
            for g in range(NCH):
                pe.wait_ge(both_ready, g + 1)
                for t in range(PT):
                    last = nc.tensor.transpose(ps[:, g, t * P:(t + 1) * P], chosen_out[:, 0, g * PT + t, :],
                                               k.eye[:, :])
                last.then_inc(tokens_ready, 1)

        @block.vector
        def _(dve):
            def add(g):
                dve.wait_ge(tokens_ready, g + 1)
                nc.vector.tensor_tensor(k.x[:, cols(g)], k.x[:, cols(g)], ps[:, g, :], ALU.add)\
                    .then_inc(out_added, 1)

            for g in range(NCH):
                dve.wait_ge(out_loaded[g], 16 * TOP)
                at = slice(g * PT, (g + 1) * PT)
                nc.vector.tensor_tensor(chosen_out[:, 0, at, :], chosen_out[:, 0, at, :], chosen_out[:, 1, at, :],
                                        ALU.add).then_inc(both_ready, 1)
                if g:
                    add(g - 1)
            add(NCH - 1)
    stage.close()
    with counters, nc.Block() as block:

        @block.sync
        def _(sp):
            for s in used:
                sp.sem_clear(s)


def mixer_b_stage(k, d):
    nc, ps = k.nc, k.ps
    stage = ExitStack()
    sb = lambda name, shape, dt=F32, ctx=None: k.sb("b_" + name, shape, dt, ctx=ctx or stage)
    sem = lambda name: k.sem("b_" + name)
    HEADS, HD = 4, 64
    TT = T // P
    CONV = 4
    MT = 3
    conv = sb("conv", [P, 4, T])
    xs, bT, cT = conv[:, 0:2, :], conv[:, 2, :], conv[:, 3, :]
    sz, y = [sb(n, [P, FT, T]) for n in ("sz", "y")]
    head_rows = sb("head_rows", [P, 2, HEADS])
    dt = sb("dt", [P, TT, HEADS])
    dt_log = sb("dt_log", [P, TT, HEADS])
    dta = sb("dta", [P, TT, HEADS])
    neg_a = sb("neg_a", [P, HEADS])
    w_out = sb("w_out", [P, FT, P])
    pre = ExitStack()
    xp = sb("xp", [P, BATCH, PADDED], ctx=pre)
    w_in = sb("w_in", [P, 2 * DI + 2 * P + HEADS], ctx=pre)
    w_tap = sb("w_tap", [P, TAPS, P], ctx=pre)
    taps = sb("taps", [P, TAPS, P], ctx=pre)
    raw = sb("raw_conv", [P, CONV - 1, BATCH, PADDED], ctx=pre)
    loaded, pad_zero, taps_ready, xz_ready, bank_read, conv_step, silu_done, dt_ready, dt_step, a_ready, dta_ready = [sem(n) for n in (
        "loaded pad_zero taps_ready xz_ready bank_read conv_step silu_done dt_ready dt_step a_ready dta_ready").split()]

    with nc.Block() as block:

        @block.sync
        def _(sp):
            sp.dma_start(taps[:, :, :].rearrange("p a b -> p (a b)"), d["tapsB"].partition_broadcast(P))\
                .then_inc(loaded, 16)
            sp.dma_start(w_in[:, :], d["w_inB"]).then_inc(loaded, 16)
            sp.dma_start(w_out[:, :, :], d["w_outB"]).then_inc(loaded, 16)
            sp.dma_start(head_rows[:, :, :].rearrange("p a b -> p (a b)"), d["headsB"].partition_broadcast(P))\
                .then_inc(loaded, 16)

        @block.gpsimd
        def _(pool):
            nc.gpsimd.memset(xp[:, :, 0:PADC], 0.0).then_inc(pad_zero, 1)
            nc.gpsimd.memset(raw[:, :, :, 0:PADC], 0.0).then_inc(pad_zero, 1)

    norm_stage(k, "nb", k.x, k.xn, True, k.eps5, weight=k.vec[:, VB_NORM:VB_NORM + 1], rms_eps=k.eps6, out=xp)

    JT = CONV + FT
    RAW = CONV - 1

    with pre, nc.Block() as block:

        @block.tensor
        def _(pe):
            pe.wait_ge(loaded, 16 * 4)
            pe.wait_ge(pad_zero, 1)
            for t in range(TT):
                b, t0 = divmod(t * P, SEQ)
                last = nc.tensor.matmul(ps[:, 4, t * HEADS:(t + 1) * HEADS], xp[:, b, PADC + t0:PADC + t0 + P],
                                        w_in[:, 2 * DI + 2 * P:], start=True, stop=True)
            last.then_inc(dt_ready, 1)
            pe.wait_ge(taps_ready, TAPS)
            for c in range(NCH):
                b, t0 = divmod(c * CH, SEQ)
                for j in range(JT):
                    n = c * JT + j
                    if n >= 4:
                        pe.wait_ge(bank_read, n - 3)
                    if j == JT - 1:
                        for tap in range(TAPS):
                            off = PADC + t0 - (TAPS - 1) + tap
                            last = nc.tensor.matmul(ps[:, n % 4, :], w_tap[:, tap, :], xp[:, b, off:off + CH],
                                                    start=(tap == 0), stop=(tap == TAPS - 1))
                    else:
                        at = (FT + j) * P if j < RAW else (j - RAW) * P
                        last = nc.tensor.matmul(ps[:, n % 4, :], w_in[:, at:at + P],
                                                xp[:, b, PADC + t0:PADC + t0 + CH], start=True, stop=True)
                    last.then_inc(xz_ready, 1)

        @block.scalar
        def _(act):
            act.wait_ge(dt_step, 1)
            nc.scalar.activation(dt_log[:, :, :], dt[:, :, :], ACT.Abs).then_inc(dt_step, 1)
            act.wait_ge(dt_step, 2)
            nc.scalar.activation(dt_log[:, :, :], dt_log[:, :, :], ACT.Exp, scale=-1.0).then_inc(dt_step, 1)
            nc.scalar.activation(neg_a[:, :], head_rows[:, 1, :], ACT.Exp).then_inc(a_ready, 1)
            act.wait_ge(dt_step, 3)
            nc.scalar.activation(dt_log[:, :, :], dt_log[:, :, :], ACT.Ln, bias=1.0).then_inc(dt_step, 1)
            act.wait_ge(pad_zero, 2)

            def silu_conv(c):
                for j in range(RAW):
                    act.wait_ge(conv_step, (c * TAPS + TAPS - 1) * RAW + j + 1)
                    nc.scalar.activation(conv[:, j, cols(c)], conv[:, j, cols(c)], ACT.Silu,
                                         bias=k.vec[:, VB_CB + j:VB_CB + j + 1]).then_inc(silu_done, 1)

            for c in range(NCH):
                b, t0 = divmod(c * CH, SEQ)
                for j in range(JT):
                    n = c * JT + j
                    act.wait_ge(xz_ready, n + 1)
                    if j < RAW:
                        nc.scalar.activation(raw[:, j, b, PADC + t0:PADC + t0 + CH], ps[:, n % 4, :], ACT.Copy)\
                            .then_inc(bank_read, 1)
                    elif j < JT - 1:
                        nc.scalar.activation(sz[:, j - RAW, cols(c)], ps[:, n % 4, :], ACT.Silu).then_inc(bank_read, 1)
                    else:
                        nc.scalar.activation(conv[:, RAW, cols(c)], ps[:, n % 4, :], ACT.Silu,
                                             bias=k.vec[:, VB_CB + RAW:VB_CB + RAW + 1]).then_inc(bank_read, 1)
                if c:
                    silu_conv(c - 1)
            silu_conv(NCH - 1)

        @block.vector
        def _(dve):
            dve.wait_ge(loaded, 16 * 4)
            for tap in range(TAPS):
                nc.vector.tensor_tensor(w_tap[:, tap, :], w_in[:, DI + RAW * P:DI + CONV * P], taps[:, tap, :], ALU.mult)\
                    .then_inc(taps_ready, 1)
            dve.wait_ge(dt_ready, 1)
            nc.vector.tensor_tensor(dt[:, :, :], ps[:, 4, 0:TT * HEADS].rearrange("p (t h) -> p t h", h=HEADS),
                                    head_rows[:, 0, :].unsqueeze(1).to_broadcast([P, TT, HEADS]), ALU.add)\
                .then_inc(dt_step, 1)
            dve.wait_ge(dt_step, 4)
            nc.vector.scalar_tensor_tensor(out=dt[:, :, :], in0=dt[:, :, :], scalar=0.0, in1=dt_log[:, :, :],
                                           op0=ALU.max, op1=ALU.add).then_inc(dt_step, 1)
            dve.wait_ge(a_ready, 1)
            nc.vector.tensor_scalar(neg_a[:, :], neg_a[:, :], -1.0, None, ALU.mult).then_inc(a_ready, 1)
            dve.wait_ge(dt_step, 5)
            dve.wait_ge(a_ready, 2)
            nc.vector.tensor_tensor(dta[:, :, :], dt[:, :, :],
                                    neg_a[:, :].unsqueeze(1).to_broadcast([P, TT, HEADS]), ALU.mult)\
                .then_inc(dta_ready, 1)
            dve.wait_ge(pad_zero, 2)
            for c in range(NCH):
                b, t0 = divmod(c * CH, SEQ)
                for tap in range(TAPS):
                    off = PADC + t0 - (TAPS - 1) + tap
                    for j in range(RAW):
                        src, to = raw[:, j, b, off:off + CH], conv[:, j, cols(c)]
                        w = k.vec[:, VB_TAPS + j * TAPS + tap:VB_TAPS + j * TAPS + tap + 1]
                        if tap == 0:
                            dve.wait_ge(bank_read, c * JT + j + 1)
                            nc.vector.tensor_scalar(to, src, w, None, ALU.mult).then_inc(conv_step, 1)
                        else:
                            dve.wait_ge(conv_step, (c * TAPS + tap - 1) * RAW + j + 1)
                            nc.vector.scalar_tensor_tensor(out=to, in0=src, scalar=w, in1=to, op0=ALU.mult,
                                                           op1=ALU.add).then_inc(conv_step, 1)

    ssd = ExitStack()
    one = sb("one", [P, P], ctx=ssd)
    masks = sb("masks", [P, 2, P], ctx=ssd)
    steps = sb("steps", [P, 2, HEADS, P], ctx=ssd)
    decay = sb("decay", [P, 2, HEADS, P], ctx=ssd)
    into = sb("into", [P, 2, HEADS, P], ctx=ssd)
    toks = sb("toks", [P, 2, 3 * P], ctx=ssd)
    gram = sb("gram", [P, 2, P], ctx=ssd)
    mix = sb("mix", [P, 2, HEADS, P], ctx=ssd)
    c_in = sb("c_in", [P, 2, HEADS, P], ctx=ssd)
    x_dt = sb("x_dt", [P, 2, HEADS, HD], ctx=ssd)
    x_end = sb("x_end", [P, 2, HEADS, HD], ctx=ssd)
    state = sb("state", [P, 2, HEADS, HD], ctx=ssd)
    kept = sb("kept", [P, HEADS, HD], ctx=ssd)
    D, E, F, TR, Y, S = 0, 1, 2, 3, 4, 6
    PER_SEQ = SEQ // P
    masks_loaded, one_set, steps_ready, d_ready, e_ready, f_ready, tr_ready, decay_ready, into_ready, toks_ready, \
        gram_ready, mix_ready, c_in_ready, x_dt_ready, x_end_ready, y_summed, ds_ready, kept_ready, state_ready, \
        yd_ready, yz_ready = [sem(n) for n in (
            "masks_loaded one_set steps_ready d_ready e_ready f_ready tr_ready decay_ready into_ready toks_ready "
            "gram_ready mix_ready c_in_ready x_dt_ready x_end_ready y_summed ds_ready kept_ready state_ready "
            "yd_ready yz_ready").split()]

    with ssd, nc.Block() as block:

        @block.sync
        def _(sp):
            sp.dma_start(masks[:, :, :], d["masks"]).then_inc(masks_loaded, 16)

        @block.tensor
        def _(pe):
            def chunk_inputs(c):
                ts = slice(c * P, (c + 1) * P)
                pe.wait_ge(steps_ready, c + 1)
                if c >= 1:
                    pe.wait_ge(decay_ready, c)
                    pe.wait_ge(into_ready, c)
                    pe.wait_ge(gram_ready, c)
                    pe.wait_ge(toks_ready, c)
                nc.tensor.matmul(ps[:, F, 0:P], bT[:, ts], cT[:, ts], start=True, stop=True).then_inc(f_ready, 1)
                nc.tensor.matmul(ps[:, D, :], masks[:, 1, :], steps[:, c % 2, :, :].rearrange("p h i -> p (h i)"),
                                 start=True, stop=True).then_inc(d_ready, 1)
                nc.tensor.transpose(ps[:, TR, 0:P], xs[:, 0, ts], k.eye[:, :])
                nc.tensor.transpose(ps[:, TR, P:2 * P], xs[:, 1, ts], k.eye[:, :])
                nc.tensor.transpose(ps[:, TR, 2 * P:3 * P], bT[:, ts], k.eye[:, :]).then_inc(tr_ready, 1)
                nc.tensor.matmul(ps[:, E, :], one[:, :], steps[:, c % 2, :, :].rearrange("p h i -> p (h i)"),
                                 start=True, stop=True).then_inc(e_ready, 1)

            def chunk_outputs(c):
                if c % 4 == 0 and c:
                    pe.wait_ge(yd_ready, c // 4 * FT)
                pe.wait_ge(x_dt_ready, c + 1)
                pe.wait_ge(mix_ready, c + 1)
                pe.wait_ge(c_in_ready, c + 1)
                pe.wait_ge(state_ready, c + 1)
                for h in range(HEADS):
                    out = ps[HD * (h % 2):HD * (h % 2) + HD, Y + h // 2, (c % 4) * P:(c % 4 + 1) * P]
                    nc.tensor.matmul(out, x_dt[:, c % 2, h, :], mix[:, c % 2, h, :], start=True, stop=False)
                    last = nc.tensor.matmul(out, state[:, c % 2, h, :], c_in[:, c % 2, h, :], start=False, stop=True)
                last.then_inc(y_summed, 1)
                pe.wait_ge(x_end_ready, c + 1)
                nc.tensor.matmul(ps[:, S, 0:HEADS * HD], toks[:, c % 2, 2 * P:3 * P],
                                 x_end[:, c % 2, :, :].rearrange("p h q -> p (h q)"), start=True, stop=True)\
                    .then_inc(ds_ready, 1)

            pe.wait_ge(one_set, 1)
            pe.wait_ge(masks_loaded, 16)
            chunk_inputs(0)
            for c in range(TT):
                if c + 1 < TT:
                    chunk_inputs(c + 1)
                chunk_outputs(c)

        @block.scalar
        def _(act):
            for c in range(TT):
                if c >= 2:
                    act.wait_ge(ds_ready, c - 1)
                    act.wait_ge(kept_ready, c - 1)
                act.wait_ge(d_ready, c + 1)
                nc.scalar.activation(decay[:, c % 2, :, :].rearrange("p h i -> p (h i)"), ps[:, D, :], ACT.Exp)\
                    .then_inc(decay_ready, 1)
                act.wait_ge(tr_ready, c + 1)
                nc.scalar.activation(toks[:, c % 2, :], ps[:, TR, 0:3 * P], ACT.Copy).then_inc(toks_ready, 1)
                act.wait_ge(e_ready, c + 1)
                nc.scalar.activation(into[:, c % 2, :, :].rearrange("p h i -> p (h i)"), ps[:, E, :], ACT.Exp)\
                    .then_inc(into_ready, 1)

        @block.gpsimd
        def _(pool):
            def make_steps(c):
                if c >= 2:
                    pool.wait_ge(e_ready, c - 1)
                nc.gpsimd.tensor_tensor(steps[:, c % 2, :, :], masks[:, 0, :].unsqueeze(1).to_broadcast([P, HEADS, P]),
                                        dta[:, c, :].unsqueeze(2).to_broadcast([P, HEADS, P]), ALU.mult)\
                    .then_inc(steps_ready, 1)

            nc.gpsimd.memset(one[:, :], 1.0).then_inc(one_set, 1)
            pool.wait_ge(masks_loaded, 16)
            make_steps(0)
            for c in range(TT):
                if c + 1 < TT:
                    make_steps(c + 1)
                if c >= 2:
                    pool.wait_ge(ds_ready, c - 1)
                pool.wait_ge(toks_ready, c + 1)
                nc.gpsimd.tensor_tensor(x_dt[:, c % 2, :, :],
                                        toks[:, c % 2, 0:2 * P].rearrange("p (h q) -> p h q", h=HEADS),
                                        dt[:, c, :].unsqueeze(2).to_broadcast([P, HEADS, HD]), ALU.mult)\
                    .then_inc(x_dt_ready, 1)
                pool.wait_ge(x_dt_ready, c + 1)
                pool.wait_ge(decay_ready, c + 1)
                nc.gpsimd.tensor_tensor(x_end[:, c % 2, :, :], x_dt[:, c % 2, :, :],
                                        decay[:, c % 2, :, P - 1:P].to_broadcast([P, HEADS, HD]), ALU.mult)\
                    .then_inc(x_end_ready, 1)

        @block.vector
        def _(dve):
            nc.vector.memset(state[:, 0, :, :], 0.0).then_inc(state_ready, 1)
            dve.wait_ge(masks_loaded, 16)

            def prepare(c):
                ts = slice(c * P, (c + 1) * P)
                dve.wait_ge(f_ready, c + 1)
                if c >= 2:
                    dve.wait_ge(y_summed, c - 1)
                    dve.wait_ge(mix_ready, c - 1)
                nc.vector.tensor_tensor(gram[:, c % 2, :], ps[:, F, 0:P], masks[:, 0, :], ALU.mult)\
                    .then_inc(gram_ready, 1)
                dve.wait_ge(decay_ready, c + 1)
                dve.wait_ge(gram_ready, c + 1)
                nc.vector.tensor_tensor(mix[:, c % 2, :, :], decay[:, c % 2, :, :],
                                        gram[:, c % 2, :].unsqueeze(1).to_broadcast([P, HEADS, P]), ALU.mult)\
                    .then_inc(mix_ready, 1)
                dve.wait_ge(into_ready, c + 1)
                nc.vector.tensor_tensor(c_in[:, c % 2, :, :], into[:, c % 2, :, :],
                                        cT[:, ts].unsqueeze(1).to_broadcast([P, HEADS, P]), ALU.mult)\
                    .then_inc(c_in_ready, 1)

            prepare(0)
            for c in range(TT):
                if c + 1 < TT:
                    prepare(c + 1)
                    if c >= 1:
                        dve.wait_ge(y_summed, c)
                    if (c + 1) % PER_SEQ == 0:
                        nc.vector.memset(kept[:, :, :], 0.0).then_inc(kept_ready, 1)
                        dve.wait_ge(kept_ready, c + 1)
                        nc.vector.memset(state[:, (c + 1) % 2, :, :], 0.0).then_inc(state_ready, 1)
                    else:
                        dve.wait_ge(state_ready, c + 1)
                        nc.vector.tensor_tensor(kept[:, :, :], state[:, c % 2, :, :],
                                                into[:, c % 2, :, P - 1:P].to_broadcast([P, HEADS, HD]), ALU.mult)\
                            .then_inc(kept_ready, 1)
                        dve.wait_ge(kept_ready, c + 1)
                        dve.wait_ge(ds_ready, c + 1)
                        nc.vector.tensor_tensor(state[:, (c + 1) % 2, :, :], kept[:, :, :],
                                                ps[:, S, 0:HEADS * HD].rearrange("p (h q) -> p h q", h=HEADS), ALU.add)\
                            .then_inc(state_ready, 1)
                if c % 4 == 3:
                    g = c // 4
                    dve.wait_ge(y_summed, c + 1)
                    for f in range(FT):
                        nc.vector.scalar_tensor_tensor(out=y[:, f, cols(g)], in0=xs[:, f, cols(g)],
                                                       scalar=k.vec[:, VB_D + f:VB_D + f + 1], in1=ps[:, Y + f, :],
                                                       op0=ALU.mult, op1=ALU.add).then_inc(yd_ready, 1)
                    for f in range(FT):
                        dve.wait_ge(yd_ready, g * FT + f + 1)
                        nc.vector.tensor_tensor(y[:, f, cols(g)], y[:, f, cols(g)], sz[:, f, cols(g)], ALU.mult)\
                            .then_inc(yz_ready, 1)

    post = ExitStack()
    sq = sb("sq", [P, FT, T], ctx=post)
    rs = sb("rs", [P, T], ctx=post)
    squared, ms_ready, log_done, rms_ready, scaled, out_ready, res_done = [sem(n) for n in (
        "squared ms_ready log_done rms_ready scaled out_ready res_done").split()]

    with post, nc.Block() as block:

        @block.tensor
        def _(pe):
            for c in range(NCH):
                for f in range(FT):
                    pe.wait_ge(squared, c * FT + f + 1)
                    last = nc.tensor.matmul(ps[:, c, :], k.ones[:, :], sq[:, f, cols(c)],
                                            start=(f == 0), stop=(f == FT - 1))
                last.then_inc(ms_ready, 1)
            for c in range(NCH):
                for f in range(FT):
                    pe.wait_ge(scaled, c * FT + f + 1)
                    last = nc.tensor.matmul(ps[:, 4 + c, :], w_out[:, f, :], y[:, f, cols(c)],
                                            start=(f == 0), stop=(f == FT - 1))
                last.then_inc(out_ready, 1)

        @block.scalar
        def _(act):
            for c in range(NCH):
                for f in range(FT):
                    nc.scalar.activation(sq[:, f, cols(c)], y[:, f, cols(c)], ACT.Square).then_inc(squared, 1)
            for c in range(NCH):
                act.wait_ge(ms_ready, c + 1)
                nc.scalar.activation(rs[:, cols(c)], ps[:, c, :], ACT.Ln, bias=k.eps6[:, 0:1], scale=P / DI)\
                    .then_inc(log_done, 1)
            for c in range(NCH):
                act.wait_ge(log_done, NCH)
                nc.scalar.activation(rs[:, cols(c)], rs[:, cols(c)], ACT.Exp, scale=-0.5).then_inc(rms_ready, 1)

        @block.vector
        def _(dve):
            for c in range(NCH):
                dve.wait_ge(rms_ready, c + 1)
                for f in range(FT):
                    nc.vector.scalar_tensor_tensor(out=y[:, f, cols(c)], in0=y[:, f, cols(c)],
                                                   scalar=k.vec[:, VB_SSM + f:VB_SSM + f + 1], in1=rs[:, cols(c)],
                                                   op0=ALU.mult, op1=ALU.mult).then_inc(scaled, 1)
            for c in range(NCH):
                dve.wait_ge(out_ready, c + 1)
                nc.vector.tensor_tensor(k.xn[:, cols(c)], k.xn[:, cols(c)], ps[:, 4 + c, :], ALU.add)\
                    .then_inc(res_done, 1)

    mlp_in = conv[:, 0, :]
    x_hi, x_lo = [sb(n, [P, T], F32R) for n in ("x_hi", "x_lo")]
    norm_stage(k, "nm", None, k.xn, False, None, weight=k.vec[:, VB_POST:VB_POST + 1], rms_eps=k.eps6,
               out=mlp_in, split=(x_hi, x_lo))
    mlp = ExitStack()
    WC = 3 * MT * P
    raw = sb("raw", [P, WC], ctx=mlp)
    w_hi, w_lo = sb("w_hi", [P, WC], F32R, ctx=mlp), sb("w_lo", [P, WC], F32R, ctx=mlp)
    gate, prod = sb("gate", [P, 2, CH], ctx=mlp), sb("prod", [P, 2, CH], ctx=mlp)
    p_hi, p_lo = sb("p_hi", [P, 4, CH], F32R, ctx=mlp), sb("p_lo", [P, 4, CH], F32R, ctx=mlp)
    total = sb("total", [P, 2, CH], ctx=mlp)
    G, U, O = 0, 2, 4
    raw_loaded, w_high, w_ready, g_ready, u_ready, gate_done, prod_done, high_ready, low_ready, tile_summed, \
        total_ready, x_added = [sem("mlp_" + n) for n in (
            "raw_loaded w_high w_ready g_ready u_ready gate_done prod_done high_ready low_ready tile_summed "
            "total_ready x_added").split()]

    with stage, mlp, nc.Block() as block:

        @block.sync
        def _(sp):
            sp.dma_start(raw[:, 0:2 * MT * P], d["w_guB"]).then_inc(raw_loaded, 16)
            sp.dma_start(raw[:, 2 * MT * P:], d["w_dnB"]).then_inc(raw_loaded, 16)

        @block.gpsimd
        def _(pool):
            pool.wait_ge(raw_loaded, 32)
            nc.gpsimd.tensor_copy(w_hi[:, :], raw[:, :]).then_inc(w_high, 1)
            pool.wait_ge(w_high, 1)
            nc.gpsimd.tensor_tensor(w_lo[:, :], raw[:, :], w_hi[:, :].bitcast(F32), ALU.subtract).then_inc(w_ready, 1)

        @block.tensor
        def _(pe):
            def product(out, a, v_hi, v_lo, start, stop):
                nc.tensor.matmul(out, w_hi[:, a:a + P], v_hi, start=start, stop=False)
                nc.tensor.matmul(out, w_hi[:, a:a + P], v_lo, start=False, stop=False)
                return nc.tensor.matmul(out, w_lo[:, a:a + P], v_hi, start=False, stop=stop)

            def down(q):
                c, i = divmod(q, MT)
                if i == 0 and c >= 2:
                    pe.wait_ge(total_ready, c - 1)
                pe.wait_ge(low_ready, q + 1)
                product(ps[:, O + c % 2, :], (2 * MT + i) * P, p_hi[:, q % 4, :], p_lo[:, q % 4, :],
                        i == 0, i == MT - 1).then_inc(tile_summed, 1)

            pe.wait_ge(w_ready, 1)
            for q in range(NCH * MT):
                c, i = divmod(q, MT)
                if q >= 2:
                    pe.wait_ge(prod_done, q - 1)
                xh, xl = x_hi[:, cols(c)], x_lo[:, cols(c)]
                product(ps[:, G + q % 2, :], i * P, xh, xl, True, True).then_inc(g_ready, 1)
                product(ps[:, U + q % 2, :], (MT + i) * P, xh, xl, True, True).then_inc(u_ready, 1)
                if q >= 2:
                    down(q - 2)
            down(NCH * MT - 2)
            down(NCH * MT - 1)

        @block.scalar
        def _(act):
            def high(q):
                act.wait_ge(prod_done, q + 1)
                if q >= 4:
                    act.wait_ge(tile_summed, q - 3)
                nc.scalar.activation(p_hi[:, q % 4, :], prod[:, q % 2, :], ACT.Copy).then_inc(high_ready, 1)

            for q in range(NCH * MT):
                act.wait_ge(g_ready, q + 1)
                nc.scalar.activation(gate[:, q % 2, :], ps[:, G + q % 2, :], ACT.Silu).then_inc(gate_done, 1)
                if q:
                    high(q - 1)
            high(NCH * MT - 1)

        @block.vector
        def _(dve):
            def low(q):
                dve.wait_ge(high_ready, q + 1)
                nc.vector.tensor_tensor(p_lo[:, q % 4, :], prod[:, q % 2, :], p_hi[:, q % 4, :].bitcast(F32),
                                        ALU.subtract).then_inc(low_ready, 1)

            def finish(c):
                dve.wait_ge(tile_summed, (c + 1) * MT)
                if c >= 2:
                    dve.wait_ge(x_added, c - 1)
                nc.vector.tensor_tensor(total[:, c % 2, :], ps[:, O + c % 2, :], k.xn[:, cols(c)], ALU.add)\
                    .then_inc(total_ready, 1)
                dve.wait_ge(total_ready, c + 1)
                nc.vector.tensor_tensor(k.x[:, cols(c)], k.x[:, cols(c)], total[:, c % 2, :], ALU.add)\
                    .then_inc(x_added, 1)

            for q in range(NCH * MT):
                dve.wait_ge(gate_done, q + 1)
                dve.wait_ge(u_ready, q + 1)
                if q >= 2:
                    dve.wait_ge(low_ready, q - 1)
                nc.vector.tensor_tensor(prod[:, q % 2, :], gate[:, q % 2, :], ps[:, U + q % 2, :], ALU.mult)\
                    .then_inc(prod_done, 1)
                if q:
                    low(q - 1)
                if q % MT == 2 and q > MT:
                    finish(q // MT - 1)
            low(NCH * MT - 1)
            finish(NCH - 1)


def store_stage(k, out):
    nc = k.nc
    stored = k.sem("stored")
    with nc.Block() as block:

        @block.sync
        def _(sp):
            sp.dma_start(out, k.x[:, :]).then_inc(stored, 16)
            sp.wait_ge(stored, 16)


def build(nc, d, out, stages=4):
    ctx = ExitStack()
    with ctx:
        k = Core(nc, ctx)
        load_stage(k, d)
        mixer_a_stage(k, d)
        if stages > 1:
            ffn_stage(k, d, 0, "f")
        if stages > 2:
            mixer_b_stage(k, d)
        if stages > 3:
            ffn_stage(k, d, 1, "g")
        store_stage(k, out)


def layout(i):
    a = lambda n: np.asarray(i[n])
    col = lambda v: a(v).reshape(-1, P).T
    vec = [col("L0_attn_a_norm_w"), col("L0_attn_a_conv_b"), col("L0_attn_a_dt_proj_b"), col("L0_attn_a_D"),
           a("L0_attn_a_A_log").reshape(FT, P, NST).transpose(1, 0, 2).reshape(P, FT * NST),
           col("L0_attn_b_norm_w"), col("L0_attn_b_post_norm_w"), col("L0_attn_b_ssm_norm_w"),
           col("L0_attn_b_conv_b"), np.repeat(a("L0_attn_b_D"), 64).reshape(FT, P).T,
           a("L0_attn_a_conv_w").reshape(FT, P, TAPS).transpose(1, 0, 2).reshape(P, FT * TAPS),
           a("L0_attn_b_conv_w").reshape(4, P, TAPS).transpose(1, 0, 2).reshape(P, 4 * TAPS)]
    xw = a("L0_attn_a_x_proj_w")
    order = np.concatenate([xw[RANK:], xw[:RANK]])
    m = {
        "xT": a("L0_attn_a_x").reshape(T, P).T,
        "vec": np.concatenate(vec, axis=1),
        "eye": np.eye(P, dtype=np.float32),
        "tapsA": a("L0_attn_a_conv_w")[P:, 0, :].T.reshape(TAPS * P),
        "w_inA": a("L0_attn_a_in_proj_w").T,
        "w_xA": order.T.reshape(FT, P, 40).transpose(1, 0, 2),
        "w_dtA": a("L0_attn_a_dt_proj_w").T,
        "w_outA": a("L0_attn_a_out_proj_w").T.reshape(FT, P, P).transpose(1, 0, 2),
    }
    w = a("L0_attn_b_in_proj_w")
    m["w_inB"] = w.T
    m["tapsB"] = a("L0_attn_b_conv_w")[3 * P:].T.reshape(TAPS * P)
    m["headsB"] = np.concatenate([a("L0_attn_b_dt_bias"), a("L0_attn_b_A_log")])
    m["w_outB"] = a("L0_attn_b_out_proj_w").T.reshape(FT, P, P).transpose(1, 0, 2)
    m["masks"] = np.stack([np.triu(np.ones((P, P), np.float32)), np.tril(np.ones((P, P), np.float32), -1)], axis=1)
    m["w_guB"] = np.concatenate([a("L0_attn_b_gate_w"), a("L0_attn_b_up_w")]).T
    m["w_dnB"] = a("L0_attn_b_down_w").T.reshape(3, P, P).transpose(1, 0, 2).reshape(P, 3 * P)
    gu = np.concatenate([a("L0_ffn_shared_gate_up")[None], a("L0_ffn_experts_gate_up")])
    full = NI * P
    m["gu_shared"] = np.concatenate([gu[0, :full], gu[0, INTER:INTER + full], gu[0, full:INTER],
                                     gu[0, INTER + full:]]).T
    w0 = HALVES[0]
    m["gu"] = np.concatenate([gu[1:, :w0], gu[1:, INTER:INTER + w0], gu[1:, w0:INTER], gu[1:, INTER + w0:]], axis=1)\
        .transpose(0, 2, 1)
    m["dn"] = np.concatenate([a("L0_ffn_shared_down")[None], a("L0_ffn_experts_down")]).transpose(0, 2, 1)
    m["w_gateF"] = a("L0_ffn_gate_weight").T
    more = np.arange(TT) * P
    more[0] = -1
    place = (np.arange(EXPERTS) + 1) % RING
    m["fc"] = np.concatenate([np.arange(EXPERTS, 0, -1), more, np.arange(SLOT_TILES), np.diff(place)])\
        .astype(np.float32)
    m["places"] = (np.arange(TOP * TT) * P + np.arange(P)[:, None]).astype(np.int32)
    m["slots"] = np.zeros((SLOT_TILES * P, ROW), np.float32)
    m["slots"].view(np.int32)[:, P] = TOP * T + np.arange(SLOT_TILES * P)
    return {n: np.ascontiguousarray(v) for n, v in m.items()}


def kernel(**inputs):
    import concourse.bacc as bacc
    from concourse.bass_utils import run_bass_kernel_spmd

    nc = bacc.Bacc("TRN2", target_bir_lowering=False, num_devices=1)
    arrays = layout(inputs)
    d = {n: nc.dram_tensor("in_" + n, v.shape, mybir.dt.from_np(v.dtype), kind="ExternalInput").ap()
         for n, v in arrays.items()}
    out = nc.dram_tensor("out", (P, T), F32, kind="ExternalOutput").ap()
    build(nc, d, out)
    r = run_bass_kernel_spmd(nc, [{"in_" + n: v for n, v in arrays.items()}], core_ids=[0])
    return r.results[0]["out"].T.reshape(BATCH, SEQ, P)
```

```python
from contextlib import ExitStack

import numpy as np

import concourse.bass as bass
from concourse import mybir

F32 = mybir.dt.float32
F32R = mybir.dt.float32r
I32 = mybir.dt.int32
ALU = mybir.AluOpType
ACT = mybir.ActivationFunctionType
AX = mybir.AxisListType

P = 128
BATCH, SEQ = 2, 1024
T = BATCH * SEQ
CH = 512
NCH = T // CH
DI = 256
FT = DI // P
TAPS = 4
NST = 16
RANK = 8
PADC = 4
PADDED = SEQ + PADC
EXPERTS = 8
INTER = 938
NI = 7
TAIL = INTER - NI * P
UT = 64
GU = 2 * NI * P + UT + TAIL
TOP = 2
TT = T // P
TILES = NI + 1
RING = 4
SLOT_TILES = (TOP * T + EXPERTS * (P - 1)) // P
ROW = P + 2
HALVES = (INTER // 2 + 1, INTER // 2 - 1)
EARLY = 3
NFC = EXPERTS + TT + SLOT_TILES + EXPERTS - 1

VA_NORM, VA_CB, VA_DTB, VA_D, VA_ALOG = 0, 1, 3, 5, 7
VB_NORM, VB_POST, VB_SSM, VB_CB, VB_D = 39, 40, 41, 43, 47
VA_TAPS, VB_TAPS = 49, 57
NV = 73


class Core:

    def __init__(self, nc, ctx):
        self.nc, self.ctx = nc, ctx

    def sb(self, name, shape, dt=F32, ctx=None):
        return (ctx or self.ctx).enter_context(self.nc.sbuf_tensor(name, shape, dt))

    def sem(self, name, ctx=None):
        return (ctx or self.ctx).enter_context(self.nc.semaphore(name))


def cols(c):
    return slice(c * CH, (c + 1) * CH)


def load_stage(k, d):
    nc = k.nc
    k.x = k.sb("x", [P, T])
    k.xn = k.sb("xn", [P, T])
    k.vec = k.sb("vec", [P, NV])
    k.ones = k.sb("ones", [P, P])
    k.eye = k.sb("eye", [P, P])
    k.eps5 = k.sb("eps5", [P, 1])
    k.eps6 = k.sb("eps6", [P, 1])
    k.ps = k.ctx.enter_context(nc.psum_tensor("ps", [P, 8, CH], F32))
    k.x_loaded = [k.sem(f"x_loaded{c}") for c in range(NCH)]
    k.vec_loaded = k.sem("vec_loaded")
    k.eye_loaded = k.sem("eye_loaded")
    k.masks = k.sb("masks", [P, 2, P])
    k.fc = k.sb("fc", [P, NFC])
    k.places = k.sb("places", [P, TOP * TT], I32)
    k.slot_rows = [nc.dram_tensor(f"slot_rows{i}", (SLOT_TILES * P, ROW), F32, kind="Internal").ap() for i in range(2)]
    k.token_rows = nc.dram_tensor("token_rows", ((TOP * T + SLOT_TILES * P), P), F32, kind="Internal").ap()
    k.slots_filled = k.sem("slots_filled")
    k.rows_sent, k.outputs_sent = k.sem("rows_sent"), k.sem("outputs_sent")
    k.raw_gu = k.sb("raw_gu", [P, 2, GU])
    k.raw_dn = k.sb("raw_dn", [P, 2, TILES, P])
    k.raw_loaded = [k.sem("raw_loaded0"), k.sem("raw_loaded1")]
    k.raw_zero = k.sem("raw_zero")
    k.late_loaded = [k.sem("late_loaded0"), k.sem("late_loaded1")]
    consts_set = k.sem("consts_set")
    with nc.Block() as block:

        @block.sync
        def _(sp):
            for c in range(NCH):
                sp.dma_start(k.x[:, cols(c)], d["xT"][:, cols(c)]).then_inc(k.x_loaded[c], 16)
            sp.dma_start(k.vec[:, :], d["vec"]).then_inc(k.vec_loaded, 16)
            sp.dma_start(k.eye[:, :], d["eye"]).then_inc(k.eye_loaded, 16)
            sp.dma_start(k.fc[:, :], d["fc"].partition_broadcast(P)).then_inc(k.eye_loaded, 16)
            sp.dma_start(k.places[:, :], d["places"]).then_inc(k.eye_loaded, 16)
            sp.dma_start(k.masks[:, :, :], d["masks"]).then_inc(k.eye_loaded, 16)

        @block.gpsimd
        def _(pool):
            nc.gpsimd.memset(k.raw_gu[:, 1, 2 * INTER:GU], 0.0).then_inc(k.raw_zero, 1)
            nc.gpsimd.memset(k.raw_dn[:, :, NI, :], 0.0).then_inc(k.raw_zero, 1)
            zero_gap(k)

        @block.vector
        def _(dve):
            nc.vector.memset(k.ones[:, :], 1.0 / P)
            nc.vector.memset(k.eps5[:, :], 1e-5)
            nc.vector.memset(k.eps6[:, :], 1e-6).then_inc(consts_set, 1)


def zero_gap(k):
    k.nc.gpsimd.memset(k.raw_gu[:, 0, GU - UT:GU - TAIL], 0.0).then_inc(k.raw_zero, 1)


def norm_stage(k, tag, src, dst, center, eps, weight=None, rms_eps=None, out=None, split=None,
               sync_part=None, pool_part=None, tensor_part=None):
    nc = k.nc
    stage = ExitStack()
    sq = k.sb(tag + "_sq", [P, T], ctx=stage)
    rs = k.sb(tag + "_rs", [P, T], ctx=stage)
    mean_ready, centred, squared, var_ready, rstd_ready, normed, squared2, ms_ready, rms_ready, scaled, \
        high_ready, low_ready, log_done = [k.sem(f"{tag}_{n}", stage) for n in (
            "mean_ready centred squared var_ready rstd_ready normed squared2 ms_ready rms_ready scaled "
            "high_ready low_ready log_done").split()]
    final = out if out is not None else dst

    with stage, nc.Block() as block:
        if sync_part is not None:
            @block.sync
            def _(sp):
                sync_part(sp)

            @block.gpsimd
            def _(pool):
                pool_part(pool)

        @block.tensor
        def _(pe):
            if center:
                for c in range(NCH):
                    pe.wait_ge(k.x_loaded[c], 16)
                    nc.tensor.matmul(k.ps[:, c, :], k.ones[:, :], src[:, cols(c)], start=True, stop=True)\
                        .then_inc(mean_ready, 1)
                for c in range(NCH):
                    pe.wait_ge(squared, c + 1)
                    nc.tensor.matmul(k.ps[:, 4 + c, :], k.ones[:, :], sq[:, cols(c)], start=True, stop=True)\
                        .then_inc(var_ready, 1)
            if rms_eps is not None:
                for c in range(NCH):
                    pe.wait_ge(squared2, c + 1)
                    nc.tensor.matmul(k.ps[:, c, :], k.ones[:, :], sq[:, cols(c)], start=True, stop=True)\
                        .then_inc(ms_ready, 1)
            if tensor_part is not None:
                pe.wait_ge(log_done, NCH)
                for c in range(NCH):
                    pe.wait_ge(normed, c + 1)
                    tensor_part(pe, c)

        @block.scalar
        def _(act):
            if center:
                for c in range(NCH):
                    act.wait_ge(centred, c + 1)
                    nc.scalar.activation(sq[:, cols(c)], dst[:, cols(c)], ACT.Square).then_inc(squared, 1)
                for c in range(NCH):
                    act.wait_ge(var_ready, c + 1)
                    nc.scalar.activation(rs[:, cols(c)], k.ps[:, 4 + c, :], ACT.Ln, bias=eps[:, 0:1])\
                        .then_inc(log_done, 1)
                for c in range(NCH):
                    act.wait_ge(log_done, NCH)
                    nc.scalar.activation(rs[:, cols(c)], rs[:, cols(c)], ACT.Exp, scale=-0.5)\
                        .then_inc(rstd_ready, 1)
            if rms_eps is not None:
                for c in range(NCH):
                    if center:
                        act.wait_ge(normed, c + 1)
                    nc.scalar.activation(sq[:, cols(c)], dst[:, cols(c)], ACT.Square).then_inc(squared2, 1)
                for c in range(NCH):
                    act.wait_ge(ms_ready, c + 1)
                    nc.scalar.activation(rs[:, cols(c)], k.ps[:, c, :], ACT.Ln, bias=rms_eps[:, 0:1])\
                        .then_inc(log_done, 1)
                for c in range(NCH):
                    act.wait_ge(log_done, NCH * (2 if center else 1))
                    nc.scalar.activation(rs[:, cols(c)], rs[:, cols(c)], ACT.Exp, scale=-0.5)\
                        .then_inc(rms_ready, 1)
            if split:
                for c in range(NCH):
                    act.wait_ge(scaled if rms_eps is not None else normed, c + 1)
                    nc.scalar.activation(split[0][:, cols(c)], final[:, cols(c)], ACT.Copy).then_inc(high_ready, 1)

        @block.vector
        def _(dve):
            if center:
                for c in range(NCH):
                    dve.wait_ge(mean_ready, c + 1)
                    nc.vector.tensor_tensor(dst[:, cols(c)], src[:, cols(c)], k.ps[:, c, :], ALU.subtract)\
                        .then_inc(centred, 1)
                for c in range(NCH):
                    dve.wait_ge(rstd_ready, c + 1)
                    nc.vector.tensor_tensor(dst[:, cols(c)], dst[:, cols(c)], rs[:, cols(c)], ALU.mult)\
                        .then_inc(normed, 1)
            if rms_eps is not None:
                for c in range(NCH):
                    dve.wait_ge(rms_ready, c + 1)
                    where = out[:, cols(c)] if len(out.shape) == 2 else out[:, c // 2, PADC + (c % 2) * CH:
                                                                           PADC + (c % 2 + 1) * CH]
                    nc.vector.scalar_tensor_tensor(out=where, in0=dst[:, cols(c)], scalar=weight,
                                                   in1=rs[:, cols(c)], op0=ALU.mult, op1=ALU.mult)\
                        .then_inc(scaled, 1)
            if split:
                for c in range(NCH):
                    dve.wait_ge(high_ready, c + 1)
                    nc.vector.tensor_tensor(split[1][:, cols(c)], final[:, cols(c)],
                                            split[0][:, cols(c)].bitcast(F32), ALU.subtract).then_inc(low_ready, 1)

    with nc.Block() as block:

        @block.sync
        def _(sp):
            for used in (mean_ready, centred, squared, var_ready, rstd_ready, normed, squared2, ms_ready, rms_ready,
                         scaled, high_ready, low_ready, log_done):
                sp.sem_clear(used)


def mixer_a_stage(k, d):
    nc = k.nc
    stage = ExitStack()
    sb = lambda name, shape, dt=F32: k.sb("a_" + name, shape, dt, ctx=stage)
    sem = lambda name: k.sem("a_" + name)
    w_in = sb("w_in", [P, 2 * DI])
    w_tap = sb("w_tap", [P, TAPS, P])
    taps = sb("taps", [P, TAPS, P])
    raw = sb("raw", [P, BATCH, PADDED])
    w_x = sb("w_x", [P, FT, 40])
    w_dt = sb("w_dt", [40, DI])
    w_out = sb("w_out", [P, FT, P])
    xp = sb("xp", [P, BATCH, PADDED])
    neg_a = sb("neg_a", [P, FT, NST])
    u, sz, delta, du = [sb(n, [P, FT, T]) for n in ("u", "sz", "delta", "du")]
    sel = sb("sel", [64, 32, P], F32R)
    rows = sb("rows", [64, T], F32R)
    sel_set = sem("sel_set")
    dt_row = sb("dt_row", [40, T])
    ps = k.ps

    w_loaded, taps_loaded, pad_zero, taps_ready, xz_ready, bank_read, conv_step, u_ready, bc_ready, high_done, \
        rows_done, dt_ready, \
        pre_ready, abs_done, exp_done, log_done, delta_ready, du_ready, a_ready = [sem(n) for n in (
            "w_loaded taps_loaded pad_zero taps_ready xz_ready bank_read conv_step u_ready bc_ready high_done "
            "rows_done dt_ready "
            "pre_ready abs_done exp_done log_done delta_ready du_ready a_ready").split()]

    with nc.Block() as block:

        @block.sync
        def _(sp):
            sp.dma_start(taps[:, :, :].rearrange("p a b -> p (a b)"), d["tapsA"].partition_broadcast(P))\
                .then_inc(taps_loaded, 16)
            sp.dma_start(w_in[:, :], d["w_inA"]).then_inc(w_loaded, 16)
            sp.dma_start(w_x[:, :, :], d["w_xA"]).then_inc(w_loaded, 16)
            sp.dma_start(w_dt[32:40, :], d["w_dtA"]).then_inc(w_loaded, 16)
            sp.dma_start(w_out[:, :, :], d["w_outA"]).then_inc(w_loaded, 16)
            for scratch in k.slot_rows:
                sp.dma_start(scratch, d["slots"]).then_inc(k.slots_filled, 16)

        @block.gpsimd
        def _(pool):
            nc.gpsimd.memset(xp[:, :, 0:PADC], 0.0).then_inc(pad_zero, 1)
            nc.gpsimd.memset(raw[:, :, 0:PADC], 0.0).then_inc(pad_zero, 1)

        @block.vector
        def _(dve):
            dve.wait_ge(k.eye_loaded, 64)
            for half in range(2):
                src = k.eye[32 * half:32 * half + 32, 32 * half:32 * half + 32]
                nc.vector.tensor_copy(sel[32 * half:32 * half + 32, :, :],
                                      src.unsqueeze(2).to_broadcast([32, 32, P])).then_inc(sel_set, 1)

    norm_stage(k, "na", k.x, k.xn, True, k.eps5, weight=k.vec[:, VA_NORM:VA_NORM + 1], rms_eps=k.eps5, out=xp)

    with nc.Block() as block:

        @block.tensor
        def _(pe):
            pe.wait_ge(w_loaded, 16 * 4)
            pe.wait_ge(taps_ready, TAPS)
            pe.wait_ge(pad_zero, 2)

            def in_proj(c):
                b, t0 = divmod(c * CH, SEQ)
                for j in range(2 * FT):
                    n = c * 2 * FT + j
                    if n >= 4:
                        pe.wait_ge(bank_read, n - 3)
                    if j == 1:
                        for tap in range(TAPS):
                            off = PADC + t0 - (TAPS - 1) + tap
                            last = nc.tensor.matmul(ps[:, n % 4, :], w_tap[:, tap, :],
                                                    xp[:, b, off:off + CH], start=(tap == 0), stop=(tap == TAPS - 1))
                    else:
                        last = nc.tensor.matmul(ps[:, n % 4, :], w_in[:, j * P:(j + 1) * P],
                                                xp[:, b, PADC + t0:PADC + t0 + CH], start=True, stop=True)
                    last.then_inc(xz_ready, 1)

            def x_proj(c):
                pe.wait_ge(bank_read, c * 2 * FT + 2)
                pe.wait_ge(u_ready, c + 1)
                if c >= 1:
                    pe.wait_ge(rows_done, c)
                for f in range(FT):
                    last = nc.tensor.matmul(ps[0:40, 4, :], w_x[:, f, :], u[:, f, cols(c)],
                                            start=(f == 0), stop=(f == FT - 1))
                last.then_inc(bc_ready, 1)

            def dt_proj(c):
                pe.wait_ge(rows_done, c + 1)
                for f in range(FT):
                    n = c * FT + f
                    if n >= 2:
                        pe.wait_ge(pre_ready, n - 1)
                    nc.tensor.matmul(ps[:, 5 + n % 2, :], w_dt[32:40, f * P:(f + 1) * P],
                                     dt_row[32:40, cols(c)], start=True, stop=True).then_inc(dt_ready, 1)

            in_proj(0)
            for c in range(NCH):
                if c + 1 < NCH:
                    in_proj(c + 1)
                x_proj(c)
                dt_proj(c)

        @block.scalar
        def _(act):
            act.wait_ge(k.vec_loaded, 16)
            act.wait_ge(pad_zero, 2)
            for c in range(NCH):
                b, t0 = divmod(c * CH, SEQ)
                for j in range(2 * FT):
                    n = c * 2 * FT + j
                    act.wait_ge(xz_ready, n + 1)
                    if j == 0:
                        nc.scalar.activation(raw[:, b, PADC + t0:PADC + t0 + CH], ps[:, n % 4, :], ACT.Copy)\
                            .then_inc(bank_read, 1)
                    elif j < FT:
                        nc.scalar.activation(u[:, j, cols(c)], ps[:, n % 4, :], ACT.Silu,
                                             bias=k.vec[:, VA_CB + j:VA_CB + j + 1]).then_inc(bank_read, 1)
                    else:
                        nc.scalar.activation(sz[:, j - FT, cols(c)], ps[:, n % 4, :], ACT.Silu).then_inc(bank_read, 1)
                act.wait_ge(conv_step, (c + 1) * TAPS)
                nc.scalar.activation(u[:, 0, cols(c)], u[:, 0, cols(c)], ACT.Silu, bias=k.vec[:, VA_CB:VA_CB + 1])\
                    .then_inc(u_ready, 1)
            nc.scalar.activation(neg_a[:, :, :], k.vec[:, VA_ALOG:VA_ALOG + FT * NST]
                                 .rearrange("p (f n) -> p f n", f=FT), ACT.Exp).then_inc(a_ready, 1)
            for b in range(BATCH):
                at = slice(b * SEQ, (b + 1) * SEQ)
                act.wait_ge(pre_ready, (b + 1) * 2 * FT)
                for f in range(FT):
                    nc.scalar.activation(du[:, f, at], delta[:, f, at], ACT.Abs).then_inc(abs_done, 1)
                for f in range(FT):
                    act.wait_ge(abs_done, b * FT + f + 1)
                    nc.scalar.activation(du[:, f, at], du[:, f, at], ACT.Exp, scale=-1.0).then_inc(exp_done, 1)
                for f in range(FT):
                    act.wait_ge(exp_done, b * FT + f + 1)
                    nc.scalar.activation(du[:, f, at], du[:, f, at], ACT.Ln, bias=1.0).then_inc(log_done, 1)

        @block.vector
        def _(dve):
            dve.wait_ge(taps_loaded, 16)
            dve.wait_ge(w_loaded, 16 * 4)
            for tap in range(TAPS):
                nc.vector.tensor_tensor(w_tap[:, tap, :], w_in[:, P:DI], taps[:, tap, :], ALU.mult)\
                    .then_inc(taps_ready, 1)
            dve.wait_ge(k.vec_loaded, 16)
            dve.wait_ge(pad_zero, 2)

            def convolve(c):
                b, t0 = divmod(c * CH, SEQ)
                for tap in range(TAPS):
                    off = PADC + t0 - (TAPS - 1) + tap
                    src, to, w = raw[:, b, off:off + CH], u[:, 0, cols(c)], k.vec[:, VA_TAPS + tap:VA_TAPS + tap + 1]
                    if tap == 0:
                        dve.wait_ge(bank_read, c * 2 * FT + 1)
                        nc.vector.tensor_scalar(to, src, w, None, ALU.mult).then_inc(conv_step, 1)
                    else:
                        dve.wait_ge(conv_step, c * TAPS + tap)
                        nc.vector.scalar_tensor_tensor(out=to, in0=src, scalar=w, in1=to, op0=ALU.mult,
                                                       op1=ALU.add).then_inc(conv_step, 1)

            convolve(0)
            for c in range(NCH):
                if c + 1 < NCH:
                    convolve(c + 1)
                dve.wait_ge(bc_ready, c + 1)
                nc.vector.tensor_copy(rows[0:32, cols(c)], ps[0:32, 4, :]).then_inc(high_done, 1)
                nc.vector.tensor_copy(dt_row[32:40, cols(c)], ps[32:40, 4, :])
                dve.wait_ge(high_done, c + 1)
                nc.vector.tensor_tensor(rows[32:64, cols(c)], ps[0:32, 4, :],
                                        rows[0:32, cols(c)].bitcast(F32), ALU.subtract).then_inc(rows_done, 1)
                for f in range(FT):
                    n = c * FT + f
                    dve.wait_ge(dt_ready, n + 1)
                    nc.vector.tensor_scalar(delta[:, f, cols(c)], ps[:, 5 + n % 2, :],
                                            k.vec[:, VA_DTB + f:VA_DTB + f + 1], None, ALU.add).then_inc(pre_ready, 1)
            dve.wait_ge(a_ready, 1)
            nc.vector.tensor_scalar(neg_a[:, :, :], neg_a[:, :, :], -1.0, None, ALU.mult).then_inc(a_ready, 1)
            for b in range(BATCH):
                at = slice(b * SEQ, (b + 1) * SEQ)
                for f in range(FT):
                    n = b * FT + f + 1
                    dve.wait_ge(log_done, n)
                    nc.vector.scalar_tensor_tensor(out=delta[:, f, at], in0=delta[:, f, at], scalar=0.0,
                                                   in1=du[:, f, at], op0=ALU.max, op1=ALU.add).then_inc(delta_ready, 1)
                    dve.wait_ge(delta_ready, n)
                    nc.vector.tensor_tensor(du[:, f, at], delta[:, f, at], u[:, f, at], ALU.mult).then_inc(du_ready, 1)

    HALVES = SEQ // CH
    STEPS = NST * FT
    DEPTH = 4
    decayed_in = sb("b_u", [P, DEPTH, CH])
    h = sb("h", [P, DEPTH, CH])
    hc = sb("hc", [P, DEPTH, CH])
    c_sb = sb("c_sb", [P, 2, CH])
    state = sb("state", [P, STEPS])
    yz = sb("yz", [P, FT, CH])
    yd = sb("yd", [P, FT, CH])
    Y, B, C, A, O = 0, 2, 4, 5, 7
    b_ready, c_ready, c_copied, decay_ready, bu_ready, scanned, saved, hc_ready, y_added, y_ready, yd_ready, \
        yz_ready, out_ready, res_ready, x_added = [sem(n) for n in (
            "b_ready c_ready c_copied decay_ready bu_ready scanned saved hc_ready y_added y_ready yd_ready "
            "yz_ready out_ready res_ready x_added").split()]

    def at_half(b, half):
        return bass.ds(b * SEQ + half * CH, CH)

    with stage, nc.Block() as block:

        @block.sync
        def _(sp):
            sp.wait_ge(k.raw_zero, 3)
            load_weights(k, d, sp, 0)
            load_weights(k, d, sp, 1)

        @block.tensor
        def _(pe):
            def half_sequence(b, half):
                first = half == 0 and b == 0
                g = b * HALVES + half
                def broadcast(n):
                    m = g * NST + n
                    if not (first and n < 2):
                        pe.wait_ge(bu_ready, (m - 1) * FT)
                    nc.tensor.matmul(ps[:, B + n % 2, :], sel[:, n, :], rows[:, at_half(b, half)],
                                     start=True, stop=True).then_inc(b_ready, 1)
                    if not (first and n < 1):
                        pe.wait_ge(c_copied, m)
                    nc.tensor.matmul(ps[:, C, :], sel[:, NST + n, :], rows[:, at_half(b, half)],
                                     start=True, stop=True).then_inc(c_ready, 1)

                def accumulate(n):
                    for f in range(FT):
                        s = n * FT + f
                        pe.wait_ge(hc_ready, g * STEPS + s + 1)
                        if n == 0 and not first:
                            pe.wait_ge(yd_ready, (g - 1) * FT + f + 1)
                        nc.tensor.matmul(ps[:, Y + f, :], k.eye[:, :], hc[:, s % DEPTH, :],
                                         start=(n == 0), stop=(n == NST - 1)).then_inc(y_added, 1)

                broadcast(0)
                broadcast(1)
                for n in range(2, NST):
                    broadcast(n)
                    accumulate(n - 2)
                    if n == 4 and not first:
                        project(g - 1)
                accumulate(NST - 2)
                accumulate(NST - 1)

            def project(g):
                if g:
                    pe.wait_ge(res_ready, g)
                for f in range(FT):
                    pe.wait_ge(yz_ready, g * FT + f + 1)
                    last = nc.tensor.matmul(ps[:, O, :], w_out[:, f, :], yz[:, f, :], start=(f == 0), stop=(f == FT - 1))
                last.then_inc(out_ready, 1)

            for b in range(BATCH):
                for half in range(HALVES):
                    half_sequence(b, half)
            project(BATCH * HALVES - 1)

        @block.scalar
        def _(act):
            def half_sequence(b, half):
                first = half == 0 and b == 0
                g = b * HALVES + half
                for n in range(NST):
                    for f in range(FT):
                        s = n * FT + f
                        if not (first and s < 2):
                            act.wait_ge(scanned, g * STEPS + s - 1)
                        nc.scalar.activation(ps[:, A + s % 2, :], delta[:, f, at_half(b, half)], ACT.Exp,
                                             scale=neg_a[:, f, n:n + 1]).then_inc(decay_ready, 1)
                        if f == 0:
                            act.wait_ge(c_ready, g * NST + n + 1)
                            if not (first and n < 2):
                                act.wait_ge(hc_ready, g * STEPS + s - 2)
                            nc.scalar.activation(c_sb[:, n % 2, :], ps[:, C, :], ACT.Copy).then_inc(c_copied, 1)
                        if half + 1 < HALVES and s >= 1:
                            act.wait_ge(scanned, g * STEPS + s)
                            nc.scalar.activation(state[:, s - 1:s], h[:, (s - 1) % DEPTH, CH - 1:CH], ACT.Copy)\
                                .then_inc(saved, 1)
                if half + 1 < HALVES:
                    act.wait_ge(scanned, (g + 1) * STEPS)
                    nc.scalar.activation(state[:, STEPS - 1:STEPS], h[:, (STEPS - 1) % DEPTH, CH - 1:CH], ACT.Copy)\
                        .then_inc(saved, 1)

            for b in range(BATCH):
                for half in range(HALVES):
                    half_sequence(b, half)

        @block.vector
        def _(dve):
            def half_sequence(b, half):
                first = half == 0 and b == 0
                g = b * HALVES + half
                def times_b(s):
                    n, f = divmod(s, FT)
                    if f == 0:
                        dve.wait_ge(b_ready, g * NST + n + 1)
                    if not (first and s < DEPTH):
                        dve.wait_ge(scanned, g * STEPS + s - DEPTH + 1)
                    nc.vector.tensor_tensor(decayed_in[:, s % DEPTH, :], du[:, f, at_half(b, half)], ps[:, B + n % 2, :],
                                            ALU.mult).then_inc(bu_ready, 1)

                times_b(0)
                for s in range(STEPS):
                    if s + 1 < STEPS:
                        times_b(s + 1)
                    dve.wait_ge(decay_ready, g * STEPS + s + 1)
                    dve.wait_ge(bu_ready, g * STEPS + s + 1)
                    if not (first and s < DEPTH):
                        dve.wait_ge(hc_ready, g * STEPS + s - DEPTH + 1)
                    if half == 0 and s >= DEPTH:
                        dve.wait_ge(saved, b * STEPS + s - DEPTH + 1)
                    if half == 1:
                        dve.wait_ge(saved, b * STEPS + (STEPS if s < DEPTH else s + 1))
                    initial = state[:, s:s + 1] if half else 0.0
                    nc.vector.tensor_tensor_scan(h[:, s % DEPTH, :], ps[:, A + s % 2, :], decayed_in[:, s % DEPTH, :],
                                                 initial, ALU.mult, ALU.add).then_inc(scanned, 1)
                    if s == 2 and not first:
                        gate(g - 1)
                    if s == 10 and not first:
                        add(g - 1)

            def gate(g):
                at = slice(g * CH, (g + 1) * CH)
                dve.wait_ge(y_added, (g + 1) * STEPS)
                for f in range(FT):
                    nc.vector.scalar_tensor_tensor(out=yd[:, f, :], in0=u[:, f, at],
                                                   scalar=k.vec[:, VA_D + f:VA_D + f + 1], in1=ps[:, Y + f, :],
                                                   op0=ALU.mult, op1=ALU.add).then_inc(yd_ready, 1)
                for f in range(FT):
                    dve.wait_ge(yd_ready, g * FT + f + 1)
                    nc.vector.tensor_tensor(yz[:, f, :], yd[:, f, :], sz[:, f, at], ALU.mult).then_inc(yz_ready, 1)

            def add(g):
                at = slice(g * CH, (g + 1) * CH)
                dve.wait_ge(out_ready, g + 1)
                nc.vector.tensor_tensor(yd[:, 0, :], ps[:, O, :], k.xn[:, at], ALU.add).then_inc(res_ready, 1)
                dve.wait_ge(res_ready, g + 1)
                nc.vector.tensor_tensor(k.x[:, at], k.x[:, at], yd[:, 0, :], ALU.add).then_inc(x_added, 1)

            for b in range(BATCH):
                for half in range(HALVES):
                    half_sequence(b, half)
            gate(BATCH * HALVES - 1)
            add(BATCH * HALVES - 1)

        @block.gpsimd
        def _(pool):
            def half_sequence(b, half):
                first = half == 0 and b == 0
                g = b * HALVES + half
                for s in range(STEPS):
                    n, f = divmod(s, FT)
                    pool.wait_ge(scanned, g * STEPS + s + 1)
                    if f == 0:
                        pool.wait_ge(c_copied, g * NST + n + 1)
                    if not (first and s < DEPTH):
                        pool.wait_ge(y_added, g * STEPS + s - DEPTH + 1)
                    nc.gpsimd.tensor_tensor(hc[:, s % DEPTH, :], h[:, s % DEPTH, :], c_sb[:, n % 2, :], ALU.mult)\
                        .then_inc(hc_ready, 1)

            for b in range(BATCH):
                for half in range(HALVES):
                    half_sequence(b, half)


def load_weights(k, d, eng, n):
    done = k.raw_loaded[n % 2] if n < EARLY else k.late_loaded[n % 2]
    gu, dn = k.raw_gu[:, n % 2, :], k.raw_dn[:, n % 2, :, :]
    if n == 0:
        eng.dma_start(gu[:, 0:2 * NI * P + TAIL], d["gu_shared"][:, 0:2 * NI * P + TAIL]).then_inc(done, 16)
        eng.dma_start(gu[:, GU - TAIL:GU], d["gu_shared"][:, 2 * NI * P + TAIL:2 * NI * P + 2 * TAIL])\
            .then_inc(done, 16)
    else:
        eng.dma_start(gu[:, 0:INTER], d["gu"][n - 1, :, 0:INTER]).then_inc(done, 16)
        eng.dma_start(gu[:, INTER:2 * INTER], d["gu"][n - 1, :, INTER:2 * INTER]).then_inc(done, 16)
    eng.dma_start(dn[:, 0:NI, :], d["dn"][n, 0:NI * P, :].rearrange("(i p) m -> p i m", p=P)).then_inc(done, 16)
    eng.dma_start(dn[0:TAIL, NI, :], d["dn"][n, NI * P:INTER, :]).then_inc(done, 16)


def ffn_stage(k, d, which, tag, out=None):
    nc, ps, slot_rows = k.nc, k.ps, k.slot_rows[which]
    stage, counters = ExitStack(), ExitStack()
    sb = lambda name, shape, dt=F32, ctx=None: k.sb(f"{tag}_{name}", shape, dt, ctx=ctx or stage)
    used = []

    def sems(names):
        out = [k.sem(f"{tag}_{n}", counters) for n in names.split()]
        used.extend(out)
        return out

    gu_hi, gu_lo = [sb(n, [P, RING, GU], F32R) for n in ("gu_hi", "gu_lo")]
    dn_w = sb("dn_w", [P, RING, 2, TILES * P], F32R)
    zero = sb("zero", [P, 1])
    BUF = 3
    x_rows = sb("x_rows", [P, BUF, ROW])
    x_loaded = sems(" ".join(f"x_loaded{b}" for b in range(BUF)))
    slot = sb("slot", [P, TOP, TT], I32)
    table = sb("table", [1, 2 * SLOT_TILES + EXPERTS], I32)
    zero_set, split_step, w_ready, summed = sems("zero_set split_step w_ready summed")
    rows_sent, sent = k.rows_sent, k.outputs_sent
    LATE = (EXPERTS + 1 - EARLY) // 2
    PIECES = [(a, min(a + CH, GU)) for a in range(0, GU, CH)]
    NPIECE = len(PIECES) + TILES * P // CH

    def split_weights(pool, n):
        if n < EARLY:
            pool.wait_ge(k.raw_loaded[n % 2], 64 * (n // 2 + 1 + (EARLY + 1 - n % 2) // 2 * which))
        else:
            pool.wait_ge(k.late_loaded[n % 2], 64 * ((n - EARLY) // 2 + 1 + LATE * which))
        place = n % RING
        gu, dn = k.raw_gu[:, n % 2, :], k.raw_dn[:, n % 2, :, :].rearrange("p i m -> p (i m)")
        parts = [(gu[:, a:b], gu_hi[:, place, a:b], gu_lo[:, place, a:b]) for a, b in PIECES]
        parts += [(dn[:, a:a + CH], dn_w[:, place, 0, a:a + CH], dn_w[:, place, 1, a:a + CH])
                  for a in range(0, TILES * P, CH)]

        def low(j):
            src, hi, lo = parts[j]
            pool.wait_ge(split_step, n * NPIECE + j + 1)
            nc.gpsimd.tensor_tensor(lo, src, hi.bitcast(F32), ALU.subtract).then_inc(w_ready, 1)

        for j, (src, hi, lo) in enumerate(parts):
            nc.gpsimd.tensor_tensor(hi, src, zero[:, :].to_broadcast([P, src.shape[1]]), ALU.add)\
                .then_inc(split_step, 1)
            if j:
                low(j - 1)
        low(NPIECE - 1)

    shared = ExitStack()
    x_hi, x_lo = [sb(n, [P, T], F32R, ctx=shared) for n in ("x_hi", "x_lo")]
    w_gate = sb("w_gate", [P, EXPERTS], ctx=shared)
    one = sb("one", [P, P], ctx=shared)
    names = "logit prob chosen rank hit1 hit2 spare place"
    logit, prob, chosen, rank, hit1, hit2, spare, place = [sb(n, [P, TT, EXPERTS], ctx=shared) for n in names.split()]
    top, best1, best2, den, first_max, slot_f = [sb(n, [P, TT], ctx=shared) for n in
                                                 "top best1 best2 den first_max slot_f".split()]
    total, upto, keep, more = [sb(n, [P, EXPERTS, TT], ctx=shared) for n in "total upto keep more".split()]
    tiles, tiles_upto = [sb(n, [P, EXPERTS], ctx=shared) for n in ("tiles", "tiles_upto")]
    past = sb("past", [1, SLOT_TILES, EXPERTS - 1], ctx=shared)
    found = sb("found", [1, SLOT_TILES], ctx=shared)
    gate_loaded, one_set, logits_ready, step, exp_ready, chosen_ready, counts_ready, turned, slots_ready, \
        rows_copied, rows_ready, table_ready = sems(
            "gate_loaded one_set logits_ready router_step exp_ready chosen_ready counts_ready turned slots_ready "
            "rows_copied rows_ready table_ready")
    L = EXPERTS
    G, U, Y, R, XT = 0, 2, 4, 6, 7
    thresholds = k.fc[:, L:L + TT]
    numbers = k.fc[0:1, L + TT:L + TT + SLOT_TILES]
    ring_steps = k.fc[0:1, L + TT + SLOT_TILES:]

    def first_load(sp):
        sp.dma_start(w_gate[:, :], d["w_gateF"]).then_inc(gate_loaded, 16)

    def first_split(pool):
        nc.gpsimd.memset(zero[:, :], 0.0).then_inc(zero_set, 1)
        nc.gpsimd.memset(one[:, :], 1.0).then_inc(one_set, 1)
        pool.wait_ge(zero_set, 1)
        split_weights(pool, 0)

    def logits_of(pe, c):
        if c == 0:
            pe.wait_ge(gate_loaded, 16)
        for t in range(c * TT // NCH, (c + 1) * TT // NCH):
            last = nc.tensor.matmul(ps[:, R, t * EXPERTS:(t + 1) * EXPERTS], k.xn[:, t * P:(t + 1) * P],
                                    w_gate[:, :], start=True, stop=True)
        last.then_inc(logits_ready, 1)

    norm_stage(k, tag + "n", k.x, k.xn, True, k.eps5, split=(x_hi, x_lo), sync_part=first_load,
               pool_part=first_split, tensor_part=logits_of)
    rows = sb("rows", [P, TOP, TT, ROW], ctx=shared)

    def wide(v):
        return v[:, :].unsqueeze(2).to_broadcast([P, TT, EXPERTS])

    gate = sb("gate", [P, 2, CH], ctx=shared)
    prod = sb("prod", [P, 2, CH], ctx=shared)
    p_hi, p_lo = [sb(n, [P, 4, CH], F32R, ctx=shared) for n in ("p_hi", "p_lo")]
    N = TT * EXPERTS
    PER = NCH * TILES
    g_ready, gu_ready, silu_done, prod_done, high_ready, low_ready, x_added = sems(
        "g_ready gu_ready silu_done prod_done high_ready low_ready x_added")

    def k_of(i):
        return P if i < NI else TAIL

    with shared, nc.Block() as block:

        @block.sync
        def _(sp):
            load_weights(k, d, sp, 2)
            sp.wait_ge(rows_sent, 16 * TOP * TT * (which + 1))
            for j in range(BUF):
                sp.dma_start(x_rows[:, j, :], slot_rows[j * P:(j + 1) * P, :]).then_inc(x_loaded[j], 16)

        @block.gpsimd
        def _(pool):
            split_weights(pool, 1)
            pool.wait_ge(k.slots_filled, 32)
            pool.wait_ge(rows_copied, TOP * TT // 4)
            pool.wait_ge(rows_ready, 1 + TOP)
            pool.wait_ge(slots_ready, TOP)
            for t in range(TT):
                for c in range(TOP):
                    nc.gpsimd.indirect_dma_start(slot_rows, bass.IndirectOffsetOnAxis(ap=slot[:, c, t:t + 1], axis=0),
                                                 rows[:, c, t, :], None).then_inc(rows_sent, 16)
            pool.wait_ge(rows_sent, 16 * TOP * TT * (which + 1))

        @block.tensor
        def _(pe):
            def product(out, w_hi, w_lo, v_hi, v_lo, start, stop):
                nc.tensor.matmul(out, w_hi, v_hi, start=start, stop=False)
                nc.tensor.matmul(out, w_hi, v_lo, start=False, stop=False)
                return nc.tensor.matmul(out, w_lo, v_hi, start=False, stop=stop)

            def gate_up(q):
                c, i = divmod(q, TILES)
                xs = (x_hi[:, cols(c)], x_lo[:, cols(c)])
                if q >= 2:
                    pe.wait_ge(prod_done, q - 1)
                if i < NI:
                    a = i * P
                    product(ps[:, G + i % 2, :], gu_hi[:, 0, a:a + P], gu_lo[:, 0, a:a + P], *xs, True, True)\
                        .then_inc(g_ready, 1)
                    a += NI * P
                    product(ps[:, U + i % 2, :], gu_hi[:, 0, a:a + P], gu_lo[:, 0, a:a + P], *xs, True, True)\
                        .then_inc(gu_ready, 1)
                else:
                    a, m = 2 * NI * P, UT + TAIL
                    product(ps[0:m, G + i % 2, :], gu_hi[:, 0, a:a + m], gu_lo[:, 0, a:a + m], *xs, True, True)\
                        .then_inc(g_ready, 1)

            def down(q):
                c, i = divmod(q, TILES)
                if i == 0 and c >= 2:
                    pe.wait_ge(x_added, c - 1)
                pe.wait_ge(low_ready, q + 1)
                m, a = k_of(i), i * P
                product(ps[:, Y + c % 2, :], dn_w[0:m, 0, 0, a:a + P], dn_w[0:m, 0, 1, a:a + P],
                        p_hi[0:m, q % 4, :], p_lo[0:m, q % 4, :], i == 0, i == TILES - 1).then_inc(summed, 1)

            for q in range(PER):
                gate_up(q)
                if q >= 2:
                    down(q - 2)
                if 2 <= q < 2 + TT // 4:
                    g = q - 2
                    if g:
                        pe.wait_ge(rows_copied, TOP * g)
                    for t in range(4):
                        last = nc.tensor.transpose(ps[:, XT, t * P:(t + 1) * P],
                                                   k.xn[:, (4 * g + t) * P:(4 * g + t + 1) * P], k.eye[:, :])
                    last.then_inc(turned, 1)
                if q == 7:
                    pe.wait_ge(one_set, 1)
                    pe.wait_ge(chosen_ready, 1)
                    flat = chosen[:, :, :].rearrange("p t e -> p (t e)")
                    nc.tensor.matmul(ps[:, R, N:2 * N], k.masks[:, 0, :], flat, start=True, stop=True)
                    nc.tensor.matmul(ps[:, R, 2 * N:3 * N], one[:, :], flat, start=True, stop=True)\
                        .then_inc(counts_ready, 1)
            down(PER - 2)
            down(PER - 1)

        @block.scalar
        def _(act):
            def high(q):
                m = k_of(q % TILES)
                act.wait_ge(prod_done, q + 1)
                if q >= 4:
                    act.wait_ge(summed, q - 3)
                nc.scalar.activation(p_hi[0:m, q % 4, :], prod[0:m, q % 2, :], ACT.Copy).then_inc(high_ready, 1)

            act.wait_ge(step, 2)
            nc.scalar.activation(prob[:, :, :], logit[:, :, :], ACT.Exp).then_inc(exp_ready, 1)
            for q in range(PER):
                i, m = q % TILES, k_of(q % TILES)
                if 3 <= q < 3 + TT // 4:
                    g = q - 3
                    act.wait_ge(turned, g + 1)
                    for c in range(TOP):
                        nc.scalar.activation(rows[:, c, 4 * g:4 * g + 4, 0:P],
                                             ps[:, XT, :].rearrange("p (t d) -> p t d", d=P), ACT.Copy)\
                            .then_inc(rows_copied, 1)
                act.wait_ge(g_ready, q + 1)
                nc.scalar.activation(gate[0:m, q % 2, :], ps[0:m, G + i % 2, :], ACT.Silu).then_inc(silu_done, 1)
                if q:
                    high(q - 1)
            high(PER - 1)

        @block.vector
        def _(dve):
            done = [0]

            def then(ins):
                done[0] += 1
                ins.then_inc(step, 1)
                dve.wait_ge(step, done[0])

            def softmax():
                dve.wait_ge(logits_ready, NCH)
                logits = ps[:, R, 0:N].rearrange("p (t e) -> p t e", e=EXPERTS)
                then(nc.vector.tensor_reduce(top[:, :], logits, AX.X, ALU.max))
                then(nc.vector.tensor_tensor(logit[:, :, :], logits, wide(top), ALU.subtract))
                nc.vector.tensor_copy(rows[:, :, :, P:P + 1].rearrange("p a t o -> p (a t) o").bitcast(I32),
                                      k.places[:, 0:TOP * TT].unsqueeze(2)).then_inc(rows_ready, 1)
                nc.vector.memset(keep[:, :, :], 1.0).then_inc(step, 1)
                dve.wait_ge(step, 3)
                nc.vector.memset(keep[:, :, 0:1], 0.0).then_inc(step, 1)
                done[0] += 2
                dve.wait_ge(exp_ready, 1)
                then(nc.vector.tensor_reduce(den[:, :], prob[:, :, :], AX.X, ALU.add))
                then(nc.vector.reciprocal(den[:, :], den[:, :]))
                then(nc.vector.tensor_tensor(prob[:, :, :], prob[:, :, :], wide(den), ALU.mult))

            def rank_largest(left, best):
                then(nc.vector.tensor_reduce(best[:, :], left[:, :, :], AX.X, ALU.max))
                then(nc.vector.tensor_tensor(rank[:, :, :], left[:, :, :], wide(best), ALU.is_ge))
                then(nc.vector.tensor_tensor(rank[:, :, :], rank[:, :, :],
                                             k.fc[:, 0:L].unsqueeze(1).to_broadcast([P, TT, EXPERTS]), ALU.mult))

            def choose(hit):
                then(nc.vector.tensor_reduce(first_max[:, :], rank[:, :, :], AX.X, ALU.max))
                then(nc.vector.tensor_tensor(hit[:, :, :], rank[:, :, :], wide(first_max), ALU.is_equal))
                if hit is hit1:
                    then(nc.vector.scalar_tensor_tensor(out=spare[:, :, :], in0=hit1[:, :, :], scalar=-4.0,
                                                        in1=prob[:, :, :], op0=ALU.mult, op1=ALU.add))

            def weigh():
                then(nc.vector.tensor_tensor(chosen[:, :, :], hit1[:, :, :], hit2[:, :, :], ALU.add))
                nc.vector.scalar_tensor_tensor(out=den[:, :], in0=best1[:, :], scalar=1e-8, in1=best2[:, :],
                                               op0=ALU.add, op1=ALU.add).then_inc(chosen_ready, 1)
                dve.wait_ge(chosen_ready, 1)
                then(nc.vector.reciprocal(den[:, :], den[:, :]))
                for c, best in enumerate((best1, best2)):
                    nc.vector.tensor_tensor(rows[:, c, :, P + 1], best[:, :], den[:, :], ALU.mult)\
                        .then_inc(rows_ready, 1)

            def count_tiles():
                dve.wait_ge(counts_ready, 1)
                then(nc.vector.tensor_copy(total[:, :, :],
                                           ps[:, R, 2 * N:3 * N].rearrange("p (t e) -> p e t", e=EXPERTS)))
                then(nc.vector.tensor_tensor_scan(upto[:, :, :].rearrange("p e t -> p (e t)"),
                                                  keep[:, :, :].rearrange("p e t -> p (e t)"),
                                                  total[:, :, :].rearrange("p e t -> p (e t)"), 0.0, ALU.mult, ALU.add))
                then(nc.vector.tensor_tensor(more[:, :, :], upto[:, :, TT - 1:TT].to_broadcast([P, EXPERTS, TT]),
                                             thresholds.unsqueeze(1).to_broadcast([P, EXPERTS, TT]), ALU.is_gt))
                then(nc.vector.tensor_reduce(tiles[:, :], more[:, :, :], AX.X, ALU.add))

            def place_experts():
                then(nc.vector.tensor_tensor_scan(tiles_upto[:, :], one[:, 0:EXPERTS], tiles[:, :], 0.0,
                                                  ALU.mult, ALU.add))
                then(nc.vector.tensor_tensor(tiles[:, :], tiles_upto[:, :], tiles[:, :], ALU.subtract))
                then(nc.vector.tensor_tensor(upto[:, :, :], upto[:, :, :], total[:, :, :], ALU.subtract))
                then(nc.vector.scalar_tensor_tensor(out=upto[:, :, :],
                                                    in0=tiles[:, :].unsqueeze(2).to_broadcast([P, EXPERTS, TT]),
                                                    scalar=float(P), in1=upto[:, :, :], op0=ALU.mult, op1=ALU.add))

            def slots_in_order():
                then(nc.vector.tensor_tensor(place[:, :, :], ps[:, R, N:2 * N].rearrange("p (t e) -> p t e", e=EXPERTS),
                                             chosen[:, :, :], ALU.subtract))
                then(nc.vector.tensor_tensor(place[:, :, :], place[:, :, :],
                                             upto[:, :, :].rearrange("p e t -> p t e"), ALU.add))

            def slots_of(c, hit):
                then(nc.vector.tensor_tensor(rank[:, :, :], hit[:, :, :], place[:, :, :], ALU.mult))
                then(nc.vector.tensor_reduce(slot_f[:, :], rank[:, :, :], AX.X, ALU.add))
                nc.vector.tensor_copy(slot[:, c, :], slot_f[:, :]).then_inc(slots_ready, 1)
                dve.wait_ge(slots_ready, c + 1)

            def fill_table():
                shape = [1, SLOT_TILES, EXPERTS - 1]
                then(nc.vector.tensor_tensor(past[:, :, :], numbers.unsqueeze(2).to_broadcast(shape),
                                             tiles[0:1, 1:EXPERTS].unsqueeze(1).to_broadcast(shape), ALU.is_ge))
                then(nc.vector.tensor_reduce(found[:, :], past[:, :, :], AX.X, ALU.add))
                then(nc.vector.tensor_copy(table[:, 0:SLOT_TILES], found[:, :]))

            def fill_ring_places():
                then(nc.vector.tensor_tensor(past[:, :, :], past[:, :, :],
                                             ring_steps.unsqueeze(1).to_broadcast([1, SLOT_TILES, EXPERTS - 1]),
                                             ALU.mult))
                then(nc.vector.tensor_reduce(found[:, :], past[:, :, :], AX.X, ALU.add))
                then(nc.vector.tensor_scalar(found[:, :], found[:, :], 1.0, None, ALU.add))
                then(nc.vector.tensor_copy(table[:, SLOT_TILES:2 * SLOT_TILES], found[:, :]))
                nc.vector.tensor_copy(table[:, 2 * SLOT_TILES:], tiles[0:1, :]).then_inc(table_ready, 1)

            def low(q):
                m = k_of(q % TILES)
                dve.wait_ge(high_ready, q + 1)
                nc.vector.tensor_tensor(p_lo[0:m, q % 4, :], prod[0:m, q % 2, :],
                                        p_hi[0:m, q % 4, :].bitcast(F32), ALU.subtract).then_inc(low_ready, 1)

            def add(c):
                dve.wait_ge(summed, (c + 1) * TILES)
                nc.vector.tensor_tensor(k.x[:, cols(c)], k.x[:, cols(c)], ps[:, Y + c % 2, :], ALU.add)\
                    .then_inc(x_added, 1)

            softmax()
            for q in range(PER):
                c, i = divmod(q, TILES)
                m = k_of(i)
                dve.wait_ge(silu_done, q + 1)
                if i < NI:
                    dve.wait_ge(gu_ready, c * NI + i + 1)
                    up = ps[:, U + i % 2, :]
                else:
                    up = ps[UT:UT + TAIL, G + i % 2, :]
                if q >= 2:
                    dve.wait_ge(low_ready, q - 1)
                nc.vector.tensor_tensor(prod[0:m, q % 2, :], gate[0:m, q % 2, :], up, ALU.mult).then_inc(prod_done, 1)
                if q:
                    low(q - 1)
                if i == 3 and c:
                    add(c - 1)
                if q == 1:
                    rank_largest(prob, best1)
                if q == 2:
                    choose(hit1)
                if q == 3:
                    rank_largest(spare, best2)
                if q == 4:
                    choose(hit2)
                if q == 5:
                    weigh()
                if q == 8:
                    count_tiles()
                if q == 9:
                    place_experts()
                if q == 10:
                    slots_in_order()
                if q == 11:
                    slots_of(0, hit1)
                if q == 12:
                    slots_of(1, hit2)
                if q == 15:
                    fill_table()
                if q == 17:
                    fill_ring_places()
            low(PER - 1)
            add(NCH - 1)

    routed = ExitStack()
    xt_hi, xt_lo = [sb(n, [P, BUF, P], F32R, ctx=routed) for n in ("xt_hi", "xt_lo")]
    gates = sb("gates", [P, 2, HALVES[0]], ctx=routed)
    prods = sb("prods", [P, BUF, TILES * P], ctx=routed)
    q_hi, q_lo = [sb(n, [P, BUF, TILES * P], F32R, ctx=routed) for n in ("q_hi", "q_lo")]
    cross = sb("cross", [P, BUF, P], ctx=routed)
    outs = sb("outs", [P, SLOT_TILES, P], ctx=routed)
    back = sb("back", [P, SLOT_TILES], I32, ctx=routed)
    share = sb("share", [P, BUF], ctx=routed)
    XB, TR, Y2 = 4, 5, 7
    rest_zero, back_ready, share_ready, x_turned, x_high, x_low, gates_ready, ups_ready, gates_silu, prods_ready, \
        prods_turned, q_high, q_low, cross_ready, outs_ready = sems(
            "rest_zero back_ready share_ready x_turned x_high x_low gates_ready ups_ready gates_silu prods_ready "
            "prods_turned q_high q_low cross_ready outs_ready")

    def all_tiles(eng, tile):
        for b in range(BUF):
            tile(b, b, 0)
        with eng.Fori(1, SLOT_TILES // BUF) as turn:
            for b in range(BUF):
                tile(turn * BUF + b, b, turn)

    def reached(j, first):
        return not isinstance(j, int) or j >= first

    def from_tile(eng, j, first, sem, value):
        if reached(j, first):
            eng.wait_ge(sem, value)

    with routed, nc.Block() as block:

        @block.sync
        def _(sp):
            with sp.Fori(1, SLOT_TILES // BUF) as turn:
                for b in range(BUF):
                    j = turn * BUF + b
                    sp.wait_ge(x_turned, j - BUF + 1)
                    sp.wait_ge(back_ready, j - BUF + 1)
                    sp.wait_ge(share_ready, j - BUF + 1)
                    sp.dma_start(x_rows[:, b, :], slot_rows[bass.ds(j * P, P), :]).then_inc(x_loaded[b], 16)

        @block.gpsimd
        def _(pool):
            load_weights(k, d, pool, EARLY)
            for n in range(2, EXPERTS + 1):
                if EARLY < n + 1 <= EXPERTS:
                    pool.wait_ge(w_ready, n * NPIECE)
                    load_weights(k, d, pool, n + 1)
                if n == RING:
                    pool.wait_ge(summed, PER)
                if n > RING:
                    first = pool.value_load(table[0:1, 2 * SLOT_TILES + n - RING:2 * SLOT_TILES + n - RING + 1],
                                            min_val=1, max_val=SLOT_TILES)
                    pool.wait_ge(summed, first + PER)
                split_weights(pool, n)
            for j in range(SLOT_TILES):
                pool.wait_ge(back_ready, j + 1)
                pool.wait_ge(outs_ready, j + 1)
                nc.gpsimd.indirect_dma_start(k.token_rows, bass.IndirectOffsetOnAxis(ap=back[:, j:j + 1], axis=0),
                                             outs[:, j, :], None).then_inc(sent, 16)
            pool.wait_ge(sent, 16 * SLOT_TILES * (which + 1))

        @block.tensor
        def _(pe):
            def turn_products(j, b):
                pe.wait_ge(prods_ready, 2 * j + 2)
                from_tile(pe, j, 1, q_low, 2 * j)
                for i in range(TILES):
                    last = nc.tensor.transpose(ps[:, TR + i // 4, (i % 4) * P:(i % 4 + 1) * P],
                                               prods[:, b, i * P:(i + 1) * P], k.eye[:, :])
                    if i % 4 == 3:
                        last.then_inc(prods_turned, 1)

            def down(j, b, ring):
                pe.wait_ge(q_low, 2 * j + 2)
                from_tile(pe, j, 1, outs_ready, j)
                for i in range(TILES):
                    a = slice(i * P, (i + 1) * P)
                    nc.tensor.matmul(ps[:, Y2, 0:2 * P], q_hi[:, b, a], dn_at(ring, i), start=(i == 0),
                                     stop=False, skip_group_check=True)
                    last = nc.tensor.matmul(ps[:, Y2, 0:P], q_lo[:, b, a], dn_high_at(ring, i), start=False,
                                            stop=(i == TILES - 1), skip_group_check=True)
                last.then_inc(summed, 1)
                return last

            def dn_at(ring, i):
                return dn_w[:, bass.ds(ring, 1), :, i * P:(i + 1) * P].rearrange("p r h m -> p (r h) m")

            def dn_high_at(ring, i):
                return dn_w[:, bass.ds(ring, 1), 0, i * P:(i + 1) * P].rearrange("p r m -> p (r m)")

            def tile(j, b, turn):
                expert = pe.value_load(table[0:1, bass.ds(j, 1)], min_val=0, max_val=EXPERTS - 1)
                ring = pe.value_load(table[0:1, bass.ds(SLOT_TILES + j, 1)], min_val=0, max_val=RING - 1)
                pe.wait_ge(x_loaded[b], turn * 16 + 16)
                from_tile(pe, j, 1, x_low, j)
                nc.tensor.transpose(ps[:, XB, 0:P], x_rows[:, b, 0:P], k.eye[:, :]).then_inc(x_turned, 1)
                if reached(j, 2):
                    before = pe.value_load(table[0:1, bass.ds(SLOT_TILES + j - 2, 1)], min_val=0, max_val=RING - 1)
                    down(j - 2, (b - 2) % BUF, before)
                if reached(j, 1):
                    turn_products(j - 1, (b - 1) % BUF)
                pe.wait_ge(w_ready, expert * NPIECE + 2 * NPIECE)
                pe.wait_ge(x_low, j + 1)
                for half in range(2):
                    for up in range(2):
                        a, m = (half * 2 * HALVES[0]) + up * HALVES[half], HALVES[half]
                        out = ps[:, 2 * half + up, 0:m]
                        w_hi = gu_hi[:, bass.ds(ring, 1), a:a + m].rearrange("p r m -> p (r m)")
                        w_lo = gu_lo[:, bass.ds(ring, 1), a:a + m].rearrange("p r m -> p (r m)")
                        nc.tensor.matmul(out, xt_hi[:, b, :], w_hi, start=True, stop=False)
                        nc.tensor.matmul(out, xt_hi[:, b, :], w_lo, start=False, stop=False)
                        nc.tensor.matmul(out, xt_lo[:, b, :], w_hi, start=False, stop=True)\
                            .then_inc(ups_ready if up else gates_ready, 1)

            pe.wait_ge(rest_zero, 1)
            all_tiles(pe, tile)
            J = SLOT_TILES
            before = pe.value_load(table[0:1, 2 * J - 2:2 * J - 1], min_val=0, max_val=RING - 1)
            down(J - 2, (J - 2) % BUF, before)
            turn_products(J - 1, (J - 1) % BUF)
            before = pe.value_load(table[0:1, 2 * J - 1:2 * J], min_val=0, max_val=RING - 1)
            down(J - 1, (J - 1) % BUF, before)

        @block.scalar
        def _(act):
            def evac(j, b):
                for half in range(2):
                    act.wait_ge(prods_turned, 2 * j + half + 1)
                    from_tile(act, j, BUF, summed, PER + j - BUF + 1)
                    nc.scalar.activation(q_hi[:, b, half * CH:(half + 1) * CH], ps[:, TR + half, :], ACT.Copy)\
                        .then_inc(q_high, 1)

            def crossed(j, b):
                act.wait_ge(summed, PER + j + 1)
                act.wait_ge(share_ready, j + 1)
                nc.scalar.activation(cross[:, b, :], ps[:, Y2, P:2 * P], ACT.Copy, scale=share[:, b:b + 1])\
                    .then_inc(cross_ready, 1)

            def tile(j, b, turn):
                act.wait_ge(x_turned, j + 1)
                nc.scalar.activation(xt_hi[:, b, :], ps[:, XB, 0:P], ACT.Copy).then_inc(x_high, 1)
                if reached(j, 2):
                    crossed(j - 2, (b - 2) % BUF)
                if reached(j, 1):
                    evac(j - 1, (b - 1) % BUF)
                for half in range(2):
                    act.wait_ge(gates_ready, 2 * j + half + 1)
                    if reached(j, 1):
                        act.wait_ge(prods_ready, 2 * j + half - 1)
                    nc.scalar.activation(gates[:, half, 0:HALVES[half]], ps[:, 2 * half, 0:HALVES[half]], ACT.Silu)\
                        .then_inc(gates_silu, 1)

            all_tiles(act, tile)
            J = SLOT_TILES
            crossed(J - 2, (J - 2) % BUF)
            evac(J - 1, (J - 1) % BUF)
            crossed(J - 1, (J - 1) % BUF)

        @block.vector
        def _(dve):
            def evac(j, b):
                for half in range(2):
                    dve.wait_ge(q_high, 2 * j + half + 1)
                    at = slice(half * CH, (half + 1) * CH)
                    nc.vector.tensor_tensor(q_lo[:, b, at], ps[:, TR + half, :], q_hi[:, b, at].bitcast(F32),
                                            ALU.subtract).then_inc(q_low, 1)

            def finish(j, b):
                dve.wait_ge(cross_ready, j + 1)
                nc.vector.scalar_tensor_tensor(out=outs[:, bass.ds(j, 1), :].rearrange("p a m -> p (a m)"),
                                               in0=ps[:, Y2, 0:P], scalar=share[:, b:b + 1], in1=cross[:, b, :],
                                               op0=ALU.mult, op1=ALU.add).then_inc(outs_ready, 1)

            def tile(j, b, turn):
                dve.wait_ge(x_high, j + 1)
                nc.vector.tensor_copy(back[:, bass.ds(j, 1)], x_rows[:, b, P:P + 1].bitcast(I32)).then_inc(back_ready, 1)
                from_tile(dve, j, BUF, cross_ready, j - BUF + 1)
                from_tile(dve, j, BUF, outs_ready, j - BUF + 1)
                nc.vector.tensor_copy(share[:, b:b + 1], x_rows[:, b, P + 1:ROW]).then_inc(share_ready, 1)
                nc.vector.tensor_tensor(xt_lo[:, b, :], ps[:, XB, 0:P], xt_hi[:, b, :].bitcast(F32),
                                        ALU.subtract).then_inc(x_low, 1)
                if reached(j, 2):
                    finish(j - 2, (b - 2) % BUF)
                if reached(j, 1):
                    evac(j - 1, (b - 1) % BUF)
                for half in range(2):
                    dve.wait_ge(gates_silu, 2 * j + half + 1)
                    dve.wait_ge(ups_ready, 2 * j + half + 1)
                    nc.vector.tensor_tensor(prods[:, b, half * HALVES[0]:half * HALVES[0] + HALVES[half]],
                                            gates[:, half, 0:HALVES[half]], ps[:, 2 * half + 1, 0:HALVES[half]],
                                            ALU.mult).then_inc(prods_ready, 1)

            nc.vector.memset(prods[:, :, INTER:], 0.0).then_inc(rest_zero, 1)
            all_tiles(dve, tile)
            J = SLOT_TILES
            finish(J - 2, (J - 2) % BUF)
            evac(J - 1, (J - 1) % BUF)
            finish(J - 1, (J - 1) % BUF)

    combine = ExitStack()
    chosen_out = sb("chosen_out", [P, TOP, TT, P], ctx=combine)
    out_loaded = sems(" ".join(f"out_loaded{g}" for g in range(NCH)))
    both_ready, tokens_ready, out_added, stored = sems("both_ready tokens_ready out_added stored")
    PT = TT // NCH
    with combine, nc.Block() as block:

        @block.sync
        def _(sp):
            for g in range(NCH):
                for c in range(TOP):
                    sp.dma_start(chosen_out[:, c, g * PT:(g + 1) * PT, :],
                                 k.token_rows[c * T + g * CH:c * T + (g + 1) * CH, :]
                                 .rearrange("(t p) m -> p t m", p=P)).then_inc(out_loaded[g], 16)
            if out is not None:
                for g in range(NCH):
                    sp.wait_ge(out_added, g + 1)
                    sp.dma_start(out[:, cols(g)], k.x[:, cols(g)]).then_inc(stored, 16)
                sp.wait_ge(stored, 16 * NCH)

        @block.tensor
        def _(pe):
            for g in range(NCH):
                pe.wait_ge(both_ready, g + 1)
                for t in range(PT):
                    last = nc.tensor.transpose(ps[:, g, t * P:(t + 1) * P], chosen_out[:, 0, g * PT + t, :],
                                               k.eye[:, :])
                last.then_inc(tokens_ready, 1)

        @block.vector
        def _(dve):
            def add(g):
                dve.wait_ge(tokens_ready, g + 1)
                nc.vector.tensor_tensor(k.x[:, cols(g)], k.x[:, cols(g)], ps[:, g, :], ALU.add)\
                    .then_inc(out_added, 1)

            for g in range(NCH):
                dve.wait_ge(out_loaded[g], 16 * TOP)
                at = slice(g * PT, (g + 1) * PT)
                nc.vector.tensor_tensor(chosen_out[:, 0, at, :], chosen_out[:, 0, at, :], chosen_out[:, 1, at, :],
                                        ALU.add).then_inc(both_ready, 1)
                if g:
                    add(g - 1)
            add(NCH - 1)
    stage.close()
    with counters, nc.Block() as block:

        @block.sync
        def _(sp):
            for s in used:
                sp.sem_clear(s)


def mixer_b_stage(k, d):
    nc, ps = k.nc, k.ps
    stage = ExitStack()
    sb = lambda name, shape, dt=F32, ctx=None: k.sb("b_" + name, shape, dt, ctx=ctx or stage)
    sem = lambda name: k.sem("b_" + name)
    HEADS, HD = 4, 64
    CONV = 4
    MT = 3
    conv = sb("conv", [P, 4, T])
    xs, bT, cT = conv[:, 0:2, :], conv[:, 2, :], conv[:, 3, :]
    sz, y = [sb(n, [P, FT, T]) for n in ("sz", "y")]
    head_rows = sb("head_rows", [P, 2, HEADS])
    dt = sb("dt", [P, TT, HEADS])
    dt_log = sb("dt_log", [P, TT, HEADS])
    dta = sb("dta", [P, TT, HEADS])
    dta_hi, dta_lo = [sb(n, [P, TT, HEADS], F32R) for n in ("dta_hi", "dta_lo")]
    neg_a = sb("neg_a", [P, HEADS])
    w_out = sb("w_out", [P, FT, P])
    pre = ExitStack()
    xp = sb("xp", [P, BATCH, PADDED], ctx=pre)
    w_in = sb("w_in", [P, 2 * DI + 2 * P + HEADS], ctx=pre)
    w_tap = sb("w_tap", [P, TAPS, P], ctx=pre)
    taps = sb("taps", [P, TAPS, P], ctx=pre)
    raw = sb("raw_conv", [P, CONV - 1, BATCH, PADDED], ctx=pre)
    loaded, pad_zero, taps_ready, xz_ready, bank_read, conv_step, silu_done, dt_ready, dt_step, a_ready, \
        dta_ready = [sem(n) for n in (
        "loaded pad_zero taps_ready xz_ready bank_read conv_step silu_done dt_ready dt_step a_ready dta_ready").split()]

    with nc.Block() as block:

        @block.sync
        def _(sp):
            sp.dma_start(taps[:, :, :].rearrange("p a b -> p (a b)"), d["tapsB"].partition_broadcast(P))\
                .then_inc(loaded, 16)
            sp.dma_start(w_in[:, :], d["w_inB"]).then_inc(loaded, 16)
            sp.dma_start(w_out[:, :, :], d["w_outB"]).then_inc(loaded, 16)
            sp.dma_start(head_rows[:, :, :].rearrange("p a b -> p (a b)"), d["headsB"].partition_broadcast(P))\
                .then_inc(loaded, 16)

        @block.gpsimd
        def _(pool):
            nc.gpsimd.memset(xp[:, :, 0:PADC], 0.0).then_inc(pad_zero, 1)
            nc.gpsimd.memset(raw[:, :, :, 0:PADC], 0.0).then_inc(pad_zero, 1)

    norm_stage(k, "nb", k.x, k.xn, True, k.eps5, weight=k.vec[:, VB_NORM:VB_NORM + 1], rms_eps=k.eps6, out=xp)

    JT = CONV + FT
    RAW = CONV - 1

    with pre, nc.Block() as block:

        @block.tensor
        def _(pe):
            pe.wait_ge(loaded, 16 * 4)
            pe.wait_ge(pad_zero, 1)
            for t in range(TT):
                b, t0 = divmod(t * P, SEQ)
                last = nc.tensor.matmul(ps[:, 4, t * HEADS:(t + 1) * HEADS], xp[:, b, PADC + t0:PADC + t0 + P],
                                        w_in[:, 2 * DI + 2 * P:], start=True, stop=True)
            last.then_inc(dt_ready, 1)
            pe.wait_ge(taps_ready, TAPS)
            for c in range(NCH):
                b, t0 = divmod(c * CH, SEQ)
                for j in range(JT):
                    n = c * JT + j
                    if n >= 4:
                        pe.wait_ge(bank_read, n - 3)
                    if j == JT - 1:
                        for tap in range(TAPS):
                            off = PADC + t0 - (TAPS - 1) + tap
                            last = nc.tensor.matmul(ps[:, n % 4, :], w_tap[:, tap, :], xp[:, b, off:off + CH],
                                                    start=(tap == 0), stop=(tap == TAPS - 1))
                    else:
                        at = (FT + j) * P if j < RAW else (j - RAW) * P
                        last = nc.tensor.matmul(ps[:, n % 4, :], w_in[:, at:at + P],
                                                xp[:, b, PADC + t0:PADC + t0 + CH], start=True, stop=True)
                    last.then_inc(xz_ready, 1)

        @block.scalar
        def _(act):
            act.wait_ge(dt_step, 1)
            nc.scalar.activation(dt_log[:, :, :], dt[:, :, :], ACT.Abs).then_inc(dt_step, 1)
            act.wait_ge(dt_step, 2)
            nc.scalar.activation(dt_log[:, :, :], dt_log[:, :, :], ACT.Exp, scale=-1.0).then_inc(dt_step, 1)
            nc.scalar.activation(neg_a[:, :], head_rows[:, 1, :], ACT.Exp).then_inc(a_ready, 1)
            act.wait_ge(dt_step, 3)
            nc.scalar.activation(dt_log[:, :, :], dt_log[:, :, :], ACT.Ln, bias=1.0).then_inc(dt_step, 1)
            act.wait_ge(pad_zero, 2)

            def silu_conv(c):
                for j in range(RAW):
                    act.wait_ge(conv_step, (c * TAPS + TAPS - 1) * RAW + j + 1)
                    nc.scalar.activation(conv[:, j, cols(c)], conv[:, j, cols(c)], ACT.Silu,
                                         bias=k.vec[:, VB_CB + j:VB_CB + j + 1]).then_inc(silu_done, 1)

            for c in range(NCH):
                b, t0 = divmod(c * CH, SEQ)
                for j in range(JT):
                    n = c * JT + j
                    act.wait_ge(xz_ready, n + 1)
                    if j < RAW:
                        nc.scalar.activation(raw[:, j, b, PADC + t0:PADC + t0 + CH], ps[:, n % 4, :], ACT.Copy)\
                            .then_inc(bank_read, 1)
                    elif j < JT - 1:
                        nc.scalar.activation(sz[:, j - RAW, cols(c)], ps[:, n % 4, :], ACT.Silu).then_inc(bank_read, 1)
                    else:
                        nc.scalar.activation(conv[:, RAW, cols(c)], ps[:, n % 4, :], ACT.Silu,
                                             bias=k.vec[:, VB_CB + RAW:VB_CB + RAW + 1]).then_inc(bank_read, 1)
                if c:
                    silu_conv(c - 1)
            silu_conv(NCH - 1)

        @block.vector
        def _(dve):
            dve.wait_ge(loaded, 16 * 4)
            for tap in range(TAPS):
                nc.vector.tensor_tensor(w_tap[:, tap, :], w_in[:, DI + RAW * P:DI + CONV * P], taps[:, tap, :], ALU.mult)\
                    .then_inc(taps_ready, 1)
            dve.wait_ge(dt_ready, 1)
            nc.vector.tensor_tensor(dt[:, :, :], ps[:, 4, 0:TT * HEADS].rearrange("p (t h) -> p t h", h=HEADS),
                                    head_rows[:, 0, :].unsqueeze(1).to_broadcast([P, TT, HEADS]), ALU.add)\
                .then_inc(dt_step, 1)
            dve.wait_ge(dt_step, 4)
            nc.vector.scalar_tensor_tensor(out=dt[:, :, :], in0=dt[:, :, :], scalar=0.0, in1=dt_log[:, :, :],
                                           op0=ALU.max, op1=ALU.add).then_inc(dt_step, 1)
            dve.wait_ge(a_ready, 1)
            nc.vector.tensor_scalar(neg_a[:, :], neg_a[:, :], -1.0, None, ALU.mult).then_inc(a_ready, 1)
            dve.wait_ge(dt_step, 5)
            dve.wait_ge(a_ready, 2)
            nc.vector.tensor_tensor(dta[:, :, :], dt[:, :, :],
                                    neg_a[:, :].unsqueeze(1).to_broadcast([P, TT, HEADS]), ALU.mult)\
                .then_inc(dta_ready, 1)
            dve.wait_ge(dta_ready, 1)
            nc.vector.tensor_copy(dta_hi[:, :, :], dta[:, :, :]).then_inc(dta_ready, 1)
            dve.wait_ge(dta_ready, 2)
            nc.vector.tensor_tensor(dta_lo[:, :, :], dta[:, :, :], dta_hi[:, :, :].bitcast(F32), ALU.subtract)\
                .then_inc(dta_ready, 1)
            dve.wait_ge(pad_zero, 2)
            for c in range(NCH):
                b, t0 = divmod(c * CH, SEQ)
                for tap in range(TAPS):
                    off = PADC + t0 - (TAPS - 1) + tap
                    for j in range(RAW):
                        src, to = raw[:, j, b, off:off + CH], conv[:, j, cols(c)]
                        w = k.vec[:, VB_TAPS + j * TAPS + tap:VB_TAPS + j * TAPS + tap + 1]
                        if tap == 0:
                            dve.wait_ge(bank_read, c * JT + j + 1)
                            nc.vector.tensor_scalar(to, src, w, None, ALU.mult).then_inc(conv_step, 1)
                        else:
                            dve.wait_ge(conv_step, (c * TAPS + tap - 1) * RAW + j + 1)
                            nc.vector.scalar_tensor_tensor(out=to, in0=src, scalar=w, in1=to, op0=ALU.mult,
                                                           op1=ALU.add).then_inc(conv_step, 1)

    mean_square = sb("mean_square", [P, T])
    sq = sb("sq", [P, FT, CH])
    ssd = ExitStack()
    one = sb("one", [P, P], F32R, ctx=ssd)
    later = sb("later", [P, P], F32R, ctx=ssd)
    steps_hi, steps_lo = [sb(n, [P, 2, HEADS, P], F32R, ctx=ssd) for n in ("steps_hi", "steps_lo")]
    decay = sb("decay", [P, 2, HEADS, P], ctx=ssd)
    into = sb("into", [P, 2, HEADS, P], ctx=ssd)
    toks = sb("toks", [P, 2, 3 * P], ctx=ssd)
    gram = sb("gram", [P, 2, P], ctx=ssd)
    mix = sb("mix", [P, 2, HEADS, P], ctx=ssd)
    c_in = sb("c_in", [P, 2, HEADS, P], ctx=ssd)
    x_dt = sb("x_dt", [P, 2, HEADS, HD], ctx=ssd)
    x_end = sb("x_end", [P, 2, HEADS, HD], ctx=ssd)
    state = sb("state", [P, 2, HEADS, HD], ctx=ssd)
    kept = sb("kept", [P, HEADS, HD], ctx=ssd)
    D, E, F, TR, Y, S, M = 0, 1, 2, 3, 4, 6, 7
    PER_SEQ = SEQ // P
    one_set, later_ready, steps_ready, d_ready, e_ready, f_ready, tr_ready, decay_ready, into_ready, toks_ready, \
        gram_ready, mix_ready, c_in_ready, x_dt_ready, x_end_ready, y_summed, ds_ready, kept_ready, state_ready, \
        yd_ready, yz_ready, squared, ms_ready, ms_saved, out_scaled = [sem(n) for n in (
            "one_set later_ready steps_ready d_ready e_ready f_ready tr_ready decay_ready into_ready toks_ready "
            "gram_ready mix_ready c_in_ready x_dt_ready x_end_ready y_summed ds_ready kept_ready state_ready "
            "yd_ready yz_ready squared ms_ready ms_saved out_scaled").split()]

    with ssd, nc.Block() as block:

        @block.sync
        def _(sp):
            sp.wait_ge(k.raw_zero, 4)
            load_weights(k, d, sp, 0)
            load_weights(k, d, sp, 1)

        @block.tensor
        def _(pe):
            def of_steps(out, which, c):
                nc.tensor.matmul(out, which, steps_hi[:, c % 2, :, :].rearrange("p h i -> p (h i)"),
                                 start=True, stop=False)
                return nc.tensor.matmul(out, which, steps_lo[:, c % 2, :, :].rearrange("p h i -> p (h i)"),
                                        start=False, stop=True)

            def chunk_inputs(c):
                ts = slice(c * P, (c + 1) * P)
                pe.wait_ge(steps_ready, 2 * c + 2)
                if c >= 1:
                    pe.wait_ge(decay_ready, c)
                    pe.wait_ge(into_ready, c)
                    pe.wait_ge(gram_ready, c)
                    pe.wait_ge(toks_ready, c)
                nc.tensor.matmul(ps[:, F, 0:P], bT[:, ts], cT[:, ts], start=True, stop=True).then_inc(f_ready, 1)
                of_steps(ps[:, D, :], later[:, :], c).then_inc(d_ready, 1)
                nc.tensor.transpose(ps[:, TR, 0:P], xs[:, 0, ts], k.eye[:, :])
                nc.tensor.transpose(ps[:, TR, P:2 * P], xs[:, 1, ts], k.eye[:, :])
                nc.tensor.transpose(ps[:, TR, 2 * P:3 * P], bT[:, ts], k.eye[:, :]).then_inc(tr_ready, 1)
                of_steps(ps[:, E, :], one[:, :], c).then_inc(e_ready, 1)

            def chunk_outputs(c):
                if c % 4 == 0 and c:
                    pe.wait_ge(yd_ready, c // 4 * FT)
                pe.wait_ge(x_dt_ready, c + 1)
                pe.wait_ge(mix_ready, c + 1)
                pe.wait_ge(c_in_ready, c + 1)
                pe.wait_ge(state_ready, c + 1)
                for h in range(HEADS):
                    out = ps[HD * (h % 2):HD * (h % 2) + HD, Y + h // 2, (c % 4) * P:(c % 4 + 1) * P]
                    nc.tensor.matmul(out, x_dt[:, c % 2, h, :], mix[:, c % 2, h, :], start=True, stop=False)
                    last = nc.tensor.matmul(out, state[:, c % 2, h, :], c_in[:, c % 2, h, :], start=False, stop=True)
                last.then_inc(y_summed, 1)
                pe.wait_ge(x_end_ready, c + 1)
                nc.tensor.matmul(ps[:, S, 0:HEADS * HD], toks[:, c % 2, 2 * P:3 * P],
                                 x_end[:, c % 2, :, :].rearrange("p h q -> p (h q)"), start=True, stop=True)\
                    .then_inc(ds_ready, 1)

            def mean_squares(g):
                pe.wait_ge(squared, (g + 1) * FT)
                if g:
                    pe.wait_ge(ms_saved, g)
                for f in range(FT):
                    last = nc.tensor.matmul(ps[:, M, :], k.ones[:, :], sq[:, f, :], start=(f == 0), stop=(f == FT - 1))
                last.then_inc(ms_ready, 1)

            pe.wait_ge(one_set, 1)
            pe.wait_ge(later_ready, 1)
            chunk_inputs(0)
            for c in range(TT):
                if c + 1 < TT:
                    chunk_inputs(c + 1)
                chunk_outputs(c)
                if c % 4 == 2 and c > 4:
                    mean_squares(c // 4 - 1)

        @block.scalar
        def _(act):
            def square(g):
                if g:
                    act.wait_ge(ms_ready, g)
                act.wait_ge(yz_ready, (g + 1) * FT)
                nc.scalar.activation(sq[:, :, :], y[:, :, cols(g)], ACT.Square).then_inc(squared, FT)

            def save(g):
                act.wait_ge(ms_ready, g + 1)
                nc.scalar.activation(mean_square[:, cols(g)], ps[:, M, :], ACT.Copy, scale=P / DI).then_inc(ms_saved, 1)

            for c in range(TT):
                if c % 4 == 1 and c > 4:
                    square(c // 4 - 1)
                if c % 4 == 0 and c > 4:
                    save(c // 4 - 2)
                if c >= 2:
                    act.wait_ge(ds_ready, c - 1)
                    act.wait_ge(kept_ready, c - 1)
                act.wait_ge(d_ready, c + 1)
                nc.scalar.activation(decay[:, c % 2, :, :].rearrange("p h i -> p (h i)"), ps[:, D, :], ACT.Exp)\
                    .then_inc(decay_ready, 1)
                act.wait_ge(tr_ready, c + 1)
                nc.scalar.activation(toks[:, c % 2, :], ps[:, TR, 0:3 * P], ACT.Copy).then_inc(toks_ready, 1)
                act.wait_ge(e_ready, c + 1)
                nc.scalar.activation(into[:, c % 2, :, :].rearrange("p h i -> p (h i)"), ps[:, E, :], ACT.Exp)\
                    .then_inc(into_ready, 1)
            save(TT // 4 - 2)
            square(TT // 4 - 1)

        @block.gpsimd
        def _(pool):
            def make_steps(c):
                if c >= 2:
                    pool.wait_ge(e_ready, c - 1)
                for steps, part in ((steps_hi, dta_hi), (steps_lo, dta_lo)):
                    nc.gpsimd.tensor_tensor(steps[:, c % 2, :, :],
                                            k.masks[:, 0, :].unsqueeze(1).to_broadcast([P, HEADS, P]),
                                            part[:, c, :].bitcast(F32).unsqueeze(2).to_broadcast([P, HEADS, P]),
                                            ALU.mult).then_inc(steps_ready, 1)

            nc.gpsimd.memset(one[:, :].bitcast(F32), 1.0).then_inc(one_set, 1)
            zero_gap(k)
            make_steps(0)
            for c in range(TT):
                if c + 1 < TT:
                    make_steps(c + 1)
                if c >= 2:
                    pool.wait_ge(ds_ready, c - 1)
                pool.wait_ge(toks_ready, c + 1)
                nc.gpsimd.tensor_tensor(x_dt[:, c % 2, :, :],
                                        toks[:, c % 2, 0:2 * P].rearrange("p (h q) -> p h q", h=HEADS),
                                        dt[:, c, :].unsqueeze(2).to_broadcast([P, HEADS, HD]), ALU.mult)\
                    .then_inc(x_dt_ready, 1)
                pool.wait_ge(x_dt_ready, c + 1)
                pool.wait_ge(decay_ready, c + 1)
                nc.gpsimd.tensor_tensor(x_end[:, c % 2, :, :], x_dt[:, c % 2, :, :],
                                        decay[:, c % 2, :, P - 1:P].to_broadcast([P, HEADS, HD]), ALU.mult)\
                    .then_inc(x_end_ready, 1)

        @block.vector
        def _(dve):
            nc.vector.memset(state[:, 0, :, :], 0.0).then_inc(state_ready, 1)
            for f in range(FT):
                nc.vector.tensor_scalar(w_out[:, f, :], w_out[:, f, :], k.vec[:, VB_SSM + f:VB_SSM + f + 1], None,
                                        ALU.mult).then_inc(out_scaled, 1)
            nc.vector.tensor_copy(later[:, :], k.masks[:, 1, :]).then_inc(later_ready, 1)

            def prepare(c):
                ts = slice(c * P, (c + 1) * P)
                dve.wait_ge(f_ready, c + 1)
                if c >= 2:
                    dve.wait_ge(y_summed, c - 1)
                    dve.wait_ge(mix_ready, c - 1)
                nc.vector.tensor_tensor(gram[:, c % 2, :], ps[:, F, 0:P], k.masks[:, 0, :], ALU.mult)\
                    .then_inc(gram_ready, 1)
                dve.wait_ge(decay_ready, c + 1)
                dve.wait_ge(gram_ready, c + 1)
                nc.vector.tensor_tensor(mix[:, c % 2, :, :], decay[:, c % 2, :, :],
                                        gram[:, c % 2, :].unsqueeze(1).to_broadcast([P, HEADS, P]), ALU.mult)\
                    .then_inc(mix_ready, 1)
                dve.wait_ge(into_ready, c + 1)
                nc.vector.tensor_tensor(c_in[:, c % 2, :, :], into[:, c % 2, :, :],
                                        cT[:, ts].unsqueeze(1).to_broadcast([P, HEADS, P]), ALU.mult)\
                    .then_inc(c_in_ready, 1)

            prepare(0)
            for c in range(TT):
                if c + 1 < TT:
                    prepare(c + 1)
                    if c >= 1:
                        dve.wait_ge(y_summed, c)
                    if (c + 1) % PER_SEQ == 0:
                        nc.vector.memset(kept[:, :, :], 0.0).then_inc(kept_ready, 1)
                        dve.wait_ge(kept_ready, c + 1)
                        nc.vector.memset(state[:, (c + 1) % 2, :, :], 0.0).then_inc(state_ready, 1)
                    else:
                        dve.wait_ge(state_ready, c + 1)
                        nc.vector.tensor_tensor(kept[:, :, :], state[:, c % 2, :, :],
                                                into[:, c % 2, :, P - 1:P].to_broadcast([P, HEADS, HD]), ALU.mult)\
                            .then_inc(kept_ready, 1)
                        dve.wait_ge(kept_ready, c + 1)
                        dve.wait_ge(ds_ready, c + 1)
                        nc.vector.tensor_tensor(state[:, (c + 1) % 2, :, :], kept[:, :, :],
                                                ps[:, S, 0:HEADS * HD].rearrange("p (h q) -> p h q", h=HEADS), ALU.add)\
                            .then_inc(state_ready, 1)
                if c % 4 == 3:
                    g = c // 4
                    dve.wait_ge(y_summed, c + 1)
                    for f in range(FT):
                        nc.vector.scalar_tensor_tensor(out=y[:, f, cols(g)], in0=xs[:, f, cols(g)],
                                                       scalar=k.vec[:, VB_D + f:VB_D + f + 1], in1=ps[:, Y + f, :],
                                                       op0=ALU.mult, op1=ALU.add).then_inc(yd_ready, 1)
                    for f in range(FT):
                        dve.wait_ge(yd_ready, g * FT + f + 1)
                        nc.vector.tensor_tensor(y[:, f, cols(g)], y[:, f, cols(g)], sz[:, f, cols(g)], ALU.mult)\
                            .then_inc(yz_ready, 1)

    post = ExitStack()
    out = sb("out", [P, T], ctx=post)
    last_ready = sem("last_ready")
    log_done, rms_ready, out_ready, out_done, res_done = [sem(n) for n in (
        "log_done rms_ready out_ready out_done res_done").split()]

    with post, nc.Block() as block:

        @block.tensor
        def _(pe):
            for f in range(FT):
                last = nc.tensor.matmul(ps[:, M, :], k.ones[:, :], sq[:, f, :], start=(f == 0), stop=(f == FT - 1))
            last.then_inc(last_ready, 1)
            for c in range(NCH):
                for f in range(FT):
                    last = nc.tensor.matmul(ps[:, c, :], w_out[:, f, :], y[:, f, cols(c)],
                                            start=(f == 0), stop=(f == FT - 1))
                last.then_inc(out_ready, 1)

        @block.scalar
        def _(act):
            for c in range(NCH - 1):
                nc.scalar.activation(mean_square[:, cols(c)], mean_square[:, cols(c)], ACT.Ln, bias=k.eps6[:, 0:1])\
                    .then_inc(log_done, 1)
            act.wait_ge(last_ready, 1)
            nc.scalar.activation(mean_square[:, cols(NCH - 1)], ps[:, M, :], ACT.Ln, bias=k.eps6[:, 0:1],
                                 scale=P / DI).then_inc(log_done, 1)
            for c in range(NCH):
                act.wait_ge(log_done, c + 1)
                nc.scalar.activation(mean_square[:, cols(c)], mean_square[:, cols(c)], ACT.Exp, scale=-0.5)\
                    .then_inc(rms_ready, 1)

        @block.vector
        def _(dve):
            def add(c):
                dve.wait_ge(out_done, c + 1)
                nc.vector.tensor_tensor(k.xn[:, cols(c)], k.xn[:, cols(c)], out[:, cols(c)], ALU.add)\
                    .then_inc(res_done, 1)

            for c in range(NCH):
                dve.wait_ge(out_ready, c + 1)
                dve.wait_ge(rms_ready, c + 1)
                nc.vector.tensor_tensor(out[:, cols(c)], ps[:, c, :], mean_square[:, cols(c)], ALU.mult)\
                    .then_inc(out_done, 1)
                if c:
                    add(c - 1)
            add(NCH - 1)

    mlp_in = conv[:, 0, :]
    x_hi, x_lo = [sb(n, [P, T], F32R) for n in ("x_hi", "x_lo")]
    mlp = ExitStack()
    WC = 3 * MT * P
    raw = sb("raw", [P, WC], ctx=mlp)
    w_hi, w_lo = sb("w_hi", [P, WC], F32R, ctx=mlp), sb("w_lo", [P, WC], F32R, ctx=mlp)
    raw_loaded, w_high, w_ready = sem("mlp_raw_loaded"), sem("mlp_w_high"), sem("mlp_w_ready")

    def load_mlp(sp):
        sp.dma_start(raw[:, 0:2 * MT * P], d["w_guB"]).then_inc(raw_loaded, 16)
        sp.dma_start(raw[:, 2 * MT * P:], d["w_dnB"]).then_inc(raw_loaded, 16)

    def split_mlp(pool):
        pool.wait_ge(raw_loaded, 32)
        nc.gpsimd.tensor_copy(w_hi[:, :], raw[:, :]).then_inc(w_high, 1)
        pool.wait_ge(w_high, 1)
        nc.gpsimd.tensor_tensor(w_lo[:, :], raw[:, :], w_hi[:, :].bitcast(F32), ALU.subtract).then_inc(w_ready, 1)

    norm_stage(k, "nm", None, k.xn, False, None, weight=k.vec[:, VB_POST:VB_POST + 1], rms_eps=k.eps6,
               out=mlp_in, split=(x_hi, x_lo), sync_part=load_mlp, pool_part=split_mlp)
    gate, prod = sb("gate", [P, 2, CH], ctx=mlp), sb("prod", [P, 2, CH], ctx=mlp)
    p_hi, p_lo = sb("p_hi", [P, 4, CH], F32R, ctx=mlp), sb("p_lo", [P, 4, CH], F32R, ctx=mlp)
    total = sb("total", [P, 2, CH], ctx=mlp)
    G, U, O = 0, 2, 4
    g_ready, u_ready, gate_done, prod_done, high_ready, low_ready, tile_summed, \
        total_ready, x_added = [sem("mlp_" + n) for n in (
            "g_ready u_ready gate_done prod_done high_ready low_ready tile_summed "
            "total_ready x_added").split()]

    with stage, mlp, nc.Block() as block:

        @block.tensor
        def _(pe):
            def product(out, a, v_hi, v_lo, start, stop):
                nc.tensor.matmul(out, w_hi[:, a:a + P], v_hi, start=start, stop=False)
                nc.tensor.matmul(out, w_hi[:, a:a + P], v_lo, start=False, stop=False)
                return nc.tensor.matmul(out, w_lo[:, a:a + P], v_hi, start=False, stop=stop)

            def down(q):
                c, i = divmod(q, MT)
                if i == 0 and c >= 2:
                    pe.wait_ge(total_ready, c - 1)
                pe.wait_ge(low_ready, q + 1)
                product(ps[:, O + c % 2, :], (2 * MT + i) * P, p_hi[:, q % 4, :], p_lo[:, q % 4, :],
                        i == 0, i == MT - 1).then_inc(tile_summed, 1)

            pe.wait_ge(w_ready, 1)
            for q in range(NCH * MT):
                c, i = divmod(q, MT)
                if q >= 2:
                    pe.wait_ge(prod_done, q - 1)
                xh, xl = x_hi[:, cols(c)], x_lo[:, cols(c)]
                product(ps[:, G + q % 2, :], i * P, xh, xl, True, True).then_inc(g_ready, 1)
                product(ps[:, U + q % 2, :], (MT + i) * P, xh, xl, True, True).then_inc(u_ready, 1)
                if q >= 2:
                    down(q - 2)
            down(NCH * MT - 2)
            down(NCH * MT - 1)

        @block.scalar
        def _(act):
            def high(q):
                act.wait_ge(prod_done, q + 1)
                if q >= 4:
                    act.wait_ge(tile_summed, q - 3)
                nc.scalar.activation(p_hi[:, q % 4, :], prod[:, q % 2, :], ACT.Copy).then_inc(high_ready, 1)

            for q in range(NCH * MT):
                act.wait_ge(g_ready, q + 1)
                nc.scalar.activation(gate[:, q % 2, :], ps[:, G + q % 2, :], ACT.Silu).then_inc(gate_done, 1)
                if q:
                    high(q - 1)
            high(NCH * MT - 1)

        @block.vector
        def _(dve):
            def low(q):
                dve.wait_ge(high_ready, q + 1)
                nc.vector.tensor_tensor(p_lo[:, q % 4, :], prod[:, q % 2, :], p_hi[:, q % 4, :].bitcast(F32),
                                        ALU.subtract).then_inc(low_ready, 1)

            def finish(c):
                dve.wait_ge(tile_summed, (c + 1) * MT)
                if c >= 2:
                    dve.wait_ge(x_added, c - 1)
                nc.vector.tensor_tensor(total[:, c % 2, :], ps[:, O + c % 2, :], k.xn[:, cols(c)], ALU.add)\
                    .then_inc(total_ready, 1)
                dve.wait_ge(total_ready, c + 1)
                nc.vector.tensor_tensor(k.x[:, cols(c)], k.x[:, cols(c)], total[:, c % 2, :], ALU.add)\
                    .then_inc(x_added, 1)

            for q in range(NCH * MT):
                dve.wait_ge(gate_done, q + 1)
                dve.wait_ge(u_ready, q + 1)
                if q >= 2:
                    dve.wait_ge(low_ready, q - 1)
                nc.vector.tensor_tensor(prod[:, q % 2, :], gate[:, q % 2, :], ps[:, U + q % 2, :], ALU.mult)\
                    .then_inc(prod_done, 1)
                if q:
                    low(q - 1)
                if q % MT == 2 and q > MT:
                    finish(q // MT - 1)
            low(NCH * MT - 1)
            finish(NCH - 1)


def build(nc, d, out):
    ctx = ExitStack()
    with ctx:
        k = Core(nc, ctx)
        load_stage(k, d)
        mixer_a_stage(k, d)
        ffn_stage(k, d, 0, "f")
        mixer_b_stage(k, d)
        ffn_stage(k, d, 1, "g", out)


def layout(i):
    a = lambda n: np.asarray(i[n])
    col = lambda v: a(v).reshape(-1, P).T
    vec = [col("L0_attn_a_norm_w"), col("L0_attn_a_conv_b"), col("L0_attn_a_dt_proj_b"), col("L0_attn_a_D"),
           a("L0_attn_a_A_log").reshape(FT, P, NST).transpose(1, 0, 2).reshape(P, FT * NST),
           col("L0_attn_b_norm_w"), col("L0_attn_b_post_norm_w"), col("L0_attn_b_ssm_norm_w"),
           col("L0_attn_b_conv_b"), np.repeat(a("L0_attn_b_D"), 64).reshape(FT, P).T,
           a("L0_attn_a_conv_w").reshape(FT, P, TAPS).transpose(1, 0, 2).reshape(P, FT * TAPS),
           a("L0_attn_b_conv_w").reshape(4, P, TAPS).transpose(1, 0, 2).reshape(P, 4 * TAPS)]
    xw = a("L0_attn_a_x_proj_w")
    order = np.concatenate([xw[RANK:], xw[:RANK]])
    m = {
        "xT": a("L0_attn_a_x").reshape(T, P).T,
        "vec": np.concatenate(vec, axis=1),
        "eye": np.eye(P, dtype=np.float32),
        "tapsA": a("L0_attn_a_conv_w")[P:, 0, :].T.reshape(TAPS * P),
        "w_inA": a("L0_attn_a_in_proj_w").T,
        "w_xA": order.T.reshape(FT, P, 40).transpose(1, 0, 2),
        "w_dtA": a("L0_attn_a_dt_proj_w").T,
        "w_outA": a("L0_attn_a_out_proj_w").T.reshape(FT, P, P).transpose(1, 0, 2),
    }
    w = a("L0_attn_b_in_proj_w")
    m["w_inB"] = w.T
    m["tapsB"] = a("L0_attn_b_conv_w")[3 * P:].T.reshape(TAPS * P)
    m["headsB"] = np.concatenate([a("L0_attn_b_dt_bias"), a("L0_attn_b_A_log")])
    m["w_outB"] = a("L0_attn_b_out_proj_w").T.reshape(FT, P, P).transpose(1, 0, 2)
    m["masks"] = np.stack([np.triu(np.ones((P, P), np.float32)), np.tril(np.ones((P, P), np.float32), -1)], axis=1)
    m["w_guB"] = np.concatenate([a("L0_attn_b_gate_w"), a("L0_attn_b_up_w")]).T
    m["w_dnB"] = a("L0_attn_b_down_w").T.reshape(3, P, P).transpose(1, 0, 2).reshape(P, 3 * P)
    gu = np.concatenate([a("L0_ffn_shared_gate_up")[None], a("L0_ffn_experts_gate_up")])
    full = NI * P
    m["gu_shared"] = np.concatenate([gu[0, :full], gu[0, INTER:INTER + full], gu[0, full:INTER],
                                     gu[0, INTER + full:]]).T
    w0 = HALVES[0]
    m["gu"] = np.concatenate([gu[1:, :w0], gu[1:, INTER:INTER + w0], gu[1:, w0:INTER], gu[1:, INTER + w0:]], axis=1)\
        .transpose(0, 2, 1)
    m["dn"] = np.concatenate([a("L0_ffn_shared_down")[None], a("L0_ffn_experts_down")]).transpose(0, 2, 1)
    m["w_gateF"] = a("L0_ffn_gate_weight").T
    more = np.arange(TT) * P
    more[0] = -1
    place = (np.arange(EXPERTS) + 1) % RING
    m["fc"] = np.concatenate([np.arange(EXPERTS, 0, -1), more, np.arange(SLOT_TILES), np.diff(place)])\
        .astype(np.float32)
    m["places"] = (np.arange(TOP * TT) * P + np.arange(P)[:, None]).astype(np.int32)
    m["slots"] = np.zeros((SLOT_TILES * P, ROW), np.float32)
    m["slots"].view(np.int32)[:, P] = TOP * T + np.arange(SLOT_TILES * P)
    return {n: np.ascontiguousarray(v) for n, v in m.items()}


def kernel(**inputs):
    import concourse.bacc as bacc
    from concourse.bass_utils import run_bass_kernel_spmd

    nc = bacc.Bacc("TRN2", target_bir_lowering=False, num_devices=1)
    arrays = layout(inputs)
    d = {n: nc.dram_tensor("in_" + n, v.shape, mybir.dt.from_np(v.dtype), kind="ExternalInput").ap()
         for n, v in arrays.items()}
    out = nc.dram_tensor("out", (P, T), F32, kind="ExternalOutput").ap()
    build(nc, d, out)
    r = run_bass_kernel_spmd(nc, [{"in_" + n: v for n, v in arrays.items()}], core_ids=[0])
    return r.results[0]["out"].T.reshape(BATCH, SEQ, P)
```
